# Optimizing a Trainium2 kernel written in Bass

```python
import numpy as np
import jax
import jax.numpy as jnp

def _softmax(x, axis=-1):
    return jax.nn.softmax(x, axis=axis)

def _gelu(x):
    return jax.nn.gelu(x, approximate=True)

def _silu(x):
    return jax.nn.silu(x)

def _sigmoid(x):
    return jax.nn.sigmoid(x)

def _layernorm(x, axis=-1, eps=1e-05):
    m = jnp.mean(x, axis=axis, keepdims=True)
    v = jnp.var(x, axis=axis, keepdims=True)
    return (x - m) / jnp.sqrt(v + eps)

def _scatter_add(tgt, idx, src, axis=0):
    return tgt.at[idx].add(src)

def _segment_sum(src, seg, n):
    return jax.ops.segment_sum(src, seg, n)
kernel_name = 'mk_flamingo_gated_d2_seqx_r8_afb3ca'

def setup_inputs(seed: int=0):
    np.random.seed(seed)
    _w = jnp.asarray

    def _rec_inputs():
        import jax
        import jax.numpy as jnp
        _rk = jax.random.key(seed)
        x = -0.0002928 + 1 * jax.random.normal(jax.random.fold_in(_rk, 1), (8, 100, 256), jnp.float32)
        _lenS = 100 - jax.random.randint(jax.random.fold_in(_rk, 7), (8,), 0, max(1, 100 // 4) + 1, jnp.int32)
        _lenS2 = 1444 - jax.random.randint(jax.random.fold_in(_rk, 8), (8,), 0, max(1, 1444 // 4) + 1, jnp.int32)
        _ctx_2048P = jax.random.normal(jax.random.fold_in(_rk, 11), (8, 16, 256), jnp.float32)
        _ctx_2048c = jax.random.dirichlet(jax.random.fold_in(_rk, 511), 0.3 * jnp.ones((16,), jnp.float32), (8, 1444))
        _ctx_2048t = jnp.einsum('bsk,bkd->bsd', _ctx_2048c, _ctx_2048P)
        _ctx_2048t = _ctx_2048t * jax.lax.rsqrt(jnp.mean(jnp.square(_ctx_2048t)) + 1e-12) * 0.953939
        ctx_2048 = 4.13588e-05 + 0.999923 * (_ctx_2048t + 0.3 * jax.random.normal(jax.random.fold_in(_rk, 611), (8, 1444, 256), jnp.float32))
        _validS = jnp.arange(100)[None, :] < _lenS[:, None]
        _validS2 = jnp.arange(1444)[None, :] < _lenS2[:, None]
        _causal = jnp.tril(jnp.ones((100, 100), dtype=bool))
        mask_1xSxS2_ff0 = jnp.where(jnp.ones((1, 100, 1444), dtype=bool), 0.0, -1000000000.0).astype(jnp.float32)
        _g = jax.random.normal(jax.random.fold_in(_rk, 9001), (2, 2), jnp.float32)
        _g = jnp.sign(_g) * jnp.maximum(jnp.abs(_g), 1.0) + (_g == 0) * 1.0
        g_xattn = _g[0]
        g_ffn = _g[1]
        return (x, ctx_2048, mask_1xSxS2_ff0, g_xattn, g_ffn)
    x, ctx_2048, mask_1xSxS2_ff0, g_xattn, g_ffn = _rec_inputs()

    def _L0_xattn_setup():
        import jax, jax.numpy as jnp
        import numpy as np
        H = 256
        NH = 16
        NKV = 4
        HD = 128
        GROUPS = NH // NKV
        EPS = 1e-06
        B, S, SE = (1, 256, 512)

        def _rmsnorm(x, w, eps=EPS):
            xf = x.astype(jnp.float32)
            var = jnp.mean(xf * xf, axis=-1, keepdims=True)
            return (xf * jax.lax.rsqrt(var + eps)).astype(x.dtype) * w
        key = jax.random.key(seed)
        ks = jax.random.split(key, 12)
        sc = 0.02
        return {'hidden_states': jax.random.normal(ks[0], (B, S, H), jnp.float32), 'encoder_hidden_states': jax.random.normal(ks[1], (B, SE, H), jnp.float32), 'attention_mask': jnp.zeros((B, S, SE), jnp.float32), 'Wq': jax.random.normal(ks[2], (H, NH * HD), jnp.float32) * sc, 'bq': jax.random.normal(ks[3], (NH * HD,), jnp.float32) * sc, 'Wk': jax.random.normal(ks[4], (H, NKV * HD), jnp.float32) * sc, 'bk': jax.random.normal(ks[5], (NKV * HD,), jnp.float32) * sc, 'Wv': jax.random.normal(ks[6], (H, NKV * HD), jnp.float32) * sc, 'bv': jax.random.normal(ks[7], (NKV * HD,), jnp.float32) * sc, 'Wo': jax.random.normal(ks[8], (NH * HD, H), jnp.float32) * sc, 'qn_w': jnp.ones((HD,), jnp.float32), 'kn_w': jnp.ones((HD,), jnp.float32)}
    _L0_xattn_all = _L0_xattn_setup()
    _L0_xattn_in = {k: v for k, v in _L0_xattn_all.items() if k in ('Wq', 'bq', 'Wk', 'bk', 'Wv', 'bv', 'Wo', 'qn_w', 'kn_w')}
    del _L0_xattn_all

    def _L0_ffn_setup():
        import jax, jax.numpy as jnp
        import numpy as np
        CAP_FACTOR = 1.25
        MIN_CAPACITY = 4

        def _capacity(num_tokens, num_experts):
            cap = int(np.floor(CAP_FACTOR * num_tokens / num_experts))
            cap += cap % 2
            return max(cap, MIN_CAPACITY)
        key = jax.random.key(seed)
        k1, k2, k3, k4 = jax.random.split(key, 4)
        B, S, H, I, E = (4, 256, 256, 1024, 8)
        inputs = jax.random.normal(k1, (B, S, H), dtype=jnp.float32)
        gate_weight = jax.random.normal(k2, (E, H), dtype=jnp.float32) * np.sqrt(0.1 / H)
        wi = jax.random.normal(k3, (E, H, I), dtype=jnp.float32) * np.sqrt(0.1 / H)
        wo = jax.random.normal(k4, (E, I, H), dtype=jnp.float32) * np.sqrt(0.1 / I)
        return {'inputs': inputs, 'gate_weight': gate_weight, 'wi': wi, 'wo': wo}
    _L0_ffn_all = _L0_ffn_setup()
    _L0_ffn_in = {k: v for k, v in _L0_ffn_all.items() if k in ('gate_weight', 'wi', 'wo')}
    del _L0_ffn_all

    def _L1_xattn_setup():
        import jax, jax.numpy as jnp
        import numpy as np
        D_MODEL = 256
        NUM_HEADS = 16
        HEAD_DIM = D_MODEL // NUM_HEADS

        def _fq_sym(x, axis):
            s = jnp.max(jnp.abs(x), axis=axis, keepdims=True) / 127.0
            s = jnp.maximum(s, 1e-08)
            q = jnp.clip(jnp.round(x / s), -127.0, 127.0) * s
            return x + jax.lax.stop_gradient(q - x)

        def _fq_unsigned(x, axis):
            s = jnp.max(x, axis=axis, keepdims=True) / 255.0
            s = jnp.maximum(s, 1e-08)
            q = jnp.clip(jnp.round(x / s), 0.0, 255.0) * s
            return x + jax.lax.stop_gradient(q - x)
        key = jax.random.key(seed)
        ks = jax.random.split(key, 8)
        B, N, M, C = (2, 256, 64, D_MODEL)
        return {'x': jax.random.normal(ks[0], (B, N, C), jnp.float32), 'cond': jax.random.normal(ks[1], (B, M, C), jnp.float32), 'Wq': jax.random.normal(ks[2], (C, C), jnp.float32) * 0.02, 'bq': jnp.zeros((C,), jnp.float32), 'Wkv': jax.random.normal(ks[3], (C, 2 * C), jnp.float32) * 0.02, 'bkv': jnp.zeros((2 * C,), jnp.float32), 'Wp': jax.random.normal(ks[4], (C, C), jnp.float32) * 0.02, 'bp': jnp.zeros((C,), jnp.float32)}
    _L1_xattn_all = _L1_xattn_setup()
    _L1_xattn_in = {k: v for k, v in _L1_xattn_all.items() if k in ('Wq', 'bq', 'Wkv', 'bkv', 'Wp', 'bp')}
    del _L1_xattn_all

    def _L1_ffn_setup():
        import jax, jax.numpy as jnp
        import numpy as np
        D = 256
        F = 176
        E = 8
        K = 2
        FS = 352
        B, S = (2, 128)
        key = jax.random.key(seed)
        ks = jax.random.split(key, 9)
        sc = 0.02
        return {'x': jax.random.normal(ks[0], (B, S, D), dtype=jnp.float32), 'Wr': jax.random.normal(ks[1], (E, D), dtype=jnp.float32) * sc, 'Wg': jax.random.normal(ks[2], (E, F, D), dtype=jnp.float32) * sc, 'Wu': jax.random.normal(ks[3], (E, F, D), dtype=jnp.float32) * sc, 'Wd': jax.random.normal(ks[4], (E, D, F), dtype=jnp.float32) * sc, 'Wsg': jax.random.normal(ks[5], (FS, D), dtype=jnp.float32) * sc, 'Wsu': jax.random.normal(ks[6], (FS, D), dtype=jnp.float32) * sc, 'Wsd': jax.random.normal(ks[7], (D, FS), dtype=jnp.float32) * sc}
    _L1_ffn_all = _L1_ffn_setup()
    _L1_ffn_in = {k: v for k, v in _L1_ffn_all.items() if k in ('Wr', 'Wg', 'Wu', 'Wd', 'Wsg', 'Wsu', 'Wsd')}
    del _L1_ffn_all
    return {'x': x, 'ctx_2048': ctx_2048, 'mask_1xSxS2_ff0': mask_1xSxS2_ff0, 'g_xattn': g_xattn, 'g_ffn': g_ffn, 'L0_xattn_Wq': _L0_xattn_in['Wq'], 'L0_xattn_bq': _L0_xattn_in['bq'], 'L0_xattn_Wk': _L0_xattn_in['Wk'], 'L0_xattn_bk': _L0_xattn_in['bk'], 'L0_xattn_Wv': _L0_xattn_in['Wv'], 'L0_xattn_bv': _L0_xattn_in['bv'], 'L0_xattn_Wo': _L0_xattn_in['Wo'], 'L0_xattn_qn_w': _L0_xattn_in['qn_w'], 'L0_xattn_kn_w': _L0_xattn_in['kn_w'], 'L0_ffn_gate_weight': _L0_ffn_in['gate_weight'], 'L0_ffn_wi': _L0_ffn_in['wi'], 'L0_ffn_wo': _L0_ffn_in['wo'], 'L1_xattn_Wq': _L1_xattn_in['Wq'], 'L1_xattn_bq': _L1_xattn_in['bq'], 'L1_xattn_Wkv': _L1_xattn_in['Wkv'], 'L1_xattn_bkv': _L1_xattn_in['bkv'], 'L1_xattn_Wp': _L1_xattn_in['Wp'], 'L1_xattn_bp': _L1_xattn_in['bp'], 'L1_ffn_Wr': _L1_ffn_in['Wr'], 'L1_ffn_Wg': _L1_ffn_in['Wg'], 'L1_ffn_Wu': _L1_ffn_in['Wu'], 'L1_ffn_Wd': _L1_ffn_in['Wd'], 'L1_ffn_Wsg': _L1_ffn_in['Wsg'], 'L1_ffn_Wsu': _L1_ffn_in['Wsu'], 'L1_ffn_Wsd': _L1_ffn_in['Wsd']}

def reference(x, ctx_2048, mask_1xSxS2_ff0, g_xattn, g_ffn, L0_xattn_Wq, L0_xattn_bq, L0_xattn_Wk, L0_xattn_bk, L0_xattn_Wv, L0_xattn_bv, L0_xattn_Wo, L0_xattn_qn_w, L0_xattn_kn_w, L0_ffn_gate_weight, L0_ffn_wi, L0_ffn_wo, L1_xattn_Wq, L1_xattn_bq, L1_xattn_Wkv, L1_xattn_bkv, L1_xattn_Wp, L1_xattn_bp, L1_ffn_Wr, L1_ffn_Wg, L1_ffn_Wu, L1_ffn_Wd, L1_ffn_Wsg, L1_ffn_Wsu, L1_ffn_Wsd):
    import jax
    import jax.numpy as jnp

    def _L0_xattn_ref(hidden_states, encoder_hidden_states, attention_mask, Wq, bq, Wk, bk, Wv, bv, Wo, qn_w, kn_w):
        import jax, jax.numpy as jnp
        import numpy as np
        H = 256
        NH = 16
        NKV = 4
        HD = 128
        GROUPS = NH // NKV
        EPS = 1e-06
        B, S, SE = (1, 256, 512)

        def _rmsnorm(x, w, eps=EPS):
            xf = x.astype(jnp.float32)
            var = jnp.mean(xf * xf, axis=-1, keepdims=True)
            return (xf * jax.lax.rsqrt(var + eps)).astype(x.dtype) * w
        b, s, _ = hidden_states.shape
        se = encoder_hidden_states.shape[1]
        q = (hidden_states @ Wq + bq).reshape(b, s, NH, HD).transpose(0, 2, 1, 3)
        k = (encoder_hidden_states @ Wk + bk).reshape(b, se, NKV, HD).transpose(0, 2, 1, 3)
        v = (encoder_hidden_states @ Wv + bv).reshape(b, se, NKV, HD).transpose(0, 2, 1, 3)
        k = jnp.repeat(k, GROUPS, axis=1)
        v = jnp.repeat(v, GROUPS, axis=1)
        q = _rmsnorm(q, qn_w)
        k = _rmsnorm(k, kn_w)
        scale = 1.0 / np.sqrt(HD).astype(np.float32)
        scores = jnp.einsum('bhsd,bhed->bhse', q, k) * scale
        scores = scores + attention_mask[:, None, :, :]
        probs = jax.nn.softmax(scores.astype(jnp.float32), axis=-1).astype(q.dtype)
        out = jnp.einsum('bhse,bhed->bhsd', probs, v)
        out = out.transpose(0, 2, 1, 3).reshape(b, s, NH * HD)
        return out @ Wo

    def _L0_ffn_ref(inputs, gate_weight, wi, wo):
        import jax, jax.numpy as jnp
        import numpy as np
        CAP_FACTOR = 1.25
        MIN_CAPACITY = 4

        def _capacity(num_tokens, num_experts):
            cap = int(np.floor(CAP_FACTOR * num_tokens / num_experts))
            cap += cap % 2
            return max(cap, MIN_CAPACITY)
        E, H = gate_weight.shape
        tokens = inputs.reshape(-1, H)
        T = tokens.shape[0]
        C = _capacity(T, E)
        gate_logits = tokens @ gate_weight.T
        gate = gate_logits.astype(jnp.float32)
        probs = jax.nn.softmax(gate, axis=-1)
        top1_idx = jnp.argmax(gate, axis=-1)
        mask = jax.nn.one_hot(top1_idx, E, dtype=jnp.int32)
        ranks = jnp.cumsum(mask, axis=0) - mask
        mask = mask * (ranks < C).astype(jnp.int32)
        rank1 = jnp.sum(mask * ranks, axis=-1)
        rank_oh = jax.nn.one_hot(rank1, C, dtype=inputs.dtype)
        weight = mask.astype(inputs.dtype) * probs.astype(inputs.dtype)
        combine_weights = weight[:, :, None] * rank_oh[:, None, :]
        sec_mask_f = (combine_weights != 0).astype(inputs.dtype)
        dispatch_data = jnp.einsum('tec,th->ech', sec_mask_f, tokens)
        h = jnp.einsum('ech,ehi->eci', dispatch_data, wi)
        h = jax.nn.gelu(h, approximate=False)
        expert_out = jnp.einsum('eci,eih->ech', h, wo)
        ans = jnp.einsum('tec,ech->th', combine_weights, expert_out)
        return ans.reshape(inputs.shape)

    def _L1_xattn_ref(x, cond, Wq, bq, Wkv, bkv, Wp, bp):
        import jax, jax.numpy as jnp
        import numpy as np
        D_MODEL = 256
        NUM_HEADS = 16
        HEAD_DIM = D_MODEL // NUM_HEADS

        def _fq_sym(x, axis):
            s = jnp.max(jnp.abs(x), axis=axis, keepdims=True) / 127.0
            s = jnp.maximum(s, 1e-08)
            q = jnp.clip(jnp.round(x / s), -127.0, 127.0) * s
            return x + jax.lax.stop_gradient(q - x)

        def _fq_unsigned(x, axis):
            s = jnp.max(x, axis=axis, keepdims=True) / 255.0
            s = jnp.maximum(s, 1e-08)
            q = jnp.clip(jnp.round(x / s), 0.0, 255.0) * s
            return x + jax.lax.stop_gradient(q - x)
        B, N, C = x.shape
        H, hd = (NUM_HEADS, HEAD_DIM)
        q = (x @ Wq + bq).reshape(1, B * N, H, hd)
        kv = (cond @ Wkv + bkv).reshape(1, -1, 2, H, hd)
        k, v = (kv[:, :, 0], kv[:, :, 1])
        scale = 1.0 / np.sqrt(hd).astype(np.float32)
        q = jnp.transpose(q * scale, (0, 2, 1, 3))
        k = jnp.transpose(k, (0, 2, 1, 3))
        v = jnp.transpose(v, (0, 2, 1, 3))
        q = _fq_sym(q, axis=-1)
        k = _fq_sym(k, axis=-1)
        v = _fq_sym(v, axis=2)
        attn = jnp.einsum('bhqd,bhkd->bhqk', q, k)
        attn = jax.nn.softmax(attn.astype(jnp.float32), axis=-1)
        attn = _fq_unsigned(attn, axis=-1)
        out = jnp.einsum('bhqk,bhkd->bhqd', attn, v)
        out = jnp.transpose(out, (0, 2, 1, 3)).reshape(B, N, C)
        return out @ Wp + bp

    def _L1_ffn_ref(x, Wr, Wg, Wu, Wd, Wsg, Wsu, Wsd):
        import jax, jax.numpy as jnp
        import numpy as np
        D = 256
        F = 176
        E = 8
        K = 2
        FS = 352
        B, S = (2, 128)
        silu = jax.nn.silu
        sg = silu(jnp.einsum('bsd,fd->bsf', x, Wsg))
        su = jnp.einsum('bsd,fd->bsf', x, Wsu)
        shared_out = jnp.einsum('bsf,df->bsd', sg * su, Wsd)
        logits = jnp.einsum('bsd,ed->bse', x, Wr)
        scores = jax.nn.softmax(logits, axis=-1)
        topk_scores, topk_idx = jax.lax.top_k(scores, K)
        w_full = jnp.sum(jax.nn.one_hot(topk_idx, E, dtype=x.dtype) * topk_scores[..., None], axis=-2)
        g = silu(jnp.einsum('bsd,efd->bsef', x, Wg))
        u = jnp.einsum('bsd,efd->bsef', x, Wu)
        out_e = jnp.einsum('bsef,edf->bsed', g * u, Wd)
        routed_out = jnp.einsum('bsed,bse->bsd', out_e, w_full)
        return routed_out + shared_out
    x = x + jnp.tanh(g_xattn[0]) * _L0_xattn_ref(_layernorm(x, axis=-1), ctx_2048, mask_1xSxS2_ff0, L0_xattn_Wq, L0_xattn_bq, L0_xattn_Wk, L0_xattn_bk, L0_xattn_Wv, L0_xattn_bv, L0_xattn_Wo, L0_xattn_qn_w, L0_xattn_kn_w)
    x = x + jnp.tanh(g_ffn[0]) * _L0_ffn_ref(_layernorm(x, axis=-1), L0_ffn_gate_weight, L0_ffn_wi, L0_ffn_wo)
    x = x + jnp.tanh(g_xattn[1]) * _L1_xattn_ref(_layernorm(x, axis=-1), ctx_2048, L1_xattn_Wq, L1_xattn_bq, L1_xattn_Wkv, L1_xattn_bkv, L1_xattn_Wp, L1_xattn_bp)
    x = x + jnp.tanh(g_ffn[1]) * _L1_ffn_ref(_layernorm(x, axis=-1), L1_ffn_Wr, L1_ffn_Wg, L1_ffn_Wu, L1_ffn_Wd, L1_ffn_Wsg, L1_ffn_Wsu, L1_ffn_Wsd)
    return x

_drawn_inputs = setup_inputs


def setup_inputs(seed=0):
    import zlib

    import numpy as np

    out = dict(_drawn_inputs(seed))
    spreads = {'g_ffn': (-1.0, 0.6),
     'L0_xattn_qn_w': (1.0, 0.6),
     'L0_xattn_kn_w': (1.0, 0.6),
     'L1_xattn_bq': (0.0, 0.8),
     'L1_xattn_bkv': (0.0, 0.292),
     'L1_xattn_bp': (0.0, 0.1)}
    factors = {'L0_xattn_bq': 8.0,
     'L0_xattn_bk': 8.0,
     'L0_xattn_bv': 4.31,
     'L0_ffn_gate_weight': 7.218,
     'L0_ffn_wi': 6.669,
     'L0_ffn_wo': 6.503,
     'L1_xattn_Wq': 8.0,
     'L1_xattn_Wkv': 3.876,
     'L1_ffn_Wr': 8.0,
     'L1_ffn_Wg': 8.0,
     'L1_ffn_Wu': 8.0,
     'L1_ffn_Wd': 8.0,
     'L1_ffn_Wsg': 3.525,
     'L1_ffn_Wsu': 3.493,
     'L1_ffn_Wsd': 3.495}
    for name, (base, spread) in spreads.items():
        noise = np.random.default_rng([zlib.crc32(name.encode()), seed]).standard_normal(out[name].shape)
        drawn = base * np.exp(spread * noise) if base else spread * noise
        out[name] = jnp.asarray(drawn.astype(out[name].dtype))
    for name, factor in factors.items():
        out[name] = (out[name] * factor).astype(out[name].dtype)
    return out
```

```python
from contextlib import ExitStack

import numpy as np
import concourse.bass as bass
from concourse import mybir

F32 = mybir.dt.float32
BF16 = mybir.dt.bfloat16
I16 = mybir.dt.int16
I32 = mybir.dt.int32
ALU = mybir.AluOpType
ACT = mybir.ActivationFunctionType
AX = mybir.AxisListType

P = 128
BANK = 512
B = 8
S = 100
T = B * S
NT = -(-T // P)
TR = T - (NT - 1) * P
SE = 1444
D = 256
DC = D // P
LN_EPS = 1e-5
RMS_EPS = 1e-6
HUGE = 3.0e38
ROUND = 12582912.0


class Space:

    def __init__(self, nc, ctx, stage):
        self.nc, self.ctx, self.stage, self.sems = nc, ctx, stage, []
        ctx.callback(self.release)

    def release(self):
        if self.sems:
            self.nc.clear_and_free_semaphores(self.sems)
            self.nc.all_engine_barrier()

    def sb(self, name, shape, dt=F32):
        return self.ctx.enter_context(self.nc.sbuf_tensor(f"{self.stage}_{name}", shape, dt))

    def ps(self, name, shape, dt=F32):
        return self.ctx.enter_context(self.nc.psum_tensor(f"{self.stage}_{name}", shape, dt))

    def sem(self, name):
        self.sems.append(self.nc.alloc_semaphore(f"{self.stage}_{name}"))
        return self.sems[-1]


class Chain:

    def __init__(self, eng, sem, base=0):
        self.eng, self.sem, self.base, self.n = eng, sem, base, 0

    def __call__(self, ins):
        self.n += 1
        ins.then_inc(self.sem, 1)
        self.eng.wait_ge(self.sem, self.base + self.n)


def wait_apart(eng, sem, value, passed):
    eng.wait_ge(sem, value)
    eng.sem_inc(passed, 1)


def token_tiles(ap):
    full = ap[0:(NT - 1) * P, :].rearrange("(n p) d -> p n d", p=P)
    return full, ap[(NT - 1) * P:T, :]


def make_identity(pool, ident, zeroed, done):
    pool.memset(ident[:, :], 0.0).then_inc(zeroed, 1)
    pool.wait_ge(zeroed, 1)
    pool.affine_select(out=ident[:, :], in_=ident[:, :], compare_op=ALU.not_equal, fill=1.0, base=0,
                       pattern=[[-1, P]], channel_multiplier=1).then_inc(done, 1)


def constants(nc, ident, identb, ones):
    with ExitStack() as ctx:
        sp = Space(nc, ctx, "const")
        zeroed, zeroedb, made = sp.sem("zeroed"), sp.sem("zeroedb"), sp.sem("made")
        block = ctx.enter_context(nc.Block())

        @block.gpsimd
        def _(pool):
            make_identity(pool, ident, zeroed, made)
            make_identity(pool, identb, zeroedb, made)
            pool.memset(ones[:, :], 1.0).then_inc(made, 1)


def layer_norm(nc, stage, ident, x_src, add_src, gate, x_dst, xnT, xrow=None):
    with ExitStack() as ctx:
        sp = Space(nc, ctx, stage)
        x = xrow if xrow is not None else sp.sb("x", [P, NT, D])
        sq = sp.sb("sq", [P, NT, D])
        add = sp.sb("add", [P, NT, D]) if add_src is not None else None
        g = sp.sb("g", [P, 2])
        stat = sp.sb("stat", [P, 4, NT])
        xt = [sp.ps(f"xt{i}", [P, BANK]) for i in range(4)]
        loaded, cleared, gated, tanhed, summed = (sp.sem(n) for n in
                                                  ("loaded", "cleared", "gated", "tanhed", "summed"))
        dve_own, sqrted, normed, turned, evac, stored, var_ready = (
            sp.sem(n) for n in ("dve_own", "sqrted", "normed", "turned", "evac", "stored", "var_ready"))
        block = ctx.enter_context(nc.Block())
        n_loads = 2 + (3 if add is not None else 0)
        x_full, x_rest = token_tiles(x_src)

        @block.sync
        def _(sp_):
            sp_.wait_ge(cleared, 1)
            sp_.dma_start(x[:, 0:NT - 1, :], x_full).then_inc(loaded, 16)
            sp_.dma_start(x[0:TR, NT - 1, :], x_rest).then_inc(loaded, 16)
            if add is not None:
                a_full, a_rest = token_tiles(add_src)
                sp_.dma_start(add[:, 0:NT - 1, :], a_full).then_inc(loaded, 16)
                sp_.dma_start(add[0:TR, NT - 1, :], a_rest).then_inc(loaded, 16)
                sp_.dma_start(g[:, 0:1], gate.to_broadcast([P, 1])).then_inc(loaded, 16)
            if x_dst is not None:
                d_full, d_rest = token_tiles(x_dst)
                sp_.wait_ge(summed, 1)
                sp_.dma_start(d_full, x[:, 0:NT - 1, :]).then_inc(stored, 16)
                sp_.dma_start(d_rest, x[0:TR, NT - 1, :]).then_inc(stored, 16)
                sp_.wait_ge(stored, 32)

        @block.scalar
        def _(act):
            if add is not None:
                act.wait_ge(loaded, 16 * n_loads)
                act.activation(g[:, 1:2], g[:, 0:1], ACT.Tanh).then_inc(tanhed, 1)
            if xnT is not None:
                act.wait_ge(var_ready, 1)
                act.activation(stat[:, 2, :], stat[:, 1, :], ACT.Sqrt).then_inc(sqrted, 1)

        @block.vector
        def _(dve):
            own = Chain(dve, dve_own)
            own(dve.memset(x[:, NT - 1, :], 0.0))
            if add is not None:
                own(dve.memset(add[:, NT - 1, :], 0.0))
            dve.memset(stat[:, :, :], 0.0).then_inc(cleared, 1)
            dve.wait_ge(cleared, 1)
            dve.wait_ge(loaded, 16 * n_loads)
            if add is not None:
                dve.wait_ge(tanhed, 1)
                dve.scalar_tensor_tensor(out=x[:, :, :], in0=add[:, :, :], scalar=g[:, 1:2], in1=x[:, :, :],
                                         op0=ALU.mult, op1=ALU.add).then_inc(summed, 1)
                dve.wait_ge(summed, 1)
            if xnT is None:
                return
            own(dve.tensor_reduce(stat[:, 0, :], x[:, :, :], AX.X, ALU.add))
            own(dve.tensor_scalar(stat[:, 0, :], stat[:, 0, :], 1.0 / D, None, ALU.mult))
            if x_dst is not None:
                dve.wait_ge(stored, 32)
            own(dve.tensor_tensor(x[:, :, :], x[:, :, :], stat[:, 0, :].unsqueeze(2).to_broadcast([P, NT, D]), ALU.subtract))
            own(dve.tensor_tensor(sq[:, :, :], x[:, :, :], x[:, :, :], ALU.mult))
            own(dve.tensor_reduce(stat[:, 1, :], sq[:, :, :], AX.X, ALU.add))
            dve.tensor_scalar(stat[:, 1, :], stat[:, 1, :], 1.0 / D, LN_EPS, ALU.mult, ALU.add).then_inc(var_ready, 1)
            dve.wait_ge(sqrted, 1)
            own(dve.reciprocal(stat[:, 3, :], stat[:, 2, :]))
            dve.tensor_tensor(x[:, :, :], x[:, :, :], stat[:, 3, :].unsqueeze(2).to_broadcast([P, NT, D]),
                              ALU.mult).then_inc(normed, 1)
            for j in range(4):
                c, n0 = j // 2, 4 * (j % 2)
                w = min(4 * P, T - n0 * P)
                dve.wait_ge(turned, j + 1)
                dve.tensor_copy(xnT[:, c, n0 * P:n0 * P + w], xt[j][:, 0:w]).then_inc(evac, 1)

        @block.tensor
        def _(pe):
            if xnT is None:
                return
            pe.wait_ge(normed, 1)
            for j in range(4):
                c, n0 = j // 2, 4 * (j % 2)
                tiles = range(n0, min(n0 + 4, NT))
                for n in tiles:
                    rows = P if n < NT - 1 else TR
                    at = (n - n0) * P
                    mm = pe.transpose(xt[j][:, at:at + rows], x[0:rows, n, c * P:(c + 1) * P],
                                      ident[0:rows, 0:rows])
                mm.then_inc(turned, 1)


NH, NKV, HD = 16, 4, 128
KC = -(-SE // P)
KR = SE - (KC - 1) * P
SOFT = float(HD) ** -0.5


def attention0(nc, ident, xnT, ctxT, mask, Wq, bq, Wk, bk, Wv, bv, Wo, qn_w, kn_w, out):
    G = NH // NKV
    parts = [(n * BANK, min(BANK, SE - n * BANK)) for n in range(-(-SE // BANK))]
    NP = len(parts)
    NJ = 8
    NSQ = KC * NKV + NH
    TG = 4
    NG = KC // TG
    rows_of = lambda c: P if c < KC - 1 else KR
    with ExitStack() as ctx:
        sp = Space(nc, ctx, "a0")
        wq = sp.sb("wq", [P, DC, NH * HD])
        wk = sp.sb("wk", [P, DC, NKV * HD])
        wv = sp.sb("wv", [P, DC, NKV * HD])
        wo = sp.sb("wo", [P, NH, D])
        bk_all = sp.sb("bk", [P, NKV * HD])
        bv_all = sp.sb("bv", [P, NKV * HD])
        bq_all = sp.sb("bq", [S, NH, HD])
        qn_col = sp.sb("qn", [P, 2])
        kn_col = sp.sb("kn", [P, 1])
        maskt = sp.sb("mask", [S, SE])
        xb = sp.sb("xb", [P, DC, S])
        cx = sp.sb("ctx", [P, DC, SE])
        krow = sp.sb("krow", [P, KC, NKV * HD])
        KT = sp.sb("KT", [P, NKV, SE])
        V = sp.sb("V", [P, KC, NKV * HD])
        QO = sp.sb("QO", [P, NH, S])
        orow = sp.sb("orow", [S, NH, HD])
        prob = sp.sb("prob", [S, 2, SE])
        PT = sp.sb("PT", [P, NG, TG * S])
        kstat = sp.sb("kstat", [P, 4, KC * NKV])
        qstat = sp.sb("qstat", [S, 4, NH])
        soft = sp.sb("soft", [S, 4, NH])
        junk = sp.sb("junk", [P, NJ, HD])
        ores = sp.sb("ores", [S, D])
        psum = sp.ps("banks", [P, 8, BANK])
        flat = psum[:, :, :].rearrange("p b n -> p (b n)")
        bank = [psum[:, i, :] for i in range(8)]
        SB = [bank[0:3], bank[3:6]]
        score_of = [flat[0:S, 0:SE], flat[0:S, 3 * BANK:3 * BANK + SE]]
        BPT, BO = bank[6], bank[7]
        names = ("weights", "ctx_in", "x_in", "kv_ready", "kv_evac", "ctx_used", "x_used", "squared", "k_var",
                 "k_sd", "k_rs", "k_norm", "kt_ready", "kt_evac", "q_ready", "q_evac", "q_var", "q_sd",
                 "q_rs", "q_norm", "qt_ready", "qt_evac", "s_ready", "max_found", "max_done", "sum_turned", "exp_done", "pt_ready", "pt_evac",
                 "pv_done", "o_evac", "ot_ready", "ot_evac", "wo_ready", "wo_evac", "stored", "set_up", "own")
        (weights, ctx_in, x_in, kv_ready, kv_evac, ctx_used, x_used, squared, k_var, k_sd, k_rs, k_norm, kt_ready,
         kt_evac, q_ready, q_evac, q_var, q_sd, q_rs, q_norm, qt_ready, qt_evac, s_ready, max_found, max_done, sum_turned,
         exp_done, pt_ready, pt_evac, pv_done, o_evac, ot_ready, ot_evac, wo_ready, wo_evac, stored, set_up,
         own_) = (sp.sem(n) for n in names)
        passed = sp.sem("passed")
        N_WEIGHTS = 16 * 10
        block = ctx.enter_context(nc.Block())

        @block.sync
        def _(sync):
            sync.dma_start(wk[:, :, :], Wk.rearrange("(c p) n -> p c n", p=P)).then_inc(weights, 16)
            sync.dma_start(wv[:, :, :], Wv.rearrange("(c p) n -> p c n", p=P)).then_inc(weights, 16)
            sync.dma_start(bk_all[:, :], bk.to_broadcast([P, NKV * HD])).then_inc(weights, 16)
            sync.dma_start(bv_all[:, :], bv.to_broadcast([P, NKV * HD])).then_inc(weights, 16)
            sync.dma_start(wq[:, :, :], Wq.rearrange("(c p) n -> p c n", p=P)).then_inc(weights, 16)
            sync.dma_start(bq_all[:, :, :].rearrange("p h d -> p (h d)"), bq.to_broadcast([S, NH * HD])).then_inc(weights, 16)
            sync.dma_start(qn_col[:, 0:1], qn_w).then_inc(weights, 16)
            sync.dma_start(kn_col[:, :], kn_w).then_inc(weights, 16)
            sync.dma_start(maskt[:, :], mask).then_inc(weights, 16)
            sync.dma_start(wo[:, :, :], Wo.rearrange("(h p) n -> p h n", p=P)).then_inc(weights, 16)
            with sync.Fori(0, B) as b:
                sync.wait_ge(ctx_used, b)
                sync.dma_start(cx[:, :, :], ctxT[:, :, bass.ds(b * SE, SE)].rearrange("c p n -> p c n")).then_inc(ctx_in, 16)
                sync.wait_ge(x_used, b)
                sync.dma_start(xb[:, :, :], xnT[:, :, bass.ds(b * S, S)]).then_inc(x_in, 16)
                sync.wait_ge(wo_evac, b + 1)
                sync.dma_start(out[b], ores[:, :]).then_inc(stored, 16)
            sync.wait_ge(stored, 16 * B)

        @block.tensor
        def _(pe):
            pe.wait_ge(weights, N_WEIGHTS)
            with pe.Fori(0, B) as b:
                pe.wait_ge(ctx_in, 16 * (b + 1))
                for c in range(KC):
                    n = rows_of(c)
                    for j, w in enumerate((wk, wv)):
                        if c < 3:
                            pe.wait_ge(wo_evac, b)
                        else:
                            pe.wait_ge(kv_evac, 2 * KC * b + 2 * (c - 3) + j + 1)
                        for k in range(DC):
                            mm = pe.matmul(SB[j][c % 3][0:n, :], cx[:, k, c * P:c * P + n], w[:, k, :],
                                           start=(k == 0), stop=(k == DC - 1))
                        mm.then_inc(kv_ready, 1)
                pe.nop().then_inc(ctx_used, 1)
                pe.wait_ge(x_in, 16 * (b + 1))
                pe.wait_ge(kv_evac, 2 * KC * (b + 1))
                for n in range(4):
                    for k in range(DC):
                        mm = pe.matmul(bank[n][0:S, :], xb[:, k, :], wq[:, k, n * BANK:(n + 1) * BANK],
                                       start=(k == 0), stop=(k == DC - 1))
                    mm.then_inc(q_ready, 1)
                pe.nop().then_inc(x_used, 1)
                for c in range(KC):
                    n = rows_of(c)
                    wait_apart(pe, k_norm, KC * b + c + 1, passed)
                    if c >= 2:
                        wait_apart(pe, kt_evac, KC * b + c - 1, passed)
                    for g in range(NKV):
                        mm = pe.transpose(bank[4 + c % 2][:, g * P:g * P + n], krow[0:n, c, g * HD:(g + 1) * HD],
                                          ident[0:n, 0:n])
                    mm.then_inc(kt_ready, 1)
                pe.wait_ge(q_norm, b + 1)
                for n in range(4):
                    for h in range(4):
                        mm = pe.transpose(bank[n][:, h * S:(h + 1) * S], orow[:, 4 * n + h, :], ident[0:S, 0:S])
                    mm.then_inc(qt_ready, 1)
                pe.wait_ge(qt_evac, 4 * (b + 1))
                pe.wait_ge(kt_evac, KC * (b + 1))

                def scores(h, n):
                    if n == 0 and h >= 2:
                        pe.wait_ge(max_done, NH * b + h - 1)
                    at, w = parts[n]
                    mm = pe.matmul(SB[h % 2][n][0:S, 0:w], QO[:, h, :], KT[:, h // G, at:at + w],
                                   start=True, stop=True)
                    if n == NP - 1:
                        mm.then_inc(s_ready, 1)

                def turn(h, g):
                    if g == 0:
                        pe.wait_ge(exp_done, NH * b + h + 1)
                    pe.wait_ge(pt_evac, NG * NH * b + NG * h + g)
                    for j in range(TG):
                        c = TG * g + j
                        n = rows_of(c)
                        mm = pe.transpose(BPT[0:n, j * S:(j + 1) * S], prob[:, h % 2, c * P:c * P + n],
                                          ident[0:S, 0:S])
                    mm.then_inc(pt_ready, 1)

                def weigh(h, g):
                    if g == 0:
                        pe.wait_ge(o_evac, NH * b + h)
                    pe.wait_ge(pt_evac, NG * NH * b + NG * h + g + 1)
                    for j in range(TG):
                        c = TG * g + j
                        n = rows_of(c)
                        mm = pe.matmul(BO[0:S, 0:HD], PT[0:n, g, j * S:(j + 1) * S],
                                       V[0:n, c, (h // G) * HD:(h // G + 1) * HD],
                                       start=(c == 0), stop=(c == KC - 1))
                    mm.then_inc(pv_done, 1)

                for h in range(2):
                    for n in range(NP):
                        scores(h, n)
                for h in range(NH):
                    turn(h, 0)
                    if h + 2 < NH:
                        scores(h + 2, 0)
                    turn(h, 1)
                    weigh(h, 0)
                    if h + 2 < NH:
                        scores(h + 2, 1)
                    turn(h, 2)
                    weigh(h, 1)
                    if h + 2 < NH:
                        scores(h + 2, 2)
                    weigh(h, 2)
                pe.wait_ge(o_evac, NH * (b + 1))
                for n in range(4):
                    for h in range(4):
                        mm = pe.transpose(bank[n][:, h * S:(h + 1) * S], orow[:, 4 * n + h, :], ident[0:S, 0:S])
                    mm.then_inc(ot_ready, 1)
                pe.wait_ge(ot_evac, 4 * (b + 1))
                for h in range(NH):
                    mm = pe.matmul(bank[4][0:S, 0:D], QO[:, h, :], wo[:, h, :], start=(h == 0), stop=(h == NH - 1))
                mm.then_inc(wo_ready, 1)

        @block.vector
        def _(dve):
            own0 = Chain(dve, own_)
            own0(dve.memset(kstat[:, :, :], 1.0))
            dve.wait_ge(weights, N_WEIGHTS)
            own0(dve.tensor_scalar(qn_col[:, 1:2], qn_col[:, 0:1], SOFT, None, ALU.mult))
            dve.nop().then_inc(set_up, 1)
            with dve.Fori(0, B) as b:
                if True:
                    for c in range(KC):
                        n = rows_of(c)
                        dve.wait_ge(kv_ready, 2 * KC * b + 2 * c + 1)
                        if c == 0:
                            dve.wait_ge(kt_ready, KC * b)
                        dve.tensor_tensor(krow[0:n, c, :], SB[0][c % 3][0:n, :], bk_all[0:n, :],
                                          ALU.add).then_inc(kv_evac, 1)
                        dve.wait_ge(kv_ready, 2 * KC * b + 2 * c + 2)
                        if c == 0:
                            dve.wait_ge(pv_done, NG * NH * b)
                        dve.tensor_tensor(V[0:n, c, :], SB[1][c % 3][0:n, :], bv_all[0:n, :],
                                          ALU.add).then_inc(kv_evac, 1)
                dve.wait_ge(squared, NSQ * b + KC * NKV)
                dve.tensor_scalar(kstat[:, 1, :], kstat[:, 0, :], 1.0 / HD, RMS_EPS, ALU.mult,
                                  ALU.add).then_inc(k_var, 1)
                dve.wait_ge(ot_ready, 4 * b)
                for n in range(4):
                    dve.wait_ge(q_ready, 4 * b + n + 1)
                    dve.tensor_tensor(orow[:, 4 * n:4 * n + 4, :],
                                      bank[n][0:S, :].rearrange("p (h d) -> p h d", h=4),
                                      bq_all[:, 4 * n:4 * n + 4, :], ALU.add).then_inc(q_evac, 1)
                dve.wait_ge(k_sd, b + 1)
                dve.reciprocal(kstat[:, 3, :], kstat[:, 2, :]).then_inc(k_rs, 1)
                dve.wait_ge(k_rs, b + 1)
                for c in range(KC):
                    n = rows_of(c)
                    for g in range(NKV):
                        i = dve.tensor_scalar(krow[0:n, c, g * HD:(g + 1) * HD], krow[0:n, c, g * HD:(g + 1) * HD],
                                              kstat[0:n, 3, c * NKV + g:c * NKV + g + 1], None, ALU.mult)
                    i.then_inc(k_norm, 1)
                dve.wait_ge(squared, NSQ * (b + 1))
                dve.tensor_scalar(qstat[:, 1, :], qstat[:, 0, :], 1.0 / HD, RMS_EPS, ALU.mult,
                                  ALU.add).then_inc(q_var, 1)
                dve.wait_ge(q_sd, b + 1)
                dve.reciprocal(qstat[:, 3, :], qstat[:, 2, :]).then_inc(q_rs, 1)
                dve.wait_ge(q_rs, b + 1)
                dve.tensor_tensor(orow[:, :, :], orow[:, :, :], qstat[:, 3, :].unsqueeze(2).to_broadcast([S, NH, HD]),
                                  ALU.mult).then_inc(q_norm, 1)

                def maximum(h):
                    wait_apart(dve, s_ready, NH * b + h + 1, passed)
                    if h >= 2:
                        wait_apart(dve, pt_ready, NG * NH * b + NG * (h - 1), passed)
                    dve.tensor_tensor_reduce(prob[:, h % 2, :], score_of[h % 2], maskt[:, :], 1.0, -HUGE,
                                             ALU.add, ALU.max, soft[:, 0, h:h + 1]).then_inc(max_found, 1)
                    dve.wait_ge(max_found, NH * b + h + 1)
                    dve.tensor_scalar(soft[:, 1, h:h + 1], soft[:, 0, h:h + 1], -1.0, None,
                                      ALU.mult).then_inc(max_done, 1)

                maximum(0)
                maximum(1)
                for h in range(NH):
                    dve.wait_ge(pt_ready, NG * NH * b + NG * h + 2)
                    dve.wait_ge(pv_done, NG * NH * b + max(NG * (h - 1) + 2, 0))
                    dve.tensor_copy(PT[:, 1, :], BPT[:, 0:TG * S]).then_inc(pt_evac, 1)
                    if h + 2 < NH:
                        maximum(h + 2)
                    dve.wait_ge(exp_done, NH * b + h + 1)
                    dve.reciprocal(soft[:, 3, h:h + 1], soft[:, 2, h:h + 1]).then_inc(sum_turned, 1)
                    dve.wait_ge(pv_done, NG * NH * b + NG * (h + 1))
                    dve.wait_ge(sum_turned, NH * b + h + 1)
                    dve.tensor_scalar(orow[:, h, :], BO[0:S, 0:HD], soft[:, 3, h:h + 1], None,
                                      ALU.mult).then_inc(o_evac, 1)
                dve.wait_ge(wo_ready, b + 1)
                dve.wait_ge(stored, 16 * b)
                dve.tensor_copy(ores[:, :], bank[4][0:S, 0:D]).then_inc(wo_evac, 1)

        @block.scalar
        def _(act):
            act.wait_ge(set_up, 1)
            with act.Fori(0, B) as b:
                for c in range(KC):
                    n = rows_of(c)
                    act.wait_ge(kv_evac, 2 * KC * b + 2 * c + 1)
                    for g in range(NKV):
                        m = c * NKV + g
                        if m >= NJ:
                            act.wait_ge(squared, NSQ * b + m - NJ + 1)
                        act.activation(junk[0:n, m % NJ, :], krow[0:n, c, g * HD:(g + 1) * HD], ACT.Square,
                                       accum_out=kstat[0:n, 0, m:m + 1]).then_inc(squared, 1)
                act.wait_ge(k_var, b + 1)
                act.activation(kstat[:, 2, :], kstat[:, 1, :], ACT.Sqrt).then_inc(k_sd, 1)
                for h in range(NH):
                    if h % 4 == 0:
                        act.wait_ge(q_evac, 4 * b + h // 4 + 1)
                    m = KC * NKV + h
                    act.wait_ge(squared, NSQ * b + m - NJ + 1)
                    act.activation(junk[0:S, m % NJ, :], orow[:, h, :], ACT.Square,
                                   accum_out=qstat[:, 0, h:h + 1]).then_inc(squared, 1)
                act.wait_ge(q_var, b + 1)
                act.activation(qstat[:, 2, :], qstat[:, 1, :], ACT.Sqrt).then_inc(q_sd, 1)
                for c in range(KC):
                    n = rows_of(c)
                    act.wait_ge(kt_ready, KC * b + c + 1)
                    act.activation(KT[:, :, c * P:c * P + n],
                                   bank[4 + c % 2].rearrange("p (g n) -> p g n", g=NKV)[:, :, 0:n],
                                   ACT.Copy, scale=kn_col[:, 0:1]).then_inc(kt_evac, 1)
                for n in range(4):
                    act.wait_ge(qt_ready, 4 * b + n + 1)
                    act.activation(QO[:, 4 * n:4 * n + 4, :].rearrange("p h s -> p (h s)"), bank[n][:, 0:4 * S],
                                   ACT.Copy, scale=qn_col[:, 1:2]).then_inc(qt_evac, 1)

                def exponential(h):
                    act.wait_ge(max_done, NH * b + h + 1)
                    act.activation(prob[:, h % 2, :], prob[:, h % 2, :], ACT.Exp, bias=soft[:, 1, h:h + 1],
                                   accum_out=soft[:, 2, h:h + 1]).then_inc(exp_done, 1)

                exponential(0)
                exponential(1)
                for h in range(NH):
                    for g in (0, 2):
                        act.wait_ge(pt_ready, NG * NH * b + NG * h + g + 1)
                        act.wait_ge(pv_done, NG * NH * b + max(NG * (h - 1) + g + 1, 0))
                        if g < NG - 1:
                            act.copy(PT[:, g, :], BPT[:, 0:TG * S]).then_inc(pt_evac, 1)
                        else:
                            act.copy(PT[:, g, 0:(TG - 1) * S], BPT[:, 0:(TG - 1) * S])
                            act.copy(PT[0:KR, g, (TG - 1) * S:], BPT[0:KR, (TG - 1) * S:TG * S]).then_inc(pt_evac, 1)
                    if h + 2 < NH:
                        exponential(h + 2)
                for n in range(4):
                    act.wait_ge(ot_ready, 4 * b + n + 1)
                    act.copy(QO[:, 4 * n:4 * n + 4, :].rearrange("p h s -> p (h s)"),
                             bank[n][:, 0:4 * S]).then_inc(ot_evac, 1)


E0, I0 = 8, 1024
CAP = int(np.floor(1.25 * T / E0))
CAP = max(CAP + CAP % 2, 4)


def route(sp, own, pe_logits, exped, logits, gate, small, top, E, index_weight):
    dve = own.eng
    G, work, prob_ = gate[:, 0], gate[:, 1], gate[:, 2]
    masks = [gate[:, 3 + i] for i in range(top)]
    wide = [P, NT, E]
    dve.wait_ge(pe_logits, 1)
    own(dve.tensor_copy(gate[:, 0, 0:NT - 1, :], logits[:, 0:NT - 1, :]))
    own(dve.tensor_copy(gate[0:TR, 0, NT - 1, :], logits[0:TR, NT - 1, :]))
    own(dve.tensor_reduce(small[:, 0, :], G, AX.X, ALU.max))
    own(dve.tensor_tensor(prob_, G, small[:, 0, :].unsqueeze(2).to_broadcast(wide), ALU.subtract))
    dve.nop().then_inc(exped[0], 1)
    for i in range(top):
        if i:
            own(dve.scalar_tensor_tensor(out=G, in0=masks[i - 1], scalar=-HUGE, in1=G, op0=ALU.mult, op1=ALU.add))
            own(dve.tensor_reduce(small[:, 0, :], G, AX.X, ALU.max))
        own(dve.tensor_tensor(work, G, small[:, 0, :].unsqueeze(2).to_broadcast(wide), ALU.is_equal))
        own(dve.tensor_tensor(work, work, index_weight, ALU.mult))
        own(dve.tensor_reduce(small[:, 1, :], work, AX.X, ALU.max))
        own(dve.tensor_tensor(masks[i], work, small[:, 1, :].unsqueeze(2).to_broadcast(wide), ALU.is_equal))
    dve.wait_ge(exped[1], 1)
    own(dve.tensor_reduce(small[:, 2, :], prob_, AX.X, ALU.add))
    own(dve.reciprocal(small[:, 3, :], small[:, 2, :]))
    own(dve.tensor_tensor(prob_, prob_, small[:, 3, :].unsqueeze(2).to_broadcast(wide), ALU.mult))
    return prob_, masks


def moe0(nc, ident, ones, xnT, xrow, gateT, wi, wo, out):
    HC = I0 // P
    W4 = 4 * CAP
    with ExitStack() as ctx:
        sp = Space(nc, ctx, "m0")
        gw = sp.sb("gw", [P, DC, E0])
        before = sp.sb("before", [P, P])
        slot_no = sp.sb("slot_no", [P, CAP])
        index_weight = sp.sb("index_weight", [P, NT, E0])
        gate = sp.sb("gate", [P, 4, NT, E0])
        small = sp.sb("small", [P, 6, NT])
        slot_is = sp.sb("slot_is", [P, NT, CAP])
        disp = sp.sb("disp", [P, NT, E0, CAP])
        dispT = sp.sb("dispT", [CAP, E0, T])
        xd = sp.sb("xd", [P, DC, E0, CAP])
        wi_t = sp.sb("wi", [P, 2, DC, I0])
        wo_t = sp.sb("wo", [P, 2, HC, D])
        hid = sp.sb("hid", [P, 2, HC, CAP])
        eo = sp.sb("eo", [CAP, E0, D])
        ans = sp.sb("ans", [P, NT, D])
        psum = sp.ps("banks", [P, 8, BANK])
        bank = [psum[:, i, :] for i in range(8)]
        names = ("set_up", "loaded", "logits_ready", "to_exp", "exp_done", "own", "masked", "ranked", "spread",
                 "xd_ready", "xd_evac", "dt_ready", "dt_evac", "w_in", "h_ready", "gelu_done", "e_ready", "e_evac",
                 "ans_ready", "ans_evac", "stored", "pool_own")
        (set_up, loaded, logits_ready, to_exp, exp_done, own_, masked, ranked, spread, xd_ready, xd_evac,
         dt_ready, dt_evac, w_in, h_ready, gelu_done, e_ready, e_evac, ans_ready, ans_evac, stored,
         pool_own) = (sp.sem(n) for n in names)
        passed = sp.sem("passed")
        block = ctx.enter_context(nc.Block())
        logits = bank[0][:, 0:NT * E0].rearrange("p (n e) -> p n e", n=NT)
        ranks = bank[1][:, 0:NT * E0].rearrange("p (n e) -> p n e", n=NT)

        @block.gpsimd
        def _(pool):
            pool.memset(before[:, :], 1.0).then_inc(pool_own, 1)
            pool.iota(slot_no[:, :], [[1, CAP]], 0, 0, allow_small_or_imprecise_dtypes=True).then_inc(set_up, 1)
            pool.iota(index_weight[:, :, :], [[0, NT], [-1, E0]], E0, 0,
                      allow_small_or_imprecise_dtypes=True).then_inc(set_up, 1)
            pool.memset(gate[:, 0], 0.0).then_inc(set_up, 1)
            pool.wait_ge(pool_own, 1)
            pool.affine_select(out=before[:, :], in_=before[:, :], compare_op=ALU.is_gt, fill=0.0, base=0,
                               pattern=[[1, P]], channel_multiplier=-1).then_inc(set_up, 1)

        @block.sync
        def _(sync):
            sync.dma_start(gw[:, :, :], gateT.rearrange("(c p) e -> p c e", p=P)).then_inc(loaded, 16)
            with sync.Fori(0, E0 // 2) as i:
                for j in range(2):
                    sync.wait_ge(e_ready, 2 * i)
                    sync.dma_start(wi_t[:, j, :, :],
                                   wi[2 * i + j].rearrange("(c p) n -> p c n", p=P)).then_inc(w_in, 16)
                    sync.dma_start(wo_t[:, j, :, :],
                                   wo[2 * i + j].rearrange("(c p) n -> p c n", p=P)).then_inc(w_in, 16)
                    wait_apart(sync, w_in, 64 * i + 32 * (j + 1), passed)
            full, rest = token_tiles(out)
            sync.wait_ge(ans_evac, NT)
            sync.dma_start(full, ans[:, 0:NT - 1, :]).then_inc(stored, 16)
            sync.dma_start(rest, ans[0:TR, NT - 1, :]).then_inc(stored, 16)
            sync.wait_ge(stored, 32)

        @block.vector
        def _(dve):
            own = Chain(dve, own_)
            dve.wait_ge(set_up, 4)
            prob_, masks = route(sp, own, logits_ready, (to_exp, exp_done), logits, gate, small, 1, E0,
                                 index_weight[:, :, :])
            mask = masks[0]
            dve.nop().then_inc(masked, 1)
            own(dve.tensor_tensor(prob_, prob_, mask, ALU.mult))
            own(dve.tensor_reduce(small[:, 4, :], prob_, AX.X, ALU.add))
            dve.wait_ge(ranked, 1)
            work = gate[:, 1]
            kept = gate[:, 0]
            own(dve.tensor_copy(work, ranks))
            own(dve.scalar_tensor_tensor(out=kept, in0=work, scalar=float(CAP), in1=mask, op0=ALU.is_lt,
                                         op1=ALU.mult))
            own(dve.tensor_tensor(work, work, kept, ALU.mult))
            own(dve.tensor_reduce(small[:, 5, :], work, AX.X, ALU.add))
            own(dve.tensor_tensor(slot_is[:, :, :], slot_no[:, :].unsqueeze(1).to_broadcast([P, NT, CAP]),
                                  small[:, 5, :].unsqueeze(2).to_broadcast([P, NT, CAP]), ALU.is_equal))
            for n in range(NT):
                dve.tensor_tensor(disp[:, n, :, :], slot_is[:, n, :].unsqueeze(1).to_broadcast([P, E0, CAP]),
                                  kept[:, n, :].unsqueeze(2).to_broadcast([P, E0, CAP]),
                                  ALU.mult).then_inc(spread, 1)
            for j in range(4):
                k, half = j // 2, j % 2
                dve.wait_ge(xd_ready, j + 1)
                dve.tensor_copy(xd[:, k, 4 * half:4 * half + 4, :].rearrange("p e c -> p (e c)"),
                                bank[2 + j][:, 0:W4]).then_inc(xd_evac, 1)
            for e in range(E0):
                for half in range(2):
                    w = min(4, NT - 4 * half)
                    cols = min(w * P, T - 4 * P * half)
                    dve.wait_ge(dt_ready, 2 * e + half + 1)
                    dve.tensor_copy(dispT[:, e, 4 * P * half:4 * P * half + cols],
                                    bank[6 + half][0:CAP, 0:cols]).then_inc(dt_evac, 1)
            with dve.Fori(0, E0 // 2) as i:
                for j in range(2):
                    dve.wait_ge(e_ready, 2 * i + j + 1)
                    dve.tensor_copy(eo[:, bass.ds(2 * i + j, 1), :].rearrange("p a d -> p (a d)"),
                                    bank[4 + j][0:CAP, 0:D]).then_inc(e_evac, 1)
            for n in range(NT):
                dve.wait_ge(ans_ready, n + 1)
                dve.tensor_scalar(ans[:, n, :], bank[n % 2][:, 0:D], small[:, 4, n:n + 1], None,
                                  ALU.mult).then_inc(ans_evac, 1)

        @block.scalar
        def _(act):
            act.wait_ge(to_exp, 1)
            act.activation(gate[:, 2], gate[:, 2], ACT.Exp).then_inc(exp_done, 1)
            with act.Fori(0, E0 // 2) as i:
                for j in range(2):
                    if j == 0:
                        act.wait_ge(e_ready, 2 * i)
                    for half in range(2):
                        act.wait_ge(h_ready, 4 * i + 2 * j + half + 1)
                        act.activation(hid[:, j, 4 * half:4 * half + 4, :].rearrange("p c s -> p (c s)"),
                                       bank[half + 2 * j][:, 0:W4], ACT.Gelu).then_inc(gelu_done, 1)

        @block.tensor
        def _(pe):
            pe.wait_ge(loaded, 16)
            for n in range(NT):
                rows = P if n < NT - 1 else TR
                for k in range(DC):
                    mm = pe.matmul(logits[0:rows, n, :], xnT[:, k, n * P:n * P + rows], gw[:, k, :],
                                   start=(k == 0), stop=(k == DC - 1))
            mm.then_inc(logits_ready, 1)
            pe.wait_ge(masked, 1)
            pe.wait_ge(set_up, 4)
            for n in range(NT):
                for m in range(n + 1):
                    mm = pe.matmul(ranks[:, n, :], before[:, :] if m == n else ones[:, :], gate[:, 3, m, :],
                                   start=(m == 0), stop=(m == n))
            mm.then_inc(ranked, 1)
            pe.wait_ge(spread, NT)
            for j in range(4):
                k, half = j // 2, j % 2
                for n in range(NT):
                    rows = P if n < NT - 1 else TR
                    mm = pe.matmul(bank[2 + j][:, 0:W4], xrow[0:rows, n, k * P:(k + 1) * P],
                                   disp[0:rows, n, 4 * half:4 * half + 4, :].rearrange("p e c -> p (e c)"),
                                   start=(n == 0), stop=(n == NT - 1))
                mm.then_inc(xd_ready, 1)
            for e in range(E0):
                for half in range(2):
                    if e:
                        pe.wait_ge(dt_evac, 2 * (e - 1) + half + 1)
                    for m in range(min(4, NT - 4 * half)):
                        n = 4 * half + m
                        rows = P if n < NT - 1 else TR
                        mm = pe.transpose(bank[6 + half][0:CAP, m * P:m * P + rows], disp[0:rows, n, e, :],
                                          ident[0:rows, 0:rows])
                    mm.then_inc(dt_ready, 1)
            pe.wait_ge(xd_evac, 4)
            with pe.Fori(0, E0 // 2) as i:
                for j in range(2):
                    pe.wait_ge(w_in, 64 * i + 32 * (j + 1))
                    for half in range(2):
                        pe.wait_ge(gelu_done, 4 * i)
                        for c in range(4):
                            for k in range(DC):
                                mm = pe.matmul(bank[half + 2 * j][:, c * CAP:(c + 1) * CAP],
                                               wi_t[:, j, k, (4 * half + c) * P:(4 * half + c + 1) * P],
                                               xd[:, k, bass.ds(2 * i + j, 1), :].rearrange("p a c -> p (a c)"),
                                               start=(k == 0), stop=(k == DC - 1))
                        mm.then_inc(h_ready, 1)
                for j in range(2):
                    pe.wait_ge(gelu_done, 4 * i + 2 * j + 2)
                    pe.wait_ge(e_evac, 2 * i)
                    for c in range(HC):
                        mm = pe.matmul(bank[4 + j][0:CAP, 0:D], hid[:, j, c, :], wo_t[:, j, c, :],
                                       start=(c == 0), stop=(c == HC - 1))
                    mm.then_inc(e_ready, 1)
            pe.wait_ge(e_evac, E0)
            for n in range(NT):
                rows = P if n < NT - 1 else TR
                if n >= 2:
                    pe.wait_ge(ans_evac, n - 1)
                for e in range(E0):
                    mm = pe.matmul(bank[n % 2][0:rows, 0:D], dispT[:, e, n * P:n * P + rows], eo[:, e, :],
                                   start=(e == 0), stop=(e == E0 - 1))
                mm.then_inc(ans_ready, 1)


E1, F1, FC1 = 8, 176, 88
NX1 = E1 + 2
TH = T // 2


def moe1(nc, ident, xnT, WrT, Wgu, Wd, out):
    FN = F1 // FC1
    with ExitStack() as ctx:
        sp = Space(nc, ctx, "m1")
        gw = sp.sb("gw", [P, DC, E1])
        index_weight = sp.sb("index_weight", [P, NT, E1])
        gate = sp.sb("gate", [P, 5, NT, E1])
        weight = sp.sb("weight", [P, NT, NX1])
        wcol = sp.sb("wcol", [P, 2, NT])
        small = sp.sb("small", [P, 6, NT])
        wgu = sp.sb("wgu", [P, 2, DC, 2, F1])
        wd = sp.sb("wd", [FC1, 2, FN, D])
        silu = sp.sb("silu", [FC1, 2, TH])
        gu = sp.sb("gu", [FC1, FN, T])
        acc = sp.sb("acc", [P, NT, D])
        psum = sp.ps("banks", [P, 8, BANK])
        bank = [psum[:, i, :] for i in range(8)]
        names = ("set_up", "loaded", "logits_ready", "to_exp", "exp_done", "own", "w_in", "g_ready", "u_ready",
                 "silu_done", "gu_done", "o_ready", "o_done", "wcol_in", "stored", "weighted")
        (set_up, loaded, logits_ready, to_exp, exp_done, own_, w_in, g_ready, u_ready, silu_done, gu_done,
         o_ready, o_done, wcol_in, stored, weighted) = (sp.sem(n) for n in names)
        passed = sp.sem("passed")
        logits = bank[0][:, 0:NT * E1].rearrange("p (n e) -> p n e", n=NT)
        NQ = FN * 2
        block = ctx.enter_context(nc.Block())

        @block.gpsimd
        def _(pool):
            pool.iota(index_weight[:, :, :], [[0, NT], [-1, E1]], E1, 0,
                      allow_small_or_imprecise_dtypes=True).then_inc(set_up, 1)
            pool.memset(gate[:, 0], 0.0).then_inc(set_up, 1)
            pool.memset(weight[:, :, E1:NX1], 1.0).then_inc(set_up, 1)
            pool.memset(acc[:, :, :], 0.0).then_inc(set_up, 1)

        @block.sync
        def _(sync):
            sync.dma_start(gw[:, :, :], WrT.rearrange("(c p) e -> p c e", p=P)).then_inc(loaded, 16)
            with sync.Fori(0, NX1 // 2) as i:
                for j in range(2):
                    sync.wait_ge(o_ready, 2 * NT * i)
                    sync.dma_start(wgu[:, j], Wgu[2 * i + j]).then_inc(w_in, 16)
                    sync.dma_start(wd[:, j], Wd[2 * i + j]).then_inc(w_in, 16)
                    wait_apart(sync, w_in, 64 * i + 32 * (j + 1), passed)
            full, rest = token_tiles(out)
            sync.wait_ge(o_done, NT * NX1)
            sync.dma_start(full, acc[:, 0:NT - 1, :]).then_inc(stored, 16)
            sync.dma_start(rest, acc[0:TR, NT - 1, :]).then_inc(stored, 16)
            sync.wait_ge(stored, 32)

        @block.scalar
        def _(act):
            act.wait_ge(to_exp, 1)
            act.activation(gate[:, 2], gate[:, 2], ACT.Exp).then_inc(exp_done, 1)
            with act.Fori(0, NX1 // 2) as i:
                for j in range(2):
                    for q in range(NQ):
                        m = NQ * j + q
                        act.wait_ge(g_ready, 2 * NQ * i + m + 1)
                        if m >= 2:
                            act.wait_ge(gu_done, 2 * NQ * i + m - 1)
                        else:
                            act.wait_ge(gu_done, 2 * NQ * i)
                        act.activation(silu[:, q % 2, :], bank[q % 2][0:FC1, 0:TH], ACT.Silu).then_inc(silu_done, 1)

        @block.vector
        def _(dve):
            own = Chain(dve, own_)
            dve.wait_ge(set_up, 4)
            prob_, masks = route(sp, own, logits_ready, (to_exp, exp_done), logits, gate, small, 2, E1,
                                 index_weight[:, :, :])
            own(dve.tensor_tensor(masks[0], masks[0], masks[1], ALU.add))
            dve.tensor_tensor(weight[:, :, 0:E1], prob_, masks[0], ALU.mult).then_inc(weighted, 1)
            dve.wait_ge(weighted, 1)
            with dve.Fori(0, NX1 // 2) as i:
                dve.wait_ge(o_done, 2 * NT * i)
                dve.tensor_copy(wcol[:, :, :], weight[:, :, bass.ds(2 * i, 2)].rearrange("p n e -> p e n")
                                ).then_inc(wcol_in, 1)
                for j in range(2):
                    for q in range(NQ):
                        c, half = q // 2, q % 2
                        m = NQ * j + q
                        dve.wait_ge(silu_done, 2 * NQ * i + m + 1)
                        dve.wait_ge(u_ready, 2 * NQ * i + m + 1)
                        if q == 0:
                            dve.wait_ge(o_ready, 2 * NT * i + NT * j)
                        dve.tensor_tensor(gu[:, c, half * TH:(half + 1) * TH], silu[:, q % 2, :],
                                          bank[2 + q % 2][0:FC1, 0:TH], ALU.mult).then_inc(gu_done, 1)
                    if j == 0:
                        dve.wait_ge(wcol_in, i + 1)
                    for n in range(NT):
                        rows = P if n < NT - 1 else TR
                        dve.wait_ge(o_ready, 2 * NT * i + NT * j + n + 1)
                        if j:
                            dve.wait_ge(o_done, 2 * NT * i + n + 1)
                        dve.scalar_tensor_tensor(out=acc[0:rows, n, :], in0=bank[4 + n % 4][0:rows, 0:D],
                                                 scalar=wcol[0:rows, j, n:n + 1], in1=acc[0:rows, n, :],
                                                 op0=ALU.mult, op1=ALU.add).then_inc(o_done, 1)

        @block.tensor
        def _(pe):
            pe.wait_ge(loaded, 16)
            for n in range(NT):
                rows = P if n < NT - 1 else TR
                for k in range(DC):
                    mm = pe.matmul(logits[0:rows, n, :], xnT[:, k, n * P:n * P + rows], gw[:, k, :],
                                   start=(k == 0), stop=(k == DC - 1))
            mm.then_inc(logits_ready, 1)
            pe.wait_ge(to_exp, 1)
            with pe.Fori(0, NX1 // 2) as i:
                for j in range(2):
                    pe.wait_ge(w_in, 64 * i + 32 * (j + 1))
                    for q in range(NQ):
                        c, half = q // 2, q % 2
                        m = NQ * j + q
                        for which, ready in ((0, g_ready), (1, u_ready)):
                            pe.wait_ge(gu_done, 2 * NQ * i + max(m - 1, 0))
                            for k in range(DC):
                                mm = pe.matmul(bank[2 * which + q % 2][0:FC1, 0:TH],
                                               wgu[:, j, k, which, c * FC1:(c + 1) * FC1],
                                               xnT[:, k, half * TH:(half + 1) * TH],
                                               start=(k == 0), stop=(k == DC - 1))
                            mm.then_inc(ready, 1)
                    pe.wait_ge(gu_done, 2 * NQ * i + NQ * (j + 1))
                    for n in range(NT):
                        rows = P if n < NT - 1 else TR
                        pe.wait_ge(o_done, 2 * NT * i + max(NT * j + n - 3, 0))
                        for c in range(FN):
                            mm = pe.matmul(bank[4 + n % 4][0:rows, 0:D], gu[:, c, n * P:n * P + rows],
                                           wd[:, j, c, :], start=(c == 0), stop=(c == FN - 1))
                        mm.then_inc(o_ready, 1)


H1, HD1 = 16, 16
F16 = mybir.dt.float16
NR = 4
RK = B * SE // NR
CH = -(-RK // P)
CR = RK - (CH - 1) * P
NM = -(-RK // BANK)
LW = RK - (NM - 1) * BANK
LCH = -(-LW // P)
LN255 = float(np.log(255.0))
QT1 = T // P
NMAIN = H1 * QT1
NLEFT = H1 // 4
NTILE = NMAIN + NLEFT


def kv1(nc, ident, identb, ones, ctxT, Wkv, bkv, k_dram, v_dram, sv_dram):
    rows_of = lambda c: P if c < CH - 1 else CR
    C = H1 * HD1
    with ExitStack() as ctx:
        sp = Space(nc, ctx, "kv")
        w = sp.sb("w", [P, DC, 2 * C])
        bias = sp.sb("bias", [P, 2 * C])
        cx = sp.sb("ctx", [P, DC, RK])
        vrow = sp.sb("vrow", [P, NR * CH, C])
        vint = sp.sb("vint", [P, H1, NR * CH, HD1], BF16)
        kb = sp.sb("kb", [P, 2, C])
        kst = sp.sb("kst", [P, 2, 3, H1])
        khat = sp.sb("khat", [P, 2, C])
        ksplit = sp.sb("ksplit", [P, 2, H1, 2, HD1], F16)
        kT = sp.sb("kT", [P, 2, 4, BANK], F16)
        vmax = sp.sb("vmax", [P, C])
        vcol = sp.sb("vcol", [P, DC, 3])
        vdiag = sp.sb("vdiag", [P, DC, P])
        vsc = sp.sb("vsc", [P, C])
        id16 = sp.sb("id16", [P, P], F16)
        psum = sp.ps("kvp", [P, 3, BANK])
        tps = [sp.ps(f"tp{i}", [P, 4, P], F16) for i in range(3)]
        xps = sp.ps("xp", [P, 2, BANK])
        names = ("w_in", "cx_used", "kv_ready", "kv_evac", "own", "split", "turned", "t_evac",
                  "vm_ready", "vt_ready", "vd_done", "vs_ready", "stored", "id_done", "v_done", "sv_done")
        (w_in, cx_used, kv_ready, kv_evac, own_, split, turned, t_evac, vm_ready, vt_ready,
         vd_done, vs_ready, stored, id_done, v_done, sv_done) = (sp.sem(n) for n in names)
        cx_in = [sp.sem(f"cx_in{m}") for m in range(NM)]
        stored_k = [sp.sem(f"stored_k{i}") for i in range(2)]
        block = ctx.enter_context(nc.Block())
        width = [BANK] * (NM - 1) + [LW]

        @block.sync
        def _(sync):
            sync.dma_start(w[:, :, :], Wkv.rearrange("(c p) n -> p c n", p=P)).then_inc(w_in, 16)
            sync.dma_start(bias[:, :], bkv.to_broadcast([P, 2 * C])).then_inc(w_in, 16)
            with sync.Fori(0, NR) as r:
                for m in range(NM):
                    sync.wait_ge(cx_used, NM * r + m + 1)
                    at = m * BANK
                    sync.dma_start(cx[:, :, at:at + width[m]],
                                   ctxT[:, :, bass.ds(r * RK + at, width[m])].rearrange("c p n -> p c n")
                                   ).then_inc(cx_in[m], 16)
                for m in range(NM):
                    sync.wait_ge(t_evac, CH * r + min(4 * (m + 1), CH))
                    for i in range(4):
                        dst = k_dram.rearrange("(q i) (g r) n -> i g r q n", i=4, g=NR)
                        dst = dst[i, bass.ds(r, 1), :, :, m * BANK:m * BANK + width[m]].rearrange(
                            "a r q n -> (a r) q n")
                        sync.dma_start(dst, kT[32 * i:32 * i + 32, m % 2, :, 0:width[m]]).then_inc(stored_k[m % 2], 16)
            sync.wait_ge(sv_done, 1)
            sync.dma_start(sv_dram.rearrange("(c p) a -> p c a", p=P), vcol[:, :, 1:2],
                           allow_slow_non_contiguous=True).then_inc(stored, 16)
            sync.wait_ge(v_done, 1)
            sync.dma_start(v_dram.rearrange("h p c d -> p h (c d)"),
                           vint[:, :, :, :].rearrange("p h c d -> p h (c d)")).then_inc(stored, 16)
            sync.wait_ge(stored, 32)
            for i in range(2):
                sync.wait_ge(stored_k[i], 16 * 4 * NR * NM // 2)

        @block.gpsimd
        def _(pool):
            pool.tensor_copy(id16[:, :], ident[:, :]).then_inc(id_done, 1)
            for r in range(NR):
                i = pool.memset(vrow[:, (r + 1) * CH - 1, :], 0.0)
            i.then_inc(id_done, 1)

        @block.tensor
        def _(pe):
            pe.nop().then_inc(cx_used, NM)
            pe.wait_ge(w_in, 32)
            pe.wait_ge(id_done, 2)
            with pe.Fori(0, NR) as r:
                def turn(c):
                    n = rows_of(c)
                    pe.wait_ge(split, CH * r + c + 1)
                    if c < 3:
                        pe.wait_ge(t_evac, CH * r)
                    else:
                        pe.wait_ge(t_evac, CH * r + c - 2)
                    for q in range(4):
                        mm = pe.transpose(tps[c % 3][:, q, 0:n],
                                          ksplit[0:n, c % 2, 4 * q:4 * q + 4].rearrange("p h s d -> p (h s d)"),
                                          id16[0:n, 0:n])
                    mm.then_inc(turned, 1)

                for c in range(CH):
                    n = rows_of(c)
                    if c % 4 == 0:
                        pe.wait_ge(cx_in[c // 4], 16 * (r + 1))
                    if c < 3:
                        pe.wait_ge(kv_evac, CH * r)
                    else:
                        pe.wait_ge(kv_evac, CH * r + c - 2)
                    for k in range(DC):
                        mm = pe.matmul(psum[0:n, c % 3, :], cx[:, k, c * P:c * P + n], w[:, k, :],
                                       start=(k == 0), stop=(k == DC - 1))
                    mm.then_inc(kv_ready, 1)
                    if c % 4 == 3 or c == CH - 1:
                        pe.nop().then_inc(cx_used, 1)
                    if c >= 2:
                        turn(c - 2)
                turn(CH - 2)
                turn(CH - 1)
            pe.wait_ge(vm_ready, 1)
            for k in range(DC):
                mm = pe.transpose(xps[:, 0, k * P:(k + 1) * P], vmax[:, k * P:(k + 1) * P], ident[:, :])
            mm.then_inc(vt_ready, 1)
            pe.wait_ge(vd_done, 1)
            for k in range(DC):
                mm = pe.matmul(xps[:, 1, k * P:(k + 1) * P], ones[:, :], vdiag[:, k, :], start=True, stop=True)
            mm.then_inc(vs_ready, 1)

        @block.scalar
        def _(act):
            with act.Fori(0, NR) as r:
                for c in range(CH):
                    n = rows_of(c)
                    m = c // 4
                    if c % 4 == 0:
                        act.wait_ge(stored_k[m % 2], 16 * 4 * (NM // 2 * r + m // 2))
                    act.wait_ge(turned, CH * r + c + 1)
                    at = (c % 4) * P
                    act.copy(kT[:, m % 2, :, at:at + n], tps[c % 3][:, :, 0:n]).then_inc(t_evac, 1)

        @block.vector
        def _(dve):
            wide = lambda n: [n, H1, HD1]
            heads = lambda ap: ap.rearrange("p (h d) -> p h d", h=H1)
            dve.wait_ge(w_in, 32)
            dve.wait_ge(id_done, 2)
            OWN = 8
            with dve.Fori(0, NR) as r:
                own = Chain(dve, own_, (OWN * CH) * r)
                for c in range(CH):
                    n, b = rows_of(c), c % 2
                    k_, st, kh = kb[0:n, b, :], kst[0:n, b], khat[0:n, b, :]
                    dve.wait_ge(kv_ready, CH * r + c + 1)
                    own(dve.tensor_tensor(k_, psum[0:n, c % 3, 0:C], bias[0:n, 0:C], ALU.add))
                    dve.tensor_tensor(vrow[0:n, bass.ds(r * CH + c, 1), :].rearrange("p a d -> p (a d)"),
                                      psum[0:n, c % 3, C:2 * C], bias[0:n, C:2 * C], ALU.add).then_inc(kv_evac, 1)
                    own(dve.tensor_reduce(st[:, 0, :], heads(k_), AX.X, ALU.max, apply_absolute_value=True))
                    own(dve.tensor_scalar(st[:, 1, :], st[:, 0, :], 1.0 / 127.0, 1e-8, ALU.mult, ALU.max))
                    own(dve.reciprocal(st[:, 2, :], st[:, 1, :]))
                    own(dve.tensor_tensor(heads(k_), heads(k_), st[:, 2, :].unsqueeze(2).to_broadcast(wide(n)),
                                          ALU.mult))
                    own(dve.tensor_scalar(k_, k_, ROUND, ROUND, ALU.add, ALU.subtract))
                    own(dve.tensor_tensor(heads(kh), heads(k_), st[:, 1, :].unsqueeze(2).to_broadcast(wide(n)),
                                          ALU.mult))
                    if c >= 2:
                        dve.wait_ge(turned, CH * r + c - 1)
                    else:
                        dve.wait_ge(turned, CH * r)
                    hi, lo = ksplit[0:n, b, :, 0, :], ksplit[0:n, b, :, 1, :]
                    own(dve.tensor_copy(hi, heads(kh)))
                    dve.tensor_tensor(lo, heads(kh), hi, ALU.subtract).then_inc(split, 1)
            own = Chain(dve, own_, OWN * CH * NR)
            dve.wait_ge(kv_evac, NR * CH)
            dve.tensor_reduce(vmax[:, :], vrow[:, :, :].rearrange("p c d -> p d c"), AX.X, ALU.max,
                              apply_absolute_value=True).then_inc(vm_ready, 1)
            dve.wait_ge(vt_ready, 1)
            own(dve.tensor_reduce(vcol[:, :, 0], xps[:, 0, 0:C].rearrange("p (k n) -> p k n", k=DC), AX.X, ALU.max))
            own(dve.tensor_scalar(vcol[:, :, 1], vcol[:, :, 0], 1.0 / 127.0, 1e-8, ALU.mult, ALU.max))
            dve.nop().then_inc(sv_done, 1)
            own(dve.reciprocal(vcol[:, :, 2], vcol[:, :, 1]))
            for k in range(DC):
                i = dve.tensor_scalar(vdiag[:, k, :], ident[:, :], vcol[:, k, 2:3], None, ALU.mult)
                own(i)
            dve.nop().then_inc(vd_done, 1)
            dve.wait_ge(vs_ready, 1)
            own(dve.tensor_copy(vsc[:, :], xps[:, 1, 0:C]))
            half = NR * CH // 2
            for j in range(2):
                v = vrow[:, j * half:(j + 1) * half, :]
                own(dve.tensor_tensor(v, v, vsc[:, :].unsqueeze(1).to_broadcast([P, half, C]), ALU.mult))
            for j in range(2):
                v = vrow[:, j * half:(j + 1) * half, :]
                i = dve.tensor_scalar(vint[:, :, j * half:(j + 1) * half, :].rearrange("p h c d -> p c h d"),
                                      v.rearrange("p c (h d) -> p c h d", h=H1), ROUND, ROUND, ALU.add, ALU.subtract)
                own(i)
            dve.nop().then_inc(v_done, 1)
            dve.nop().then_inc(own_, 1)


def q1(nc, ident, xnT, Wq, bq, q_dram, nsq_dram, nsql_dram):
    C = H1 * HD1
    scale = float(HD1) ** -0.5
    with ExitStack() as ctx:
        sp = Space(nc, ctx, "q1")
        w = sp.sb("w", [P, DC, C])
        bias = sp.sb("bias", [P, C])
        q = sp.sb("q", [P, NT, C])
        st = sp.sb("st", [P, 4, NT, H1])
        nsq_t = sp.sb("nsq_t", [P, H1, QT1])
        qrep = sp.sb("qrep", [P, NT, H1, 8, HD1], F16)
        qT = sp.sb("qT", [P, 2, T], F16)
        id16 = sp.sb("id16", [P, P], F16)
        psum = sp.ps("qp", [P, 4, BANK])
        tps = [sp.ps(f"tp{i}", [P, T], F16) for i in range(2)]
        names = ("w_in", "q_ready", "q_evac", "own", "rep", "turned", "t_evac", "stored", "id_done", "nsq")
        (w_in, q_ready, q_evac, own_, rep, turned, t_evac, stored, id_done, nsq) = (
            sp.sem(n) for n in names)
        stored_q = [sp.sem(f"stored_q{i}") for i in range(2)]
        block = ctx.enter_context(nc.Block())
        rows_of = lambda n: P if n < NT - 1 else TR

        @block.sync
        def _(sync):
            sync.dma_start(w[:, :, :], Wq.rearrange("(c p) n -> p c n", p=P)).then_inc(w_in, 16)
            sync.dma_start(bias[:, :], bq.to_broadcast([P, C])).then_inc(w_in, 16)
            sync.wait_ge(nsq, 1)
            sync.dma_start(nsq_dram, nsq_t[:, :, :].rearrange("p h n -> p (h n)")).then_inc(stored, 16)
            sync.dma_start(nsql_dram, st[0:TR, 3, NT - 1, :]).then_inc(stored, 16)
            for h in range(H1):
                sync.wait_ge(t_evac, h + 1)
                sync.dma_start(q_dram[h], qT[:, h % 2, :]).then_inc(stored_q[h % 2], 16)
            sync.wait_ge(stored, 32)
            for i in range(2):
                sync.wait_ge(stored_q[i], 16 * H1 // 2)

        @block.gpsimd
        def _(pool):
            pool.tensor_copy(id16[:, :], ident[:, :]).then_inc(id_done, 1)
            pool.memset(q[:, NT - 1, :], 0.0).then_inc(id_done, 1)

        @block.tensor
        def _(pe):
            pe.wait_ge(w_in, 32)
            for n in range(NT):
                rows = rows_of(n)
                for k in range(DC):
                    mm = pe.matmul(psum[0:rows, n // 2, (n % 2) * C:(n % 2 + 1) * C], xnT[:, k, n * P:n * P + rows],
                                   w[:, k, :], start=(k == 0), stop=(k == DC - 1))
                mm.then_inc(q_ready, 1)
            pe.wait_ge(rep, 1)
            pe.wait_ge(id_done, 2)
            for h in range(H1):
                if h >= 2:
                    pe.wait_ge(t_evac, h - 1)
                for n in range(NT):
                    rows = rows_of(n)
                    mm = pe.transpose(tps[h % 2][:, n * P:n * P + rows],
                                      qrep[0:rows, n, h].rearrange("p s d -> p (s d)"), id16[0:rows, 0:rows])
                mm.then_inc(turned, 1)

        @block.scalar
        def _(act):
            for h in range(H1):
                act.wait_ge(turned, h + 1)
                if h >= 2:
                    act.wait_ge(stored_q[h % 2], 16 * (h // 2))
                act.copy(qT[:, h % 2, :], tps[h % 2][:, :]).then_inc(t_evac, 1)

        @block.vector
        def _(dve):
            own = Chain(dve, own_)
            dve.wait_ge(w_in, 32)
            dve.wait_ge(id_done, 2)
            for n in range(NT):
                rows = rows_of(n)
                if n % 2 == 0:
                    dve.wait_ge(q_ready, min(n + 2, NT))
                own(dve.tensor_tensor(q[0:rows, n, :], psum[0:rows, n // 2, (n % 2) * C:(n % 2 + 1) * C],
                                      bias[0:rows, :], ALU.add))
            qh = q[:, :, :].rearrange("p n (h d) -> p n h d", h=H1)
            own(dve.tensor_scalar(q[:, :, :], q[:, :, :], scale, None, ALU.mult))
            own(dve.tensor_reduce(st[:, 0], qh, AX.X, ALU.max, apply_absolute_value=True))
            own(dve.tensor_scalar(st[:, 1], st[:, 0], 1.0 / 127.0, 1e-8, ALU.mult, ALU.max))
            own(dve.reciprocal(st[:, 2], st[:, 1]))
            own(dve.tensor_scalar(st[:, 3], st[:, 1], -1.0, None, ALU.mult))
            dve.tensor_copy(nsq_t[:, :, :].rearrange("p h n -> p n h"), st[:, 3, 0:QT1]).then_inc(nsq, 1)
            own(dve.tensor_tensor(qh, qh, st[:, 2].unsqueeze(3).to_broadcast([P, NT, H1, HD1]), ALU.mult))
            own(dve.tensor_scalar(q[:, :, :], q[:, :, :], ROUND, ROUND, ALU.add, ALU.subtract))
            for n in range(NT):
                i = dve.tensor_copy(qrep[:, n], qh[:, n].unsqueeze(2).to_broadcast([P, H1, 8, HD1]))
                own(i)
            dve.nop().then_inc(rep, 1)
            dve.nop().then_inc(own_, 1)


def attention1(nc, ident, q_dram, nsq_dram, nsql_dram, k_dram, v_dram, sv_dram, Wp, bp, out):
    C = H1 * HD1
    width = [BANK] * (NM - 1) + [LW]
    NU = 2 * NM
    NX = 16
    blocks = [(m, g) for m in range(NM) for g in range(NR)]
    assert len(blocks) == 24 and NTILE % 2 == 0
    with ExitStack() as ctx:
        sp = Space(nc, ctx, "a1")
        kb = sp.sb("kb", [P, 2, RK], F16)
        vb = sp.sb("vb", [P, 2, NR * CH, HD1], BF16)
        qb = sp.sb("qb", [P, 2, T], F16)
        kl = sp.sb("kl", [P, 2, 4, RK], F16)
        vl = sp.sb("vl", [P, 2, 4, NR * CH, HD1], BF16)
        ql = sp.sb("ql", [P, H1, TR], F16)
        nsq = sp.sb("nsq", [P, NTILE])
        sq = sp.sb("sq", [P, NTILE])
        svb = sp.sb("svb", [P, C])
        pi = sp.sb("pi", [P, 2, NR, BANK], I16)
        pb = sp.sb("pb", [P, 2, NR * BANK], BF16)
        pl = sp.sb("pl", [P, NR, LCH * P], BF16)
        pt = sp.sb("pt", [P, NM, NR * 4, P], BF16)
        mx = sp.sb("mx", [P, 2, NX])
        nb = sp.sb("nb", [P, 2, 2])
        sums = sp.sb("sums", [P, 4, NU])
        osc = sp.sb("osc", [P, 2, 2])
        ao = sp.sb("ao", [P, NT, C])
        aoT = sp.sb("aoT", [P, DC, T])
        wp = sp.sb("wp", [P, DC, D])
        bpb = sp.sb("bpb", [P, D])
        res = sp.sb("res", [P, NT, D])
        psum = sp.ps("banks", [P, 8, BANK])
        OB = 7
        names = ("w_in", "kv_in0", "kv_in1", "kl_in0", "kl_in1", "a_ready", "a_done", "max_found", "osc_done", "sq_done", "pool_own", "b_ready", "exp_done", "bias_done",
                 "conv_done", "pv_part", "o_evac", "own", "set_up", "aot_ready", "aot_evac",
                 "res_ready", "res_done", "stored")
        (w_in, kv_in0, kv_in1, kl_in0, kl_in1, a_ready, a_done, max_found, osc_done, sq_done, pool_own, b_ready, exp_done, bias_done, conv_done, pv_part,
         o_evac, own_, set_up, aot_ready, aot_evac, res_ready, res_done, stored) = (
             sp.sem(n) for n in names)
        passed = sp.sem("passed")
        kv_in, kl_in = (kv_in0, kv_in1), (kl_in0, kl_in1)
        pt_in = [sp.sem(f"pt_in{m}") for m in range(NM)]
        block = ctx.enter_context(nc.Block())

        def main_tile(par, qt):
            def operands(m, g):
                r = slice(32 * g, 32 * g + 32)
                return [(qb[r, par, qt * P:(qt + 1) * P], kb[r, par, m * BANK:m * BANK + width[m]], slice(0, P))]
            return operands, lambda c: vb[:, par, c, :]

        def left_tile(lt):
            def operands(m, g):
                r = slice(32 * g, 32 * g + 32)
                return [(ql[r, 4 * lt + i, :], kl[r, lt % 2, i, m * BANK:m * BANK + width[m]],
                         slice(32 * i, 32 * i + 32)) for i in range(4)]
            return operands, lambda c: vl[:, lt % 2, :, c, :]

        @block.sync
        def _(sync):
            sync.dma_start(nsq[:, 0:NMAIN], nsq_dram).then_inc(w_in, 16)
            for i in range(4):
                sync.dma_start(nsq[32 * i:32 * i + 32, NMAIN:NTILE],
                               nsql_dram.rearrange("t (l i) -> i t l", i=4)[i],
                               allow_slow_non_contiguous=True).then_inc(w_in, 16)
            sync.dma_start(svb[:, :], sv_dram.rearrange("n a -> a n").to_broadcast([P, C])).then_inc(w_in, 16)
            sync.dma_start(ql[:, :, :], q_dram[:, :, QT1 * P:T].rearrange("h p t -> p h t")).then_inc(w_in, 16)
            sync.dma_start(wp[:, :, :], Wp.rearrange("(c p) n -> p c n", p=P)).then_inc(w_in, 16)
            sync.dma_start(bpb[:, :], bp.to_broadcast([P, D])).then_inc(w_in, 16)

            def head(h, par):
                sync.dma_start(kb[:, par, :], k_dram[h]).then_inc(kv_in[par], 16)
                sync.dma_start(qb[:, par, :], q_dram[h]).then_inc(kv_in[par], 16)
                sync.dma_start(vb[:, par].rearrange("p c d -> p (c d)"),
                               v_dram[h].rearrange("p c d -> p (c d)")).then_inc(kv_in[par], 16)

            def left_keys(lt):
                sync.dma_start(kl[:, lt % 2], k_dram[4 * lt:4 * lt + 4].rearrange("h p n -> p h n")
                               ).then_inc(kl_in[lt % 2], 16)

            def left_values(lt):
                sync.dma_start(vl[:, lt % 2].rearrange("p h c d -> p h (c d)"),
                               v_dram[4 * lt:4 * lt + 4].rearrange("h p c d -> p h (c d)")).then_inc(kl_in[lt % 2], 16)

            def turns(tile):
                for m in range(NM):
                    wait_apart(sync, conv_done, 2 + NM * tile + m + 1, passed)
                    wait_apart(sync, pv_part, NU * tile + 2 * m + 2, passed)
                    if m < NM - 1:
                        sync.dma_start_transpose(pt[:, m], pb[:, m % 2, :]).then_inc(pt_in[m], 16)
                    else:
                        sync.dma_start_transpose(pt[:, m, 0:NR * LCH], pl[:, :, :].rearrange("p g n -> p (g n)")
                                                 ).then_inc(pt_in[m], 16)

            def pair(hp, last):
                for par in range(2):
                    for qt in range(QT1):
                        turns(hp * (2 * QT1) + par * QT1 + qt)
                        if qt == 0 and par == 0:
                            head(hp * 2 + 1, 1)
                        if qt == 0 and par == 1 and not last:
                            head(hp * 2 + 2, 0)

            sync.wait_ge(set_up, 1)
            head(0, 0)
            for lt in range(2):
                left_keys(lt)
                left_values(lt)
            with sync.Fori(0, H1 // 2 - 1) as hp:
                pair(hp, False)
            pair(H1 // 2 - 1, True)
            for lt in range(NLEFT):
                turns(NMAIN + lt)
                if lt + 2 < NLEFT:
                    left_keys(lt + 2)
                if 1 <= lt < NLEFT - 1:
                    left_values(lt + 1)
            full, rest = token_tiles(out)
            sync.wait_ge(res_done, NT)
            sync.dma_start(full, res[:, 0:NT - 1, :]).then_inc(stored, 16)
            sync.dma_start(rest, res[0:TR, NT - 1, :]).then_inc(stored, 16)
            sync.wait_ge(stored, 32)

        @block.gpsimd
        def _(pool):
            pool.memset(vb[:, 1], 0.0).then_inc(set_up, 1)
            for m in range(NM):
                pool.memset(pt[:, m], 0.0).then_inc(pt_in[m], 16)
            pool.memset(pl[:, :, :], 0.0).then_inc(pool_own, 1)
            pool.wait_ge(pool_own, 1)
            pool.nop().then_inc(conv_done, 2)
            with pool.Fori(0, NTILE // 2) as i:
                for j in range(2):
                    tile = 2 * i + j
                    for m in range(NM):
                        wait_apart(pool, exp_done, 2 + NU * tile + 2 * m + 2, passed)
                        before, back = ((4, 1), (3, 1), (0, 0), (1, 0), (2, 0), (5, 1))[m]
                        wait_apart(pool, pt_in[before], 16 * (tile + 2 - back), passed)
                        if m < NM - 1:
                            pool.tensor_scalar(pb[:, m % 2, :], pi[:, m % 2].rearrange("p g n -> p (g n)"), 1.0, 0.0,
                                               ALU.mult, ALU.add).then_inc(conv_done, 1)
                        else:
                            pool.tensor_scalar(pl[:, :, 0:LW], pi[:, m % 2, :, 0:LW], 1.0, 0.0,
                                               ALU.mult, ALU.add).then_inc(conv_done, 1)

        @block.scalar
        def _(act):
            act.nop().then_inc(exp_done, 2)
            act.wait_ge(sq_done, 1)
            with act.Fori(0, NTILE // 4) as i:
                for j in range(4):
                    tile = 4 * i + j
                    act.wait_ge(bias_done, tile + 1)
                    act.wait_ge(o_evac, tile)
                    for n in range(NU):
                        m, g = n // 2, 2 * (n % 2)
                        w = width[m]
                        wait_apart(act, b_ready, NU * tile + n + 1, passed)
                        if n % 2 == 0:
                            wait_apart(act, conv_done, NM * tile + m + 1, passed)
                        act.activation(pi[:, m % 2, g:g + 2, 0:w], psum[:, 3 + g:5 + g, 0:w], ACT.Exp,
                                       bias=nb[:, j % 2, 1:2], scale=sq[:, bass.ds(tile, 1)],
                                       accum_out=sums[:, j, n:n + 1]).then_inc(exp_done, 1)

        @block.vector
        def _(dve):
            own = Chain(dve, own_)
            dve.nop().then_inc(o_evac, 3)
            dve.wait_ge(w_in, 16 * 9)
            dve.tensor_scalar(sq[:, :], nsq[:, :], -1.0, None, ALU.mult).then_inc(sq_done, 1)

            def maximum(tile, j, first=False):
                for p in range(NX // 2):
                    k = 3 * p
                    w = width[blocks[k][0]]
                    dve.wait_ge(a_ready, NX * tile + 2 * p + 1)
                    dve.tensor_reduce(mx[:, j % 2, 2 * p:2 * p + 1], psum[:, 0:2, 0:w], AX.XY,
                                      ALU.max).then_inc(a_done, 1)
                    w = width[blocks[k + 2][0]]
                    dve.wait_ge(a_ready, NX * tile + 2 * p + 2)
                    dve.tensor_reduce(mx[:, j % 2, 2 * p + 1:2 * p + 2], psum[:, 2, 0:w], AX.X,
                                      ALU.max).then_inc(a_done, 1)
                if not first:
                    dve.wait_ge(exp_done, NU * tile - 10)
                dve.wait_ge(a_done, NX * (tile + 1))
                dve.tensor_reduce(nb[:, j % 2, 0:1], mx[:, j % 2, :], AX.X, ALU.max).then_inc(max_found, 1)
                dve.wait_ge(max_found, tile + 1)
                dve.tensor_scalar(nb[:, j % 2, 1:2], nb[:, j % 2, 0:1], nsq[:, tile_col(tile)], LN255,
                                  ALU.mult, ALU.add).then_inc(bias_done, 1)

            def tile_col(tile):
                return slice(tile, tile + 1) if isinstance(tile, int) else bass.ds(tile, 1)

            def outputs(tile, slot, places):
                dve.wait_ge(pv_part, NU * (tile + 2))
                dve.tensor_reduce(osc[:, slot % 2, 0:1], sums[:, slot % 4, :], AX.X, ALU.add).then_inc(osc_done, 1)
                dve.wait_ge(osc_done, 2 * tile + 1)
                dve.reciprocal(osc[:, slot % 2, 1:2], osc[:, slot % 2, 0:1]).then_inc(osc_done, 1)
                dve.wait_ge(osc_done, 2 * tile + 2)
                for rows, cols, dst, scales in places:
                    i = dve.scalar_tensor_tensor(out=dst, in0=psum[rows, OB, cols],
                                                 scalar=osc[rows, slot % 2, 1:2], in1=scales,
                                                 op0=ALU.mult, op1=ALU.mult)
                i.then_inc(o_evac, 1)

            def head_places(h, qt):
                at = slice(h * HD1, (h + 1) * HD1) if isinstance(h, int) else bass.ds(h * HD1, HD1)
                return [(slice(0, P), slice(0, HD1), ao[:, qt, at], svb[:, at])]

            def left_places(lt):
                out_ = []
                for i in range(4):
                    at = slice((4 * lt + i) * HD1, (4 * lt + i + 1) * HD1)
                    rows = slice(32 * i, 32 * i + 32)
                    out_.append((rows, slice(HD1 * i, HD1 * (i + 1)), ao[0:TR, NT - 1, at], svb[rows, at]))
                return out_

            maximum(0, 0, True)
            maximum(1, 1, True)
            with dve.Fori(0, NMAIN // 12 - 1) as i:
                for j in range(12):
                    maximum(12 * i + j + 2, j)
                    outputs(12 * i + j, j, head_places(2 * i + j // 6, j % 6))
            for t in range(NMAIN - 12, NTILE):
                if t + 2 < NTILE:
                    maximum(t + 2, t)
                if t < NMAIN:
                    outputs(t, t, head_places(t // 6, t % 6))
                else:
                    outputs(t, t, left_places(t - NMAIN))
            for j in range(4):
                c, n0 = j // 2, 4 * (j % 2)
                w = min(4 * P, T - n0 * P)
                dve.wait_ge(aot_ready, j + 1)
                dve.tensor_copy(aoT[:, c, n0 * P:n0 * P + w], psum[:, j, 0:w]).then_inc(aot_evac, 1)
            for n in range(NT):
                rows = P if n < NT - 1 else TR
                dve.wait_ge(res_ready, n + 1)
                dve.tensor_tensor(res[0:rows, n, :], psum[0:rows, 4 + n % 3, 0:D], bpb[0:rows, :],
                                  ALU.add).then_inc(res_done, 1)

        @block.tensor
        def _(pe):
            def a_block(ops, k, tile, first=False):
                p = k // 3
                if k % 3 != 1 and not (first and p == 0):
                    pe.wait_ge(a_done, NX * tile + 2 * (p - 1) + (1 if k % 3 == 0 else 2))
                for lhsT, rhs, rows in ops(*blocks[k]):
                    mm = pe.matmul(psum[rows, k % 3, 0:width[blocks[k][0]]], lhsT, rhs, start=True, stop=True)
                if k % 3:
                    mm.then_inc(a_ready, 1)

            def b_unit(ops, n, tile):
                pe.wait_ge(exp_done, NU * tile + n + 1)
                m = n // 2
                for g in (2 * (n % 2), 2 * (n % 2) + 1):
                    for lhsT, rhs, rows in ops(m, g):
                        mm = pe.matmul(psum[rows, 3 + g, 0:width[m]], lhsT, rhs, start=True, stop=True)
                mm.then_inc(b_ready, 1)

            def pv_piece(values, cols, k, tile):
                m = k // 2
                if k == 0:
                    pe.wait_ge(o_evac, tile + 2)
                if k % 2 == 0:
                    pe.wait_ge(pt_in[m], 16 * (tile + 1))
                n_ch = 4 if m < NM - 1 else LCH
                for g in (2 * (k % 2), 2 * (k % 2) + 1):
                    for j in range(n_ch):
                        c = 4 * m + j
                        rows = P if c < CH - 1 else CR
                        mm = pe.matmul(psum[:, OB, 0:cols], pt[0:rows, m, n_ch * g + j, :],
                                       values(g * CH + c)[0:rows], start=(k == 0 and g == 0 and j == 0),
                                       stop=(k == NU - 1 and g == NR - 1 and j == n_ch - 1))
                mm.then_inc(pv_part, 1)

            pieces = [[k for k in range(NU) if 2 + k * 10 // 12 == n] for n in range(NU)]

            def body(tile, cur, nxt, prev, prev_cols=HD1):
                for n in range(NU):
                    if cur is not None:
                        b_unit(cur[0], n, tile)
                    if nxt is not None:
                        a_block(nxt[0], 2 * n, tile + 1)
                        a_block(nxt[0], 2 * n + 1, tile + 1)
                    for k in pieces[n]:
                        pv_piece(prev[1], prev_cols, k, tile)

            def pair(hp, last):
                for par in range(2):
                    for qt in range(QT1):
                        tile = hp * (2 * QT1) + par * QT1 + qt
                        prev = main_tile(par, qt - 1) if qt else main_tile(1 - par, QT1 - 1)
                        if qt < QT1 - 1:
                            nxt = main_tile(par, qt + 1)
                        elif par == 0:
                            pe.wait_ge(kv_in[1], 48 * (hp + 1))
                            nxt = main_tile(1, 0)
                        elif not last:
                            pe.wait_ge(kv_in[0], 48 * (hp + 2))
                            nxt = main_tile(0, 0)
                        else:
                            pe.wait_ge(kl_in[0], 32)
                            nxt = left_tile(0)
                        body(tile, main_tile(par, qt), nxt, prev)

            pe.wait_ge(w_in, 16 * 9)
            pe.wait_ge(set_up, 1)
            pe.wait_ge(kv_in[0], 48)
            first = main_tile(0, 0)
            for k in range(len(blocks)):
                a_block(first[0], k, 0, True)
            with pe.Fori(0, H1 // 2 - 1) as hp:
                pair(hp, False)
            pair(H1 // 2 - 1, True)
            for lt in range(NLEFT):
                if lt + 1 < NLEFT:
                    pe.wait_ge(kl_in[(lt + 1) % 2], 32 if lt < 1 else 48)
                if lt >= 3:
                    pe.wait_ge(kl_in[(lt - 1) % 2], 64)
                body(NMAIN + lt, left_tile(lt), left_tile(lt + 1) if lt + 1 < NLEFT else None,
                     left_tile(lt - 1) if lt else main_tile(1, QT1 - 1), 4 * HD1 if lt else HD1)
            pe.wait_ge(kl_in[(NLEFT - 1) % 2], 64)
            body(NTILE, None, None, left_tile(NLEFT - 1), 4 * HD1)
            pe.wait_ge(o_evac, 3 + NTILE)
            for j in range(4):
                c, n0 = j // 2, 4 * (j % 2)
                for n in range(n0, min(n0 + 4, NT)):
                    rows = P if n < NT - 1 else TR
                    at = (n - n0) * P
                    mm = pe.transpose(psum[:, j, at:at + rows], ao[0:rows, n, c * P:(c + 1) * P], ident[0:rows, 0:rows])
                mm.then_inc(aot_ready, 1)
            pe.wait_ge(aot_evac, 4)
            for n in range(NT):
                rows = P if n < NT - 1 else TR
                if n >= 3:
                    pe.wait_ge(res_done, n - 2)
                for c in range(DC):
                    mm = pe.matmul(psum[0:rows, 4 + n % 3, 0:D], aoT[:, c, n * P:n * P + rows], wp[:, c, :],
                                   start=(c == 0), stop=(c == DC - 1))
                mm.then_inc(res_ready, 1)


def build_program(nc, a, out):
    def dram(name, shape, dt=F32):
        return nc.dram_tensor(name, shape, dt, kind="Internal").ap()

    xa, xb, xc = (dram(f"x_{n}", (T, D)) for n in "abc")
    add0, add1, add2, add3 = (dram(f"add_{n}", (T, D)) for n in range(4))
    q_dram = dram("q_int", (H1, P, T), F16)
    nsq_dram, nsql_dram = dram("q_scale", (P, NMAIN)), dram("q_scale_last", (TR, H1))
    k_dram = dram("k_split", (H1, P, RK), F16)
    v_dram = dram("v_int", (H1, P, NR * CH, HD1), BF16)
    sv_dram = dram("v_scale", (H1 * HD1, 1))
    with ExitStack() as ctx:
        sp = Space(nc, ctx, "all")
        ident, ones, xnT = sp.sb("ident", [P, P]), sp.sb("ones", [P, P]), sp.sb("xnT", [P, DC, T])
        identb = sp.sb("identb", [P, P], BF16)
        constants(nc, ident, identb, ones)
        layer_norm(nc, "ln0", ident, a["x"], None, None, None, xnT)
        attention0(nc, ident, xnT, a["ctxT"], a["mask"], a["Wq0"], a["bq0"], a["Wk0"], a["bk0"], a["Wv0"], a["bv0"],
                   a["Wo0"], a["qn_w"], a["kn_w"], add0.rearrange("(b s) d -> b s d", b=B))
        with nc.sbuf_tensor("all_xrow", [P, NT, D], F32) as xrow:
            layer_norm(nc, "ln1", ident, a["x"], add0, a["g_xattn"][0:1, 0:1], xa, xnT, xrow)
            moe0(nc, ident, ones, xnT, xrow, a["gateT0"], a["wi0"], a["wo0"], add1)
        layer_norm(nc, "ln2", ident, xa, add1, a["g_ffn"][0:1, 0:1], xb, xnT)
        kv1(nc, ident, identb, ones, a["ctxT"], a["Wkv1"], a["bkv1"], k_dram, v_dram, sv_dram)
        q1(nc, ident, xnT, a["Wq1"], a["bq1"], q_dram, nsq_dram, nsql_dram)
        attention1(nc, ident, q_dram, nsq_dram, nsql_dram, k_dram, v_dram, sv_dram, a["Wp1"], a["bp1"], add2)
        layer_norm(nc, "ln3", ident, xb, add2, a["g_xattn"][0:1, 1:2], xc, xnT)
        moe1(nc, ident, xnT, a["gateT1"], a["Wgu1"], a["Wd1"], add3)
        layer_norm(nc, "end", ident, xc, add3, a["g_ffn"][0:1, 1:2], out, None)


def lay_out(i):
    row = lambda v: v.reshape(1, -1)
    col = lambda v: v.reshape(-1, 1)
    gate = np.concatenate([i["L1_ffn_Wg"], i["L1_ffn_Wsg"].reshape(2, F1, D)])
    up = np.concatenate([i["L1_ffn_Wu"], i["L1_ffn_Wsu"].reshape(2, F1, D)])
    gate_up = np.stack([gate, up], 1).reshape(NX1, 2, F1, DC, P).transpose(0, 4, 3, 1, 2)
    down = np.concatenate([i["L1_ffn_Wd"], i["L1_ffn_Wsd"].reshape(D, 2, F1).transpose(1, 0, 2)])
    down = down.reshape(NX1, D, F1 // FC1, FC1).transpose(0, 3, 2, 1)
    return {
        "x": i["x"].reshape(T, D),
        "ctxT": i["ctx_2048"].reshape(B * SE, DC, P).transpose(1, 2, 0),
        "mask": i["mask_1xSxS2_ff0"].reshape(S, SE),
        "g_xattn": row(i["g_xattn"]), "g_ffn": row(i["g_ffn"]),
        "Wq0": i["L0_xattn_Wq"], "bq0": row(i["L0_xattn_bq"]), "Wk0": i["L0_xattn_Wk"], "bk0": row(i["L0_xattn_bk"]),
        "Wv0": i["L0_xattn_Wv"], "bv0": row(i["L0_xattn_bv"]), "Wo0": i["L0_xattn_Wo"],
        "qn_w": col(i["L0_xattn_qn_w"]), "kn_w": col(i["L0_xattn_kn_w"]),
        "gateT0": i["L0_ffn_gate_weight"].T, "wi0": i["L0_ffn_wi"], "wo0": i["L0_ffn_wo"],
        "Wq1": i["L1_xattn_Wq"], "bq1": row(i["L1_xattn_bq"]), "Wkv1": i["L1_xattn_Wkv"],
        "bkv1": row(i["L1_xattn_bkv"]), "Wp1": i["L1_xattn_Wp"], "bp1": row(i["L1_xattn_bp"]),
        "gateT1": i["L1_ffn_Wr"].T, "Wgu1": gate_up, "Wd1": down,
    }


def kernel(**inputs):
    import concourse.bacc as bacc
    from concourse.bass_utils import run_bass_kernel_spmd

    arrays = {n: np.ascontiguousarray(v) for n, v in lay_out({k: np.asarray(v) for k, v in inputs.items()}).items()}
    nc = bacc.Bacc("TRN2", target_bir_lowering=False, num_devices=1)
    args = {n: nc.dram_tensor(f"in_{n}", v.shape, mybir.dt.from_np(v.dtype), kind="ExternalInput").ap()
            for n, v in arrays.items()}
    out = nc.dram_tensor("out", (T, D), F32, kind="ExternalOutput").ap()
    build_program(nc, args, out)
    r = run_bass_kernel_spmd(nc, [{f"in_{n}": v for n, v in arrays.items()}], core_ids=[0])
    return r.results[0]["out"].reshape(B, S, D)
```

```python
from contextlib import ExitStack

import numpy as np
import concourse.bass as bass
from concourse import mybir

F32 = mybir.dt.float32
BF16 = mybir.dt.bfloat16
I16 = mybir.dt.int16
I32 = mybir.dt.int32
ALU = mybir.AluOpType
ACT = mybir.ActivationFunctionType
AX = mybir.AxisListType

P = 128
BANK = 512
B = 8
S = 100
T = B * S
NT = -(-T // P)
TR = T - (NT - 1) * P
SE = 1444
D = 256
DC = D // P
LN_EPS = 1e-5
RMS_EPS = 1e-6
HUGE = 3.0e38
ROUND = 12582912.0


class Space:

    def __init__(self, nc, ctx, stage):
        self.nc, self.ctx, self.stage, self.sems = nc, ctx, stage, []
        ctx.callback(self.release)

    def release(self):
        if self.sems:
            self.nc.clear_and_free_semaphores(self.sems)
            self.nc.all_engine_barrier()

    def sb(self, name, shape, dt=F32):
        return self.ctx.enter_context(self.nc.sbuf_tensor(f"{self.stage}_{name}", shape, dt))

    def ps(self, name, shape, dt=F32):
        return self.ctx.enter_context(self.nc.psum_tensor(f"{self.stage}_{name}", shape, dt))

    def sem(self, name):
        self.sems.append(self.nc.alloc_semaphore(f"{self.stage}_{name}"))
        return self.sems[-1]


class Chain:

    def __init__(self, eng, sem, base=0):
        self.eng, self.sem, self.base, self.n = eng, sem, base, 0

    def __call__(self, ins):
        self.n += 1
        ins.then_inc(self.sem, 1)
        self.eng.wait_ge(self.sem, self.base + self.n)


def wait_apart(eng, sem, value, passed):
    eng.wait_ge(sem, value)
    eng.sem_inc(passed, 1)


def token_tiles(ap):
    full = ap[0:(NT - 1) * P, :].rearrange("(n p) d -> p n d", p=P)
    return full, ap[(NT - 1) * P:T, :]


def make_identity(pool, ident, zeroed, done):
    pool.memset(ident[:, :], 0.0).then_inc(zeroed, 1)
    pool.wait_ge(zeroed, 1)
    pool.affine_select(out=ident[:, :], in_=ident[:, :], compare_op=ALU.not_equal, fill=1.0, base=0,
                       pattern=[[-1, P]], channel_multiplier=1).then_inc(done, 1)


def constants(nc, ident, identb, ones):
    with ExitStack() as ctx:
        sp = Space(nc, ctx, "const")
        zeroed, zeroedb, made = sp.sem("zeroed"), sp.sem("zeroedb"), sp.sem("made")
        block = ctx.enter_context(nc.Block())

        @block.gpsimd
        def _(pool):
            make_identity(pool, ident, zeroed, made)
            make_identity(pool, identb, zeroedb, made)
            pool.memset(ones[:, :], 1.0).then_inc(made, 1)


def layer_norm(nc, stage, ident, x_src, add_src, gate, x_dst, xnT, xrow=None):
    with ExitStack() as ctx:
        sp = Space(nc, ctx, stage)
        x = sp.sb("x", [P, NT, D])
        y = xrow if xrow is not None else sp.sb("y", [P, NT, D])
        sq = sp.sb("sq", [P, NT, D])
        add = sp.sb("add", [P, NT, D]) if add_src is not None else None
        g = sp.sb("g", [P, 2])
        stat = sp.sb("stat", [P, 4, NT])
        xt = [sp.ps(f"xt{i}", [P, BANK]) for i in range(4)]
        loaded, cleared, gated, tanhed, summed = (sp.sem(n) for n in
                                                  ("loaded", "cleared", "gated", "tanhed", "summed"))
        dve_own, sqrted, normed, turned, evac, stored, var_ready = (
            sp.sem(n) for n in ("dve_own", "sqrted", "normed", "turned", "evac", "stored", "var_ready"))
        block = ctx.enter_context(nc.Block())
        n_loads = 2 + (3 if add is not None else 0)
        x_full, x_rest = token_tiles(x_src)

        @block.sync
        def _(sp_):
            sp_.wait_ge(cleared, 1)
            sp_.dma_start(x[:, 0:NT - 1, :], x_full).then_inc(loaded, 16)
            sp_.dma_start(x[0:TR, NT - 1, :], x_rest).then_inc(loaded, 16)
            if add is not None:
                a_full, a_rest = token_tiles(add_src)
                sp_.dma_start(add[:, 0:NT - 1, :], a_full).then_inc(loaded, 16)
                sp_.dma_start(add[0:TR, NT - 1, :], a_rest).then_inc(loaded, 16)
                sp_.dma_start(g[:, 0:1], gate.to_broadcast([P, 1])).then_inc(loaded, 16)
            if x_dst is not None:
                d_full, d_rest = token_tiles(x_dst)
                sp_.wait_ge(summed, 1)
                sp_.dma_start(d_full, x[:, 0:NT - 1, :]).then_inc(stored, 16)
                sp_.dma_start(d_rest, x[0:TR, NT - 1, :]).then_inc(stored, 16)
                sp_.wait_ge(stored, 32)

        @block.scalar
        def _(act):
            if add is not None:
                act.wait_ge(loaded, 16 * n_loads)
                act.activation(g[:, 1:2], g[:, 0:1], ACT.Tanh).then_inc(tanhed, 1)
            if xnT is not None:
                act.wait_ge(var_ready, 1)
                act.activation(stat[:, 2, :], stat[:, 1, :], ACT.Sqrt).then_inc(sqrted, 1)

        @block.vector
        def _(dve):
            own = Chain(dve, dve_own)
            own(dve.memset(x[:, NT - 1, :], 0.0))
            if add is not None:
                own(dve.memset(add[:, NT - 1, :], 0.0))
            dve.memset(stat[:, :, :], 0.0).then_inc(cleared, 1)
            dve.wait_ge(cleared, 1)
            dve.wait_ge(loaded, 16 * n_loads)
            if add is not None:
                dve.wait_ge(tanhed, 1)
                dve.scalar_tensor_tensor(out=x[:, :, :], in0=add[:, :, :], scalar=g[:, 1:2], in1=x[:, :, :],
                                         op0=ALU.mult, op1=ALU.add).then_inc(summed, 1)
                dve.wait_ge(summed, 1)
            if xnT is None:
                return
            own(dve.tensor_reduce(stat[:, 0, :], x[:, :, :], AX.X, ALU.add))
            own(dve.tensor_scalar(stat[:, 0, :], stat[:, 0, :], 1.0 / D, None, ALU.mult))
            own(dve.tensor_tensor(y[:, :, :], x[:, :, :], stat[:, 0, :].unsqueeze(2).to_broadcast([P, NT, D]), ALU.subtract))
            own(dve.tensor_tensor(sq[:, :, :], y[:, :, :], y[:, :, :], ALU.mult))
            own(dve.tensor_reduce(stat[:, 1, :], sq[:, :, :], AX.X, ALU.add))
            dve.tensor_scalar(stat[:, 1, :], stat[:, 1, :], 1.0 / D, LN_EPS, ALU.mult, ALU.add).then_inc(var_ready, 1)
            dve.wait_ge(sqrted, 1)
            own(dve.reciprocal(stat[:, 3, :], stat[:, 2, :]))
            dve.tensor_tensor(y[:, :, :], y[:, :, :], stat[:, 3, :].unsqueeze(2).to_broadcast([P, NT, D]),
                              ALU.mult).then_inc(normed, 1)
            for j in range(4):
                c, n0 = j // 2, 4 * (j % 2)
                w = min(4 * P, T - n0 * P)
                dve.wait_ge(turned, j + 1)
                dve.tensor_copy(xnT[:, c, n0 * P:n0 * P + w], xt[j][:, 0:w]).then_inc(evac, 1)

        @block.tensor
        def _(pe):
            if xnT is None:
                return
            pe.wait_ge(normed, 1)
            for j in range(4):
                c, n0 = j // 2, 4 * (j % 2)
                tiles = range(n0, min(n0 + 4, NT))
                for n in tiles:
                    rows = P if n < NT - 1 else TR
                    at = (n - n0) * P
                    mm = pe.transpose(xt[j][:, at:at + rows], y[0:rows, n, c * P:(c + 1) * P],
                                      ident[0:rows, 0:rows])
                mm.then_inc(turned, 1)


NH, NKV, HD = 16, 4, 128
KC = -(-SE // P)
KR = SE - (KC - 1) * P
SOFT = float(HD) ** -0.5


def attention0(nc, ident, xnT, ctxT, mask, Wq, bq, Wk, bk, Wv, bv, Wo, qn_w, kn_w, out):
    G = NH // NKV
    parts = [(n * BANK, min(BANK, SE - n * BANK)) for n in range(-(-SE // BANK))]
    NP = len(parts)
    NJ = 8
    NSQ = KC * NKV + NH
    TG = 4
    NG = KC // TG
    rows_of = lambda c: P if c < KC - 1 else KR
    with ExitStack() as ctx:
        sp = Space(nc, ctx, "a0")
        wq = sp.sb("wq", [P, DC, NH * HD])
        wk = sp.sb("wk", [P, DC, NKV * HD])
        wv = sp.sb("wv", [P, DC, NKV * HD])
        wo = sp.sb("wo", [P, NH, D])
        bk_all = sp.sb("bk", [P, NKV * HD])
        bv_all = sp.sb("bv", [P, NKV * HD])
        bq_all = sp.sb("bq", [S, NH, HD])
        qn_col = sp.sb("qn", [P, 2])
        kn_col = sp.sb("kn", [P, 1])
        maskt = sp.sb("mask", [S, SE])
        xb = sp.sb("xb", [P, DC, S])
        cx = sp.sb("ctx", [P, DC, SE])
        krow = sp.sb("krow", [P, KC, NKV * HD])
        KT = sp.sb("KT", [P, NKV, SE])
        V = sp.sb("V", [P, KC, NKV * HD])
        QO = sp.sb("QO", [P, NH, S])
        orow = sp.sb("orow", [S, NH, HD])
        prob = sp.sb("prob", [S, 2, SE])
        PT = sp.sb("PT", [P, NG, TG * S])
        kstat = sp.sb("kstat", [P, 4, KC * NKV])
        qstat = sp.sb("qstat", [S, 4, NH])
        soft = sp.sb("soft", [S, 4, NH])
        junk = sp.sb("junk", [P, NJ, HD])
        ores = sp.sb("ores", [S, D])
        psum = sp.ps("banks", [P, 8, BANK])
        flat = psum[:, :, :].rearrange("p b n -> p (b n)")
        bank = [psum[:, i, :] for i in range(8)]
        SB = [bank[0:3], bank[3:6]]
        score_of = [flat[0:S, 0:SE], flat[0:S, 3 * BANK:3 * BANK + SE]]
        BO = bank[7]

        def turn_bank(unit):
            i = unit - NG * (NH - 2)
            return 6 if i < 0 else (6, 0, 1, 2, 6, 0)[i]

        names = ("wq_in", "wkv_in", "bias_in", "mask_in", "wo_in", "ctx_in", "x_in", "kv_ready", "kv_evac", "squared", "k_var",
                 "k_sd", "k_rs", "k_norm", "turned", "turned_evac", "q_ready", "q_evac", "q_var", "q_sd",
                 "q_rs", "q_norm", "s_ready", "max_found", "max_done", "sum_turned", "exp_done", "pt_ready", "pt_evac_act", "pt_evac_dve",
                 "pv_done", "o_evac", "ot_ready", "ot_evac", "wo_ready", "wo_evac", "stored", "set_up", "own")
        (wq_in, wkv_in, bias_in, mask_in, wo_in, ctx_in, x_in, kv_ready, kv_evac, squared, k_var, k_sd, k_rs, k_norm, turned,
         turned_evac, q_ready, q_evac, q_var, q_sd, q_rs, q_norm, s_ready, max_found, max_done, sum_turned,
         exp_done, pt_ready, pt_evac_act, pt_evac_dve, pv_done, o_evac, ot_ready, ot_evac, wo_ready, wo_evac, stored, set_up,
         own_) = (sp.sem(n) for n in names)
        passed = sp.sem("passed")
        after = [[(False, c - 2)] if c >= 2 else [] for c in range(KC + 2)]
        for n in range(4):
            after[4 + n].append((True, n))
        units = [u for step in after for u in step]
        NUNIT = len(units)
        block = ctx.enter_context(nc.Block())

        @block.sync
        def _(sync):
            sync.dma_start(wq[:, :, :], Wq.rearrange("(c p) n -> p c n", p=P)).then_inc(wq_in, 16)
            sync.dma_start(xb[:, :, :], xnT[:, :, 0:S]).then_inc(x_in, 16)
            sync.dma_start(bq_all[:, :, :].rearrange("p h d -> p (h d)"), bq.to_broadcast([S, NH * HD])).then_inc(bias_in, 16)
            sync.dma_start(qn_col[:, 0:1], qn_w).then_inc(bias_in, 16)
            sync.dma_start(kn_col[:, :], kn_w).then_inc(bias_in, 16)
            sync.dma_start(bk_all[:, :], bk.to_broadcast([P, NKV * HD])).then_inc(bias_in, 16)
            sync.dma_start(bv_all[:, :], bv.to_broadcast([P, NKV * HD])).then_inc(bias_in, 16)
            sync.dma_start(wk[:, :, :], Wk.rearrange("(c p) n -> p c n", p=P)).then_inc(wkv_in, 16)
            sync.dma_start(wv[:, :, :], Wv.rearrange("(c p) n -> p c n", p=P)).then_inc(wkv_in, 16)

            def batch(b):
                sync.wait_ge(kv_ready, 2 * KC * b)
                sync.dma_start(cx[:, :, :], ctxT[:, :, bass.ds(b * SE, SE)].rearrange("c p n -> p c n")).then_inc(ctx_in, 16)
                sync.wait_ge(q_ready, 4 * b)
                sync.dma_start(xb[:, :, :], xnT[:, :, bass.ds(b * S, S)]).then_inc(x_in, 16)

            sync.dma_start(cx[:, :, :], ctxT[:, :, 0:SE].rearrange("c p n -> p c n")).then_inc(ctx_in, 16)
            sync.dma_start(maskt[:, :], mask).then_inc(mask_in, 16)
            sync.dma_start(wo[:, :, :], Wo.rearrange("(h p) n -> p h n", p=P)).then_inc(wo_in, 16)
            with sync.Fori(0, B - 1) as b:
                batch(b + 1)
                sync.wait_ge(wo_evac, b + 1)
                sync.dma_start(out[b], ores[:, :]).then_inc(stored, 16)
            sync.wait_ge(wo_evac, B)
            sync.dma_start(out[B - 1], ores[:, :]).then_inc(stored, 16)
            sync.wait_ge(stored, 16 * B)

        @block.gpsimd
        def _(pool):
            with pool.Fori(0, B) as b:
                for c in range(KC):
                    n = rows_of(c)
                    wait_apart(pool, k_rs, KC * b + c + 1, passed)
                    for g in range(NKV):
                        i = pool.tensor_scalar(krow[0:n, c, g * HD:(g + 1) * HD], krow[0:n, c, g * HD:(g + 1) * HD],
                                               kstat[0:n, 3, c * NKV + g:c * NKV + g + 1], 0.0, ALU.mult, ALU.add)
                    i.then_inc(k_norm, 1)

        @block.tensor
        def _(pe):
            pe.wait_ge(wq_in, 16)
            with pe.Fori(0, B) as b:
                pe.wait_ge(x_in, 16 * (b + 1))
                for n in range(4):
                    for k in range(DC):
                        mm = pe.matmul(bank[n][0:S, :], xb[:, k, :], wq[:, k, n * BANK:(n + 1) * BANK],
                                       start=(k == 0), stop=(k == DC - 1))
                    mm.then_inc(q_ready, 1)
                pe.wait_ge(ctx_in, 16 * (b + 1))
                pe.wait_ge(wkv_in, 32)

                def project(c):
                    n = rows_of(c)
                    for j, w in enumerate((wk, wv)):
                        if c < 3:
                            pe.wait_ge(wo_evac, b)
                            pe.wait_ge(q_evac, 4 * b + (1 if c + j == 0 else 4))
                        else:
                            pe.wait_ge(kv_evac, 2 * KC * b + 2 * (c - 3) + j + 1)
                        for k in range(DC):
                            mm = pe.matmul(SB[j][c % 3][0:n, :], cx[:, k, c * P:c * P + n], w[:, k, :],
                                           start=(k == 0), stop=(k == DC - 1))
                        mm.then_inc(kv_ready, 1)

                def transpose(unit):
                    queries, m = unit
                    i = units.index(unit)
                    if i >= 2:
                        wait_apart(pe, turned_evac, NUNIT * b + i - 1, passed)
                    to = bank[6 + i % 2]
                    if queries:
                        wait_apart(pe, q_norm, 4 * b + m + 1, passed)
                        for h in range(4):
                            mm = pe.transpose(to[:, h * S:(h + 1) * S], orow[:, 4 * m + h, :], ident[0:S, 0:S])
                    else:
                        n = rows_of(m)
                        wait_apart(pe, k_norm, KC * b + m + 1, passed)
                        for g in range(NKV):
                            mm = pe.transpose(to[:, g * P:g * P + n], krow[0:n, m, g * HD:(g + 1) * HD],
                                              ident[0:n, 0:n])
                    mm.then_inc(turned, 1)

                for c in range(len(after)):
                    if c < KC:
                        project(c)
                    for unit in after[c]:
                        transpose(unit)
                pe.wait_ge(turned_evac, NUNIT * (b + 1))

                def scores(h, n):
                    if n == 0 and h >= 2:
                        pe.wait_ge(max_done, NH * b + h - 1)
                    at, w = parts[n]
                    mm = pe.matmul(SB[h % 2][n][0:S, 0:w], QO[:, h, :], KT[:, h // G, at:at + w],
                                   start=True, stop=True)
                    if n == NP - 1:
                        mm.then_inc(s_ready, 1)

                def left_psum(unit):
                    h, g = divmod(unit, NG)
                    if g == 1:
                        pe.wait_ge(pt_evac_dve, NH * b + h + 1)
                    else:
                        pe.wait_ge(pt_evac_act, 2 * NH * b + 2 * h + g // 2 + 1)

                def turn(h, g):
                    if g == 0:
                        pe.wait_ge(exp_done, NH * b + h + 1)
                    unit = NG * h + g
                    last = [u for u in range(unit) if turn_bank(u) == turn_bank(unit)]
                    if last:
                        left_psum(last[-1])
                    else:
                        pe.wait_ge(pt_evac_act, 2 * NH * b)
                    to = bank[turn_bank(unit)]
                    for j in range(TG):
                        c = TG * g + j
                        n = rows_of(c)
                        mm = pe.transpose(to[0:n, j * S:(j + 1) * S], prob[:, h % 2, c * P:c * P + n],
                                          ident[0:S, 0:S])
                    mm.then_inc(pt_ready, 1)

                def weigh(h, g):
                    if g == 0:
                        pe.wait_ge(o_evac, NH * b + h)
                    left_psum(NG * h + g)
                    for j in range(TG):
                        c = TG * g + j
                        n = rows_of(c)
                        mm = pe.matmul(BO[0:S, 0:HD], PT[0:n, g, j * S:(j + 1) * S],
                                       V[0:n, c, (h // G) * HD:(h // G + 1) * HD],
                                       start=(c == 0), stop=(c == KC - 1))
                    mm.then_inc(pv_done, 1)

                for h in range(2):
                    for n in range(NP):
                        scores(h, n)
                for h in range(NH - 2):
                    turn(h, 0)
                    scores(h + 2, 0)
                    turn(h, 1)
                    weigh(h, 0)
                    scores(h + 2, 1)
                    turn(h, 2)
                    weigh(h, 1)
                    scores(h + 2, 2)
                    weigh(h, 2)
                for g in range(NG):
                    turn(NH - 2, g)
                for g in range(NG):
                    weigh(NH - 2, g)
                    turn(NH - 1, g)
                for g in range(NG):
                    weigh(NH - 1, g)
                pe.wait_ge(o_evac, NH * (b + 1))
                for n in range(4):
                    for h in range(4):
                        mm = pe.transpose(bank[n][:, h * S:(h + 1) * S], orow[:, 4 * n + h, :], ident[0:S, 0:S])
                    mm.then_inc(ot_ready, 1)
                pe.wait_ge(ot_evac, 4 * (b + 1))
                pe.wait_ge(wo_in, 16)
                for h in range(NH):
                    mm = pe.matmul(bank[4][0:S, 0:D], QO[:, h, :], wo[:, h, :], start=(h == 0), stop=(h == NH - 1))
                mm.then_inc(wo_ready, 1)

        @block.vector
        def _(dve):
            own0 = Chain(dve, own_)
            own0(dve.memset(kstat[:, :, :], 1.0))
            dve.wait_ge(bias_in, 16 * 5)
            own0(dve.tensor_scalar(qn_col[:, 1:2], qn_col[:, 0:1], SOFT, None, ALU.mult))
            dve.nop().then_inc(set_up, 1)
            with dve.Fori(0, B) as b:
                dve.wait_ge(ot_ready, 4 * b)
                for n in range(4):
                    dve.wait_ge(q_ready, 4 * b + n + 1)
                    dve.tensor_tensor(orow[:, 4 * n:4 * n + 4, :],
                                      bank[n][0:S, :].rearrange("p (h d) -> p h d", h=4),
                                      bq_all[:, 4 * n:4 * n + 4, :], ALU.add).then_inc(q_evac, 1)
                for c in range(KC + 2):
                    if c >= 2:
                        at = (slice(0, rows_of(c - 2)), slice((c - 2) * NKV, (c - 1) * NKV))
                        dve.wait_ge(k_sd, KC * b + c - 1)
                        dve.reciprocal(kstat[at[0], 3, at[1]], kstat[at[0], 2, at[1]]).then_inc(k_rs, 1)
                    if c < KC:
                        n = rows_of(c)
                        dve.wait_ge(kv_ready, 2 * KC * b + 2 * c + 1)
                        if c == 0:
                            dve.wait_ge(turned, NUNIT * b)
                        dve.tensor_tensor(krow[0:n, c, :], SB[0][c % 3][0:n, :], bk_all[0:n, :],
                                          ALU.add).then_inc(kv_evac, 1)
                    if 1 <= c <= KC:
                        at = (slice(0, rows_of(c - 1)), slice((c - 1) * NKV, c * NKV))
                        dve.wait_ge(squared, NSQ * b + NH + c * NKV)
                        dve.tensor_scalar(kstat[at[0], 1, at[1]], kstat[at[0], 0, at[1]], 1.0 / HD, RMS_EPS, ALU.mult,
                                          ALU.add).then_inc(k_var, 1)
                    if c < KC:
                        dve.wait_ge(kv_ready, 2 * KC * b + 2 * c + 2)
                        if c == 0:
                            dve.wait_ge(pv_done, NG * NH * b)
                        dve.tensor_tensor(V[0:n, c, :], SB[1][c % 3][0:n, :], bv_all[0:n, :],
                                          ALU.add).then_inc(kv_evac, 1)
                    if c == 0:
                        dve.wait_ge(squared, NSQ * b + NH)
                        dve.tensor_scalar(qstat[:, 1, :], qstat[:, 0, :], 1.0 / HD, RMS_EPS, ALU.mult,
                                          ALU.add).then_inc(q_var, 1)
                    if c == 1:
                        dve.wait_ge(q_sd, b + 1)
                        dve.reciprocal(qstat[:, 3, :], qstat[:, 2, :]).then_inc(q_rs, 1)
                    if 2 <= c < 6:
                        hs = slice(4 * (c - 2), 4 * (c - 1))
                        dve.wait_ge(q_rs, b + 1)
                        dve.tensor_tensor(orow[:, hs, :], orow[:, hs, :],
                                          qstat[:, 3, hs].unsqueeze(2).to_broadcast([S, 4, HD]),
                                          ALU.mult).then_inc(q_norm, 1)

                def maximum(h):
                    wait_apart(dve, s_ready, NH * b + h + 1, passed)
                    if h >= 2:
                        wait_apart(dve, pt_ready, NG * NH * b + NG * (h - 1), passed)
                    dve.tensor_tensor_reduce(prob[:, h % 2, :], score_of[h % 2], maskt[:, :], 1.0, -HUGE,
                                             ALU.add, ALU.max, soft[:, 0, h:h + 1]).then_inc(max_found, 1)
                    dve.wait_ge(max_found, NH * b + h + 1)
                    dve.tensor_scalar(soft[:, 1, h:h + 1], soft[:, 0, h:h + 1], -1.0, None,
                                      ALU.mult).then_inc(max_done, 1)

                dve.wait_ge(mask_in, 16)
                maximum(0)
                maximum(1)
                for h in range(NH):
                    dve.wait_ge(pt_ready, NG * NH * b + NG * h + 2)
                    dve.wait_ge(pv_done, NG * NH * b + max(NG * (h - 1) + 2, 0))
                    dve.tensor_copy(PT[:, 1, :], bank[turn_bank(NG * h + 1)][:, 0:TG * S]).then_inc(pt_evac_dve, 1)
                    dve.wait_ge(exp_done, NH * b + h + 1)
                    dve.reciprocal(soft[:, 3, h:h + 1], soft[:, 2, h:h + 1]).then_inc(sum_turned, 1)
                    dve.wait_ge(pv_done, NG * NH * b + NG * (h + 1))
                    dve.wait_ge(sum_turned, NH * b + h + 1)
                    dve.tensor_scalar(orow[:, h, :], BO[0:S, 0:HD], soft[:, 3, h:h + 1], None,
                                      ALU.mult).then_inc(o_evac, 1)
                    if h + 2 < NH:
                        maximum(h + 2)
                dve.wait_ge(wo_ready, b + 1)
                dve.wait_ge(stored, 16 * b)
                dve.tensor_copy(ores[:, :], bank[4][0:S, 0:D]).then_inc(wo_evac, 1)

        @block.scalar
        def _(act):
            act.wait_ge(set_up, 1)
            with act.Fori(0, B) as b:
                for h in range(NH):
                    if h % 4 == 0:
                        act.wait_ge(q_evac, 4 * b + h // 4 + 1)
                    act.wait_ge(squared, NSQ * b + max(h - NJ + 1, 0))
                    act.activation(junk[0:S, h % NJ, :], orow[:, h, :], ACT.Square,
                                   accum_out=qstat[:, 0, h:h + 1]).then_inc(squared, 1)
                for c in range(len(after)):
                    if c < KC:
                        n = rows_of(c)
                        act.wait_ge(kv_evac, 2 * KC * b + 2 * c + 1)
                        for g in range(NKV):
                            m = c * NKV + g
                            act.wait_ge(squared, NSQ * b + NH + m - NJ + 1)
                            act.activation(junk[0:n, (NH + m) % NJ, :], krow[0:n, c, g * HD:(g + 1) * HD], ACT.Square,
                                           accum_out=kstat[0:n, 0, m:m + 1]).then_inc(squared, 1)
                    if c == 0:
                        act.wait_ge(q_var, b + 1)
                        act.activation(qstat[:, 2, :], qstat[:, 1, :], ACT.Sqrt).then_inc(q_sd, 1)
                    if 1 <= c <= KC:
                        at = (slice(0, rows_of(c - 1)), slice((c - 1) * NKV, c * NKV))
                        act.wait_ge(k_var, KC * b + c)
                        act.activation(kstat[at[0], 2, at[1]], kstat[at[0], 1, at[1]], ACT.Sqrt).then_inc(k_sd, 1)
                    for queries, m in after[c]:
                        i = units.index((queries, m))
                        act.wait_ge(turned, NUNIT * b + i + 1)
                        if queries:
                            act.activation(QO[:, 4 * m:4 * m + 4, :].rearrange("p h s -> p (h s)"),
                                           bank[6 + i % 2][:, 0:4 * S], ACT.Copy, scale=qn_col[:, 1:2]
                                           ).then_inc(turned_evac, 1)
                        else:
                            n = rows_of(m)
                            act.activation(KT[:, :, m * P:m * P + n],
                                           bank[6 + i % 2].rearrange("p (g n) -> p g n", g=NKV)[:, :, 0:n],
                                           ACT.Copy, scale=kn_col[:, 0:1]).then_inc(turned_evac, 1)

                def exponential(h):
                    act.wait_ge(max_done, NH * b + h + 1)
                    act.activation(prob[:, h % 2, :], prob[:, h % 2, :], ACT.Exp, bias=soft[:, 1, h:h + 1],
                                   accum_out=soft[:, 2, h:h + 1]).then_inc(exp_done, 1)

                exponential(0)
                for h in range(NH):
                    for g in (0, 2):
                        act.wait_ge(pt_ready, NG * NH * b + NG * h + g + 1)
                        act.wait_ge(pv_done, NG * NH * b + max(NG * (h - 1) + g + 1, 0))
                        of = bank[turn_bank(NG * h + g)]
                        if g < NG - 1:
                            act.copy(PT[:, g, :], of[:, 0:TG * S]).then_inc(pt_evac_act, 1)
                            if h + 1 < NH:
                                exponential(h + 1)
                        else:
                            act.copy(PT[:, g, 0:(TG - 1) * S], of[:, 0:(TG - 1) * S])
                            act.copy(PT[0:KR, g, (TG - 1) * S:], of[0:KR, (TG - 1) * S:TG * S]).then_inc(pt_evac_act, 1)
                for n in range(4):
                    act.wait_ge(ot_ready, 4 * b + n + 1)
                    act.copy(QO[:, 4 * n:4 * n + 4, :].rearrange("p h s -> p (h s)"),
                             bank[n][:, 0:4 * S]).then_inc(ot_evac, 1)


E0, I0 = 8, 1024
CAP = int(np.floor(1.25 * T / E0))
CAP = max(CAP + CAP % 2, 4)


def route(sp, own, pe_logits, exped, logits, gate, small, top, E, index_weight):
    dve = own.eng
    G, work, prob_ = gate[:, 0], gate[:, 1], gate[:, 2]
    masks = [gate[:, 3 + i] for i in range(top)]
    wide = [P, NT, E]
    dve.wait_ge(pe_logits, 1)
    own(dve.tensor_copy(gate[:, 0, 0:NT - 1, :], logits[:, 0:NT - 1, :]))
    own(dve.tensor_copy(gate[0:TR, 0, NT - 1, :], logits[0:TR, NT - 1, :]))
    own(dve.tensor_reduce(small[:, 0, :], G, AX.X, ALU.max))
    own(dve.tensor_tensor(prob_, G, small[:, 0, :].unsqueeze(2).to_broadcast(wide), ALU.subtract))
    dve.nop().then_inc(exped[0], 1)
    for i in range(top):
        if i:
            own(dve.scalar_tensor_tensor(out=G, in0=masks[i - 1], scalar=-HUGE, in1=G, op0=ALU.mult, op1=ALU.add))
            own(dve.tensor_reduce(small[:, 0, :], G, AX.X, ALU.max))
        own(dve.tensor_tensor(work, G, small[:, 0, :].unsqueeze(2).to_broadcast(wide), ALU.is_equal))
        own(dve.tensor_tensor(work, work, index_weight, ALU.mult))
        own(dve.tensor_reduce(small[:, 1, :], work, AX.X, ALU.max))
        own(dve.tensor_tensor(masks[i], work, small[:, 1, :].unsqueeze(2).to_broadcast(wide), ALU.is_equal))
    dve.wait_ge(exped[1], 1)
    own(dve.tensor_reduce(small[:, 2, :], prob_, AX.X, ALU.add))
    own(dve.reciprocal(small[:, 3, :], small[:, 2, :]))
    own(dve.tensor_tensor(prob_, prob_, small[:, 3, :].unsqueeze(2).to_broadcast(wide), ALU.mult))
    return prob_, masks


def moe0(nc, ident, ones, xnT, xrow, gateT, wi, wo, out):
    HC = I0 // P
    W4 = 4 * CAP
    NS = 4
    with ExitStack() as ctx:
        sp = Space(nc, ctx, "m0")
        gw = sp.sb("gw", [P, DC, E0])
        before = sp.sb("before", [P, P])
        slot_no = sp.sb("slot_no", [P, CAP])
        index_weight = sp.sb("index_weight", [P, NT, E0])
        gate = sp.sb("gate", [P, 4, NT, E0])
        small = sp.sb("small", [P, 6, NT])
        slot_is = sp.sb("slot_is", [P, NT, CAP])
        disp = sp.sb("disp", [P, NT, E0, CAP])
        dispT = sp.sb("dispT", [CAP, E0, T])
        xd = sp.sb("xd", [P, DC, E0, CAP])
        wi_t = sp.sb("wi", [P, NS, DC, I0])
        wo_t = sp.sb("wo", [P, NS, HC, D])
        hid = sp.sb("hid", [P, 2, HC, CAP])
        eo = sp.sb("eo", [CAP, E0, D])
        ans = sp.sb("ans", [P, NT, D])
        psum = sp.ps("banks", [P, 8, BANK])
        bank = [psum[:, i, :] for i in range(8)]
        names = ("set_up", "loaded", "logits_ready", "to_exp", "exp_done", "own", "masked", "ranked", "spread",
                 "xd_ready", "xd_evac", "dt_ready", "dt_evac", "h_ready", "gelu_done", "e_ready", "e_evac",
                 "ans_ready", "ans_evac", "stored", "pool_own")
        (set_up, loaded, logits_ready, to_exp, exp_done, own_, masked, ranked, spread, xd_ready, xd_evac,
         dt_ready, dt_evac, h_ready, gelu_done, e_ready, e_evac, ans_ready, ans_evac, stored,
         pool_own) = (sp.sem(n) for n in names)
        w_in = [sp.sem(f"w_in{j}") for j in range(NS)]
        block = ctx.enter_context(nc.Block())
        logits = bank[0][:, 0:NT * E0].rearrange("p (n e) -> p n e", n=NT)
        ranks = bank[1][:, 0:NT * E0].rearrange("p (n e) -> p n e", n=NT)

        @block.gpsimd
        def _(pool):
            pool.memset(before[:, :], 1.0).then_inc(pool_own, 1)
            pool.iota(slot_no[:, :], [[1, CAP]], 0, 0, allow_small_or_imprecise_dtypes=True).then_inc(set_up, 1)
            pool.iota(index_weight[:, :, :], [[0, NT], [-1, E0]], E0, 0,
                      allow_small_or_imprecise_dtypes=True).then_inc(set_up, 1)
            pool.memset(gate[:, 0], 0.0).then_inc(set_up, 1)
            pool.wait_ge(pool_own, 1)
            pool.affine_select(out=before[:, :], in_=before[:, :], compare_op=ALU.is_gt, fill=0.0, base=0,
                               pattern=[[1, P]], channel_multiplier=-1).then_inc(set_up, 1)

        @block.sync
        def _(sync):
            sync.dma_start(gw[:, :, :], gateT.rearrange("(c p) e -> p c e", p=P)).then_inc(loaded, 16)
            with sync.Fori(0, E0 // NS) as i:
                for j in range(NS):
                    sync.wait_ge(e_ready, NS * i + j + 1)
                    sync.dma_start(wi_t[:, j, :, :],
                                   wi[NS * i + j].rearrange("(c p) n -> p c n", p=P)).then_inc(w_in[j], 16)
                    sync.dma_start(wo_t[:, j, :, :],
                                   wo[NS * i + j].rearrange("(c p) n -> p c n", p=P)).then_inc(w_in[j], 16)
            full, rest = token_tiles(out)
            sync.wait_ge(ans_evac, NT)
            sync.dma_start(full, ans[:, 0:NT - 1, :]).then_inc(stored, 16)
            sync.dma_start(rest, ans[0:TR, NT - 1, :]).then_inc(stored, 16)
            sync.wait_ge(stored, 32)

        @block.vector
        def _(dve):
            own = Chain(dve, own_)
            dve.wait_ge(set_up, 4)
            prob_, masks = route(sp, own, logits_ready, (to_exp, exp_done), logits, gate, small, 1, E0,
                                 index_weight[:, :, :])
            mask = masks[0]
            dve.nop().then_inc(masked, 1)
            own(dve.tensor_tensor(prob_, prob_, mask, ALU.mult))
            own(dve.tensor_reduce(small[:, 4, :], prob_, AX.X, ALU.add))
            dve.wait_ge(ranked, 1)
            work = gate[:, 1]
            kept = gate[:, 0]
            own(dve.tensor_copy(work, ranks))
            own(dve.scalar_tensor_tensor(out=kept, in0=work, scalar=float(CAP), in1=mask, op0=ALU.is_lt,
                                         op1=ALU.mult))
            own(dve.tensor_tensor(work, work, kept, ALU.mult))
            own(dve.tensor_reduce(small[:, 5, :], work, AX.X, ALU.add))
            own(dve.tensor_tensor(slot_is[:, :, :], slot_no[:, :].unsqueeze(1).to_broadcast([P, NT, CAP]),
                                  small[:, 5, :].unsqueeze(2).to_broadcast([P, NT, CAP]), ALU.is_equal))
            for n in range(NT):
                dve.tensor_tensor(disp[:, n, :, :], slot_is[:, n, :].unsqueeze(1).to_broadcast([P, E0, CAP]),
                                  kept[:, n, :].unsqueeze(2).to_broadcast([P, E0, CAP]),
                                  ALU.mult).then_inc(spread, 1)
            for j in range(4):
                k, half = j // 2, j % 2
                dve.wait_ge(xd_ready, j + 1)
                dve.tensor_copy(xd[:, k, 4 * half:4 * half + 4, :].rearrange("p e c -> p (e c)"),
                                bank[2 + j][:, 0:W4]).then_inc(xd_evac, 1)
            for e in range(E0):
                for half in range(2):
                    w = min(4, NT - 4 * half)
                    cols = min(w * P, T - 4 * P * half)
                    dve.wait_ge(dt_ready, 2 * e + half + 1)
                    dve.tensor_copy(dispT[:, e, 4 * P * half:4 * P * half + cols],
                                    bank[6 + half][0:CAP, 0:cols]).then_inc(dt_evac, 1)
            with dve.Fori(0, E0 // 2) as i:
                for j in range(2):
                    dve.wait_ge(e_ready, NS + 2 * i + j + 1)
                    dve.tensor_copy(eo[:, bass.ds(2 * i + j, 1), :].rearrange("p a d -> p (a d)"),
                                    bank[4 + j][0:CAP, 0:D]).then_inc(e_evac, 1)
            for n in range(NT):
                dve.wait_ge(ans_ready, n + 1)
                dve.tensor_scalar(ans[:, n, :], bank[n % 2][:, 0:D], small[:, 4, n:n + 1], None,
                                  ALU.mult).then_inc(ans_evac, 1)

        @block.scalar
        def _(act):
            act.wait_ge(to_exp, 1)
            act.activation(gate[:, 2], gate[:, 2], ACT.Exp).then_inc(exp_done, 1)
            with act.Fori(0, E0 // 2) as i:
                for j in range(2):
                    if j == 0:
                        act.wait_ge(e_ready, NS + 2 * i)
                    for half in range(2):
                        act.wait_ge(h_ready, 4 * i + 2 * j + half + 1)
                        act.activation(hid[:, j, 4 * half:4 * half + 4, :].rearrange("p c s -> p (c s)"),
                                       bank[half + 2 * j][:, 0:W4], ACT.Gelu).then_inc(gelu_done, 1)

        @block.tensor
        def _(pe):
            pe.nop().then_inc(e_ready, NS)
            pe.wait_ge(loaded, 16)
            for n in range(NT):
                rows = P if n < NT - 1 else TR
                for k in range(DC):
                    mm = pe.matmul(logits[0:rows, n, :], xnT[:, k, n * P:n * P + rows], gw[:, k, :],
                                   start=(k == 0), stop=(k == DC - 1))
            mm.then_inc(logits_ready, 1)
            pe.wait_ge(masked, 1)
            pe.wait_ge(set_up, 4)
            for n in range(NT):
                for m in range(n + 1):
                    mm = pe.matmul(ranks[:, n, :], before[:, :] if m == n else ones[:, :], gate[:, 3, m, :],
                                   start=(m == 0), stop=(m == n))
            mm.then_inc(ranked, 1)
            pe.wait_ge(spread, NT)
            for j in range(4):
                k, half = j // 2, j % 2
                for n in range(NT):
                    rows = P if n < NT - 1 else TR
                    mm = pe.matmul(bank[2 + j][:, 0:W4], xrow[0:rows, n, k * P:(k + 1) * P],
                                   disp[0:rows, n, 4 * half:4 * half + 4, :].rearrange("p e c -> p (e c)"),
                                   start=(n == 0), stop=(n == NT - 1))
                mm.then_inc(xd_ready, 1)
            for e in range(E0):
                for half in range(2):
                    if e:
                        pe.wait_ge(dt_evac, 2 * (e - 1) + half + 1)
                    for m in range(min(4, NT - 4 * half)):
                        n = 4 * half + m
                        rows = P if n < NT - 1 else TR
                        mm = pe.transpose(bank[6 + half][0:CAP, m * P:m * P + rows], disp[0:rows, n, e, :],
                                          ident[0:rows, 0:rows])
                    mm.then_inc(dt_ready, 1)
            pe.wait_ge(xd_evac, 4)
            def pair(ii, i, p):
                for j in range(2):
                    pe.wait_ge(w_in[2 * p + j], 32 * (ii + 1))
                    for half in range(2):
                        pe.wait_ge(gelu_done, 4 * i)
                        for c in range(4):
                            for k in range(DC):
                                mm = pe.matmul(bank[half + 2 * j][:, c * CAP:(c + 1) * CAP],
                                               wi_t[:, 2 * p + j, k, (4 * half + c) * P:(4 * half + c + 1) * P],
                                               xd[:, k, bass.ds(2 * i + j, 1), :].rearrange("p a c -> p (a c)"),
                                               start=(k == 0), stop=(k == DC - 1))
                        mm.then_inc(h_ready, 1)
                for j in range(2):
                    pe.wait_ge(gelu_done, 4 * i + 2 * j + 2)
                    pe.wait_ge(e_evac, 2 * i)
                    for c in range(HC):
                        mm = pe.matmul(bank[4 + j][0:CAP, 0:D], hid[:, j, c, :], wo_t[:, 2 * p + j, c, :],
                                       start=(c == 0), stop=(c == HC - 1))
                    mm.then_inc(e_ready, 1)

            with pe.Fori(0, E0 // NS) as ii:
                for p in range(NS // 2):
                    pair(ii, NS // 2 * ii + p, p)
            pe.wait_ge(e_evac, E0)
            for n in range(NT):
                rows = P if n < NT - 1 else TR
                if n >= 2:
                    pe.wait_ge(ans_evac, n - 1)
                for e in range(E0):
                    mm = pe.matmul(bank[n % 2][0:rows, 0:D], dispT[:, e, n * P:n * P + rows], eo[:, e, :],
                                   start=(e == 0), stop=(e == E0 - 1))
                mm.then_inc(ans_ready, 1)


E1, F1, FC1 = 8, 176, 88
NX1 = E1 + 2
TH = T // 2


def moe1(nc, ident, xnT, WrT, Wgu, Wd, out):
    FN = F1 // FC1
    with ExitStack() as ctx:
        sp = Space(nc, ctx, "m1")
        gw = sp.sb("gw", [P, DC, E1])
        index_weight = sp.sb("index_weight", [P, NT, E1])
        gate = sp.sb("gate", [P, 5, NT, E1])
        weight = sp.sb("weight", [P, NT, NX1])
        wcol = sp.sb("wcol", [P, 2, NT])
        small = sp.sb("small", [P, 6, NT])
        wgu = sp.sb("wgu", [P, 2, DC, 2, F1])
        wd = sp.sb("wd", [FC1, 2, FN, D])
        silu = sp.sb("silu", [FC1, 2, TH])
        gu = sp.sb("gu", [FC1, FN, T])
        acc = sp.sb("acc", [P, NT, D])
        psum = sp.ps("banks", [P, 8, BANK])
        bank = [psum[:, i, :] for i in range(8)]
        names = ("set_up", "loaded", "logits_ready", "to_exp", "exp_done", "own", "w_in0", "w_in1", "g_ready", "u_ready",
                 "silu_done", "gu_done", "o_ready", "o_done", "wcol_in", "stored", "weighted")
        (set_up, loaded, logits_ready, to_exp, exp_done, own_, w_in0, w_in1, g_ready, u_ready, silu_done, gu_done,
         o_ready, o_done, wcol_in, stored, weighted) = (sp.sem(n) for n in names)
        w_in = (w_in0, w_in1)
        logits = bank[0][:, 0:NT * E1].rearrange("p (n e) -> p n e", n=NT)
        NQ = FN * 2
        block = ctx.enter_context(nc.Block())

        @block.gpsimd
        def _(pool):
            pool.iota(index_weight[:, :, :], [[0, NT], [-1, E1]], E1, 0,
                      allow_small_or_imprecise_dtypes=True).then_inc(set_up, 1)
            pool.memset(gate[:, 0], 0.0).then_inc(set_up, 1)
            pool.memset(weight[:, :, E1:NX1], 1.0).then_inc(set_up, 1)
            pool.memset(acc[:, :, :], 0.0).then_inc(set_up, 1)

        @block.sync
        def _(sync):
            sync.dma_start(gw[:, :, :], WrT.rearrange("(c p) e -> p c e", p=P)).then_inc(loaded, 16)
            with sync.Fori(0, NX1 // 2) as i:
                for j in range(2):
                    sync.wait_ge(o_ready, 2 * NT * i + NT * j)
                    sync.dma_start(wgu[:, j], Wgu[2 * i + j]).then_inc(w_in[j], 16)
                    sync.dma_start(wd[:, j], Wd[2 * i + j]).then_inc(w_in[j], 16)
            full, rest = token_tiles(out)
            sync.wait_ge(o_done, NT * NX1)
            sync.dma_start(full, acc[:, 0:NT - 1, :]).then_inc(stored, 16)
            sync.dma_start(rest, acc[0:TR, NT - 1, :]).then_inc(stored, 16)
            sync.wait_ge(stored, 32)

        @block.scalar
        def _(act):
            act.wait_ge(to_exp, 1)
            act.activation(gate[:, 2], gate[:, 2], ACT.Exp).then_inc(exp_done, 1)
            with act.Fori(0, NX1 // 2) as i:
                for j in range(2):
                    for q in range(NQ):
                        m = NQ * j + q
                        act.wait_ge(g_ready, 2 * NQ * i + m + 1)
                        if m >= 2:
                            act.wait_ge(gu_done, 2 * NQ * i + m - 1)
                        else:
                            act.wait_ge(gu_done, 2 * NQ * i)
                        act.activation(silu[:, q % 2, :], bank[q % 2][0:FC1, 0:TH], ACT.Silu).then_inc(silu_done, 1)

        @block.vector
        def _(dve):
            own = Chain(dve, own_)
            dve.wait_ge(set_up, 4)
            prob_, masks = route(sp, own, logits_ready, (to_exp, exp_done), logits, gate, small, 2, E1,
                                 index_weight[:, :, :])
            own(dve.tensor_tensor(masks[0], masks[0], masks[1], ALU.add))
            dve.tensor_tensor(weight[:, :, 0:E1], prob_, masks[0], ALU.mult).then_inc(weighted, 1)
            dve.wait_ge(weighted, 1)
            with dve.Fori(0, NX1 // 2) as i:
                dve.wait_ge(o_done, 2 * NT * i)
                dve.tensor_copy(wcol[:, :, :], weight[:, :, bass.ds(2 * i, 2)].rearrange("p n e -> p e n")
                                ).then_inc(wcol_in, 1)
                for j in range(2):
                    for q in range(NQ):
                        c, half = q // 2, q % 2
                        m = NQ * j + q
                        dve.wait_ge(silu_done, 2 * NQ * i + m + 1)
                        dve.wait_ge(u_ready, 2 * NQ * i + m + 1)
                        if q == 0:
                            dve.wait_ge(o_ready, 2 * NT * i + NT * (j + 1))
                        dve.tensor_tensor(gu[:, c, half * TH:(half + 1) * TH], silu[:, q % 2, :],
                                          bank[2 + q % 2][0:FC1, 0:TH], ALU.mult).then_inc(gu_done, 1)
                    if j == 0:
                        dve.wait_ge(wcol_in, i + 1)
                    for n in range(NT):
                        rows = P if n < NT - 1 else TR
                        dve.wait_ge(o_ready, 2 * NT * i + NT * (j + 1) + n + 1)
                        if j:
                            dve.wait_ge(o_done, 2 * NT * i + n + 1)
                        dve.scalar_tensor_tensor(out=acc[0:rows, n, :], in0=bank[4 + n % 4][0:rows, 0:D],
                                                 scalar=wcol[0:rows, j, n:n + 1], in1=acc[0:rows, n, :],
                                                 op0=ALU.mult, op1=ALU.add).then_inc(o_done, 1)

        @block.tensor
        def _(pe):
            pe.nop().then_inc(o_ready, NT)
            pe.wait_ge(loaded, 16)
            for n in range(NT):
                rows = P if n < NT - 1 else TR
                for k in range(DC):
                    mm = pe.matmul(logits[0:rows, n, :], xnT[:, k, n * P:n * P + rows], gw[:, k, :],
                                   start=(k == 0), stop=(k == DC - 1))
            mm.then_inc(logits_ready, 1)
            pe.wait_ge(to_exp, 1)
            with pe.Fori(0, NX1 // 2) as i:
                for j in range(2):
                    pe.wait_ge(w_in[j], 32 * (i + 1))
                    for q in range(NQ):
                        c, half = q // 2, q % 2
                        m = NQ * j + q
                        for which, ready in ((0, g_ready), (1, u_ready)):
                            pe.wait_ge(gu_done, 2 * NQ * i + max(m - 1, 0))
                            for k in range(DC):
                                mm = pe.matmul(bank[2 * which + q % 2][0:FC1, 0:TH],
                                               wgu[:, j, k, which, c * FC1:(c + 1) * FC1],
                                               xnT[:, k, half * TH:(half + 1) * TH],
                                               start=(k == 0), stop=(k == DC - 1))
                            mm.then_inc(ready, 1)
                    pe.wait_ge(gu_done, 2 * NQ * i + NQ * (j + 1))
                    for n in range(NT):
                        rows = P if n < NT - 1 else TR
                        pe.wait_ge(o_done, 2 * NT * i + max(NT * j + n - 3, 0))
                        for c in range(FN):
                            mm = pe.matmul(bank[4 + n % 4][0:rows, 0:D], gu[:, c, n * P:n * P + rows],
                                           wd[:, j, c, :], start=(c == 0), stop=(c == FN - 1))
                        mm.then_inc(o_ready, 1)


H1, HD1 = 16, 16
F16 = mybir.dt.float16
NR = 4
RK = B * SE // NR
CH = -(-RK // P)
CR = RK - (CH - 1) * P
NM = -(-RK // BANK)
LW = RK - (NM - 1) * BANK
LCH = -(-LW // P)
LN255 = float(np.log(255.0))
QT1 = T // P
NMAIN = H1 * QT1
NLEFT = H1 // 4
NTILE = NMAIN + NLEFT


def kv1(nc, ident, identb, ones, ctxT, Wkv, bkv, k_dram, v_dram, sv_dram):
    NPAIR = (CH + 1) // 2
    assert CH % 2 == 1 and NPAIR == 2 * NM
    shape_of = lambda u: (P, 2) if u < NPAIR - 1 else (CR, 1)
    C = H1 * HD1
    with ExitStack() as ctx:
        sp = Space(nc, ctx, "kv")
        w = sp.sb("w", [P, DC, 2 * C])
        bias = sp.sb("bias", [P, 2 * C])
        cx = sp.sb("ctx", [P, DC, RK])
        vrow = sp.sb("vrow", [P, NR * CH, C])
        vraw = sp.sb("vraw", [P, 2, 2, C])
        vint = sp.sb("vint", [P, H1, NR * CH, HD1], BF16)
        kb = sp.sb("kb", [P, 2, 2 * C])
        kst = sp.sb("kst", [P, 2, 3, 2 * H1])
        khat = sp.sb("khat", [P, 2, 2 * C])
        ksplit = sp.sb("ksplit", [P, 2, 2, H1, 2, HD1], F16)
        kT = sp.sb("kT", [P, 2, 4, BANK], F16)
        vmax = sp.sb("vmax", [P, C])
        vcol = sp.sb("vcol", [P, DC, 3])
        vdiag = sp.sb("vdiag", [P, DC, P])
        vsc = sp.sb("vsc", [P, C])
        id16 = sp.sb("id16", [P, P], F16)
        kps = sp.ps("kp", [P, 2, 2, C])
        vps = sp.ps("vp", [P, 2, 2, C])
        tps = sp.ps("tp", [P, 2, 2, 4, P], F16)
        xps = sp.ps("xp", [P, 2, BANK])
        names = ("w_in", "cx_used", "kv_ready", "k_evac", "v_evac", "v_added", "own", "khat_done", "hi_done", "split",
                 "turned", "t_evac", "vm_ready", "vt_ready", "vd_done", "vs_ready", "stored", "id_done", "v_done", "sv_done")
        (w_in, cx_used, kv_ready, k_evac, v_evac, v_added, own_, khat_done, hi_done, split, turned, t_evac, vm_ready, vt_ready,
         vd_done, vs_ready, stored, id_done, v_done, sv_done) = (sp.sem(n) for n in names)
        passed = sp.sem("passed")
        cx_in = [sp.sem(f"cx_in{m}") for m in range(NM)]
        stored_k = [sp.sem(f"stored_k{i}") for i in range(2)]
        block = ctx.enter_context(nc.Block())
        width = [BANK] * (NM - 1) + [LW]

        @block.sync
        def _(sync):
            sync.dma_start(w[:, :, :], Wkv.rearrange("(c p) n -> p c n", p=P)).then_inc(w_in, 16)
            sync.dma_start(bias[:, :], bkv.to_broadcast([P, 2 * C])).then_inc(w_in, 16)
            with sync.Fori(0, NR) as r:
                for m in range(NM):
                    sync.wait_ge(cx_used, NM * r + m + 1)
                    at = m * BANK
                    sync.dma_start(cx[:, :, at:at + width[m]],
                                   ctxT[:, :, bass.ds(r * RK + at, width[m])].rearrange("c p n -> p c n")
                                   ).then_inc(cx_in[m], 16)
                for m in range(NM):
                    sync.wait_ge(t_evac, NPAIR * r + 2 * (m + 1))
                    for i in range(4):
                        dst = k_dram.rearrange("(q i) (g r) n -> i g r q n", i=4, g=NR)
                        dst = dst[i, bass.ds(r, 1), :, :, m * BANK:m * BANK + width[m]].rearrange(
                            "a r q n -> (a r) q n")
                        sync.dma_start(dst, kT[32 * i:32 * i + 32, m % 2, :, 0:width[m]]).then_inc(stored_k[m % 2], 16)
            sync.wait_ge(sv_done, 1)
            sync.dma_start(sv_dram.rearrange("(c p) a -> p c a", p=P), vcol[:, :, 1:2],
                           allow_slow_non_contiguous=True).then_inc(stored, 16)
            for j in range(NR):
                sync.wait_ge(v_done, j + 1)
                at = slice(j * CH, (j + 1) * CH)
                sync.dma_start(v_dram[:, :, at, :].rearrange("h p c d -> p h (c d)"),
                               vint[:, :, at, :].rearrange("p h c d -> p h (c d)")).then_inc(stored, 16)
            sync.wait_ge(stored, 16 * (NR + 1))
            for i in range(2):
                sync.wait_ge(stored_k[i], 16 * 4 * NR * NM // 2)

        @block.gpsimd
        def _(pool):
            pool.tensor_copy(id16[:, :], ident[:, :]).then_inc(id_done, 1)
            for r in range(NR):
                i = pool.memset(vrow[:, (r + 1) * CH - 1, :], 0.0)
            i.then_inc(id_done, 1)
            pool.wait_ge(w_in, 32)
            pool.wait_ge(id_done, 2)

            def lower(r, u):
                n, count = shape_of(u)
                kh = khat[0:n, u % 2, 0:count * C].rearrange("p (c h d) -> p c h d", c=count, h=H1)
                pool.wait_ge(hi_done, NPAIR * r + u + 1)
                for c in range(count):
                    i = pool.tensor_tensor(ksplit[0:n, u % 2, c, :, 1, :], kh[:, c], ksplit[0:n, u % 2, c, :, 0, :],
                                           ALU.subtract)
                i.then_inc(split, 1)

            with pool.Fori(0, NR) as r:
                for u in range(NPAIR):
                    n, count = shape_of(u)
                    v = vrow[0:n, bass.ds(r * CH + 2 * u, count), :]
                    wait_apart(pool, v_evac, NPAIR * r + u + 1, passed)
                    pool.tensor_tensor(v, vraw[0:n, u % 2, 0:count, :],
                                       bias[0:n, C:2 * C].unsqueeze(1).to_broadcast([n, count, C]),
                                       ALU.add).then_inc(v_added, 1)
                    if u:
                        lower(r, u - 1)
                lower(r, NPAIR - 1)

        @block.tensor
        def _(pe):
            pe.nop().then_inc(cx_used, NM)
            pe.wait_ge(w_in, 32)
            pe.wait_ge(id_done, 2)
            with pe.Fori(0, NR) as r:
                def turn(u):
                    n, count = shape_of(u)
                    wait_apart(pe, split, NPAIR * r + u + 1, passed)
                    wait_apart(pe, t_evac, NPAIR * r + max(u - 1, 0), passed)
                    for c in range(count):
                        for q in range(4):
                            mm = pe.transpose(tps[:, u % 2, c, q, 0:n],
                                              ksplit[0:n, u % 2, c, 4 * q:4 * q + 4].rearrange("p h s d -> p (h s d)"),
                                              id16[0:n, 0:n])
                    mm.then_inc(turned, 1)

                for u in range(NPAIR):
                    n, count = shape_of(u)
                    if u % 2 == 0:
                        pe.wait_ge(cx_in[u // 2], 16 * (r + 1))
                    pe.wait_ge(k_evac, NPAIR * r + max(u - 1, 0))
                    pe.wait_ge(v_evac, NPAIR * r + max(u - 1, 0))
                    for c in range(count):
                        at = (2 * u + c) * P
                        for bank, cols in ((kps, slice(0, C)), (vps, slice(C, 2 * C))):
                            for k in range(DC):
                                mm = pe.matmul(bank[0:n, u % 2, c, :], cx[:, k, at:at + n], w[:, k, cols],
                                               start=(k == 0), stop=(k == DC - 1))
                    mm.then_inc(kv_ready, 1)
                    if u % 2 == 1:
                        pe.nop().then_inc(cx_used, 1)
                    if u >= 2:
                        turn(u - 2)
                turn(NPAIR - 2)
                turn(NPAIR - 1)
            pe.wait_ge(vm_ready, 1)
            for k in range(DC):
                mm = pe.transpose(xps[:, 0, k * P:(k + 1) * P], vmax[:, k * P:(k + 1) * P], ident[:, :])
            mm.then_inc(vt_ready, 1)
            pe.wait_ge(vd_done, 1)
            for k in range(DC):
                mm = pe.matmul(xps[:, 1, k * P:(k + 1) * P], ones[:, :], vdiag[:, k, :], start=True, stop=True)
            mm.then_inc(vs_ready, 1)

        @block.scalar
        def _(act):
            def out_of_psum(r, u):
                n, count = shape_of(u)
                m = u // 2
                if u % 2 == 0:
                    act.wait_ge(stored_k[m % 2], 16 * 4 * (NM // 2 * r + m // 2))
                act.wait_ge(turned, NPAIR * r + u + 1)
                at = (u % 2) * 2 * P
                act.copy(kT[:, m % 2, :, at:at + count * n].rearrange("p q (c n) -> p c q n", c=count),
                         tps[:, u % 2, 0:count, :, 0:n]).then_inc(t_evac, 1)

            with act.Fori(0, NR) as r:
                for u in range(NPAIR):
                    n, count = shape_of(u)
                    act.wait_ge(kv_ready, NPAIR * r + u + 1)
                    act.wait_ge(v_added, NPAIR * r + max(u - 1, 0))
                    act.copy(vraw[0:n, u % 2, 0:count, :], vps[0:n, u % 2, 0:count, :]).then_inc(v_evac, 1)
                    act.wait_ge(khat_done, NPAIR * r + u + 1)
                    act.wait_ge(turned, NPAIR * r + max(u - 1, 0))
                    act.copy(ksplit[0:n, u % 2, 0:count, :, 0, :].rearrange("p c h d -> p (c h) d"),
                             khat[0:n, u % 2, 0:count * C].rearrange("p (g d) -> p g d", d=HD1)).then_inc(hi_done, 1)
                    if u >= 2:
                        out_of_psum(r, u - 2)
                out_of_psum(r, NPAIR - 2)
                out_of_psum(r, NPAIR - 1)

        @block.vector
        def _(dve):
            dve.wait_ge(w_in, 32)
            OWN = 5
            with dve.Fori(0, NR) as r:
                own = Chain(dve, own_, (OWN * NPAIR) * r)
                for u in range(NPAIR):
                    n, count = shape_of(u)
                    b, H = u % 2, count * H1
                    k_, st, kh = kb[0:n, b, 0:count * C], kst[0:n, b], khat[0:n, b, 0:count * C]
                    by_head = lambda ap: ap.rearrange("p (h d) -> p h d", d=HD1)
                    dve.wait_ge(kv_ready, NPAIR * r + u + 1)
                    i = dve.tensor_tensor(k_.rearrange("p (c n) -> p c n", c=count), kps[0:n, b, 0:count, :],
                                          bias[0:n, 0:C].unsqueeze(1).to_broadcast([n, count, C]), ALU.add)
                    i.then_inc(k_evac, 1)
                    dve.wait_ge(k_evac, NPAIR * r + u + 1)
                    own(dve.tensor_reduce(st[:, 0, 0:H], by_head(k_), AX.X, ALU.max, apply_absolute_value=True))
                    own(dve.tensor_scalar(st[:, 1, 0:H], st[:, 0, 0:H], 1.0 / 127.0, 1e-8, ALU.mult, ALU.max))
                    own(dve.reciprocal(st[:, 2, 0:H], st[:, 1, 0:H]))
                    own(dve.tensor_tensor(by_head(k_), by_head(k_),
                                          st[:, 2, 0:H].unsqueeze(2).to_broadcast([n, H, HD1]), ALU.mult))
                    own(dve.tensor_scalar(k_, k_, ROUND, ROUND, ALU.add, ALU.subtract))
                    dve.wait_ge(split, NPAIR * r + max(u - 1, 0))
                    dve.tensor_tensor(by_head(kh), by_head(k_),
                                      st[:, 1, 0:H].unsqueeze(2).to_broadcast([n, H, HD1]),
                                      ALU.mult).then_inc(khat_done, 1)
            own = Chain(dve, own_, OWN * NPAIR * NR)
            dve.wait_ge(v_added, NR * NPAIR)
            dve.wait_ge(id_done, 2)
            dve.tensor_reduce(vmax[:, :], vrow[:, :, :].rearrange("p c d -> p d c"), AX.X, ALU.max,
                              apply_absolute_value=True).then_inc(vm_ready, 1)
            dve.wait_ge(vt_ready, 1)
            own(dve.tensor_reduce(vcol[:, :, 0], xps[:, 0, 0:C].rearrange("p (k n) -> p k n", k=DC), AX.X, ALU.max))
            own(dve.tensor_scalar(vcol[:, :, 1], vcol[:, :, 0], 1.0 / 127.0, 1e-8, ALU.mult, ALU.max))
            dve.nop().then_inc(sv_done, 1)
            own(dve.reciprocal(vcol[:, :, 2], vcol[:, :, 1]))
            for k in range(DC):
                i = dve.tensor_scalar(vdiag[:, k, :], ident[:, :], vcol[:, k, 2:3], None, ALU.mult)
                own(i)
            dve.nop().then_inc(vd_done, 1)
            dve.wait_ge(vs_ready, 1)
            own(dve.tensor_copy(vsc[:, :], xps[:, 1, 0:C]))
            for j in range(NR):
                v = vrow[:, j * CH:(j + 1) * CH, :]
                own(dve.tensor_tensor(v, v, vsc[:, :].unsqueeze(1).to_broadcast([P, CH, C]), ALU.mult))
                dve.tensor_scalar(vint[:, :, j * CH:(j + 1) * CH, :].rearrange("p h c d -> p c h d"),
                                  v.rearrange("p c (h d) -> p c h d", h=H1), ROUND, ROUND, ALU.add,
                                  ALU.subtract).then_inc(v_done, 1)


def q1(nc, ident, xnT, Wq, bq, q_dram, nsq_dram, nsql_dram):
    C = H1 * HD1
    scale = float(HD1) ** -0.5
    with ExitStack() as ctx:
        sp = Space(nc, ctx, "q1")
        w = sp.sb("w", [P, DC, C])
        bias = sp.sb("bias", [P, C])
        q = sp.sb("q", [P, NT, C])
        st = sp.sb("st", [P, 4, NT, H1])
        nsq_t = sp.sb("nsq_t", [P, H1, QT1])
        qrep = sp.sb("qrep", [P, NT, H1, 2, HD1], F16)
        qT = sp.sb("qT", [P, 2, T], F16)
        id16 = sp.sb("id16", [P, P], F16)
        psum = sp.ps("qp", [P, 4, BANK])
        tps = [sp.ps(f"tp{i}", [P, T], F16) for i in range(2)]
        names = ("w_in", "q_ready", "q_evac", "own", "rep", "turned", "t_evac", "stored", "id_done", "nsq")
        (w_in, q_ready, q_evac, own_, rep, turned, t_evac, stored, id_done, nsq) = (
            sp.sem(n) for n in names)
        stored_q = [sp.sem(f"stored_q{i}") for i in range(2)]
        block = ctx.enter_context(nc.Block())
        rows_of = lambda n: P if n < NT - 1 else TR

        @block.sync
        def _(sync):
            sync.dma_start(w[:, :, :], Wq.rearrange("(c p) n -> p c n", p=P)).then_inc(w_in, 16)
            sync.dma_start(bias[:, :], bq.to_broadcast([P, C])).then_inc(w_in, 16)
            sync.wait_ge(nsq, 1)
            sync.dma_start(nsq_dram, nsq_t[:, :, :].rearrange("p h n -> p (h n)")).then_inc(stored, 16)
            sync.dma_start(nsql_dram, st[0:TR, 3, NT - 1, :]).then_inc(stored, 16)
            for q4 in range(H1 // 4):
                sync.wait_ge(t_evac, q4 + 1)
                sync.dma_start(q_dram[4 * q4:4 * q4 + 4].rearrange("h p t -> (h p) t"),
                               qT[:, q4 % 2, :]).then_inc(stored_q[q4 % 2], 16)
            sync.wait_ge(stored, 32)
            for i in range(2):
                sync.wait_ge(stored_q[i], 16 * H1 // 8)

        @block.gpsimd
        def _(pool):
            pool.tensor_copy(id16[:, :], ident[:, :]).then_inc(id_done, 1)
            pool.memset(q[:, NT - 1, :], 0.0).then_inc(id_done, 1)

        @block.tensor
        def _(pe):
            pe.wait_ge(w_in, 32)
            for n in range(NT):
                rows = rows_of(n)
                for k in range(DC):
                    mm = pe.matmul(psum[0:rows, n // 2, (n % 2) * C:(n % 2 + 1) * C], xnT[:, k, n * P:n * P + rows],
                                   w[:, k, :], start=(k == 0), stop=(k == DC - 1))
                mm.then_inc(q_ready, 1)
            pe.wait_ge(rep, 1)
            pe.wait_ge(id_done, 2)
            for q4 in range(H1 // 4):
                if q4 >= 2:
                    pe.wait_ge(t_evac, q4 - 1)
                for n in range(NT):
                    rows = rows_of(n)
                    mm = pe.transpose(tps[q4 % 2][:, n * P:n * P + rows],
                                      qrep[0:rows, n, 4 * q4:4 * q4 + 4].rearrange("p h s d -> p (h s d)"),
                                      id16[0:rows, 0:rows])
                mm.then_inc(turned, 1)

        @block.scalar
        def _(act):
            for q4 in range(H1 // 4):
                act.wait_ge(turned, q4 + 1)
                if q4 >= 2:
                    act.wait_ge(stored_q[q4 % 2], 16 * (q4 // 2))
                act.copy(qT[:, q4 % 2, :], tps[q4 % 2][:, :]).then_inc(t_evac, 1)

        @block.vector
        def _(dve):
            own = Chain(dve, own_)
            dve.wait_ge(w_in, 32)
            dve.wait_ge(id_done, 2)
            for n in range(NT):
                rows = rows_of(n)
                if n % 2 == 0:
                    dve.wait_ge(q_ready, min(n + 2, NT))
                own(dve.tensor_tensor(q[0:rows, n, :], psum[0:rows, n // 2, (n % 2) * C:(n % 2 + 1) * C],
                                      bias[0:rows, :], ALU.add))
            qh = q[:, :, :].rearrange("p n (h d) -> p n h d", h=H1)
            own(dve.tensor_scalar(q[:, :, :], q[:, :, :], scale, None, ALU.mult))
            own(dve.tensor_reduce(st[:, 0], qh, AX.X, ALU.max, apply_absolute_value=True))
            own(dve.tensor_scalar(st[:, 1], st[:, 0], 1.0 / 127.0, 1e-8, ALU.mult, ALU.max))
            own(dve.reciprocal(st[:, 2], st[:, 1]))
            own(dve.tensor_scalar(st[:, 3], st[:, 1], -1.0, None, ALU.mult))
            dve.tensor_copy(nsq_t[:, :, :].rearrange("p h n -> p n h"), st[:, 3, 0:QT1]).then_inc(nsq, 1)
            own(dve.tensor_tensor(qh, qh, st[:, 2].unsqueeze(3).to_broadcast([P, NT, H1, HD1]), ALU.mult))
            own(dve.tensor_scalar(q[:, :, :], q[:, :, :], ROUND, ROUND, ALU.add, ALU.subtract))
            for n in range(NT):
                i = dve.tensor_copy(qrep[:, n], qh[:, n].unsqueeze(2).to_broadcast([P, H1, 2, HD1]))
                own(i)
            dve.nop().then_inc(rep, 1)
            dve.nop().then_inc(own_, 1)


def attention1(nc, ident, q_dram, nsq_dram, nsql_dram, k_dram, v_dram, sv_dram, Wp, bp, out):
    C = H1 * HD1
    width = [BANK] * (NM - 1) + [LW]
    NPL = 3
    AHEAD = 6
    NU = 2 * NM
    NX = NM * NR
    blocks = [(m, g) for m in range(NM) for g in range(NR)]
    assert len(blocks) == 24 and NTILE % 20 == 0
    with ExitStack() as ctx:
        sp = Space(nc, ctx, "a1")
        kb = sp.sb("kb", [P, 2, RK], F16)
        vb = sp.sb("vb", [P, 2, NR * CH, HD1], BF16)
        qb = sp.sb("qb", [P, 2, NR, T], F16)
        kl = sp.sb("kl", [P, 2, 4, RK], F16)
        vl = sp.sb("vl", [P, 2, 4, NR * CH, HD1], BF16)
        ql = sp.sb("ql", [P, NR, H1, TR], F16)
        nsq = sp.sb("nsq", [P, NTILE])
        sq = sp.sb("sq", [P, NTILE])
        svb = sp.sb("svb", [P, C])
        pi = sp.sb("pi", [P, NPL, NR, BANK], I16)
        pb = sp.sb("pb", [P, NM // 2, 2, NR * BANK], BF16)
        pt = sp.sb("pt", [P, NM, NR * 4, P], BF16)
        mx = sp.sb("mx", [P, 2, NX])
        nb = sp.sb("nb", [P, 2, 2])
        sums = sp.sb("sums", [P, 4, NU])
        osc = sp.sb("osc", [P, 2, 2])
        ao = sp.sb("ao", [P, NT, C])
        aoT = sp.sb("aoT", [P, DC, T])
        wp = sp.sb("wp", [P, DC, D])
        bpb = sp.sb("bpb", [P, D])
        res = sp.sb("res", [P, NT, D])
        psum = sp.ps("banks", [P, 8, BANK])
        OB = 7
        names = ("w_in", "kv_in0", "kv_in1", "kl_in0", "kl_in1", "a_ready", "a_done", "max_found", "osc_done", "sq_done", "pool_own", "b_ready", "exp_done", "bias_done",
                 "conv_done", "pv_part", "o_evac", "own", "set_up", "aot_ready", "aot_evac",
                 "res_ready", "res_done", "stored")
        (w_in, kv_in0, kv_in1, kl_in0, kl_in1, a_ready, a_done, max_found, osc_done, sq_done, pool_own, b_ready, exp_done, bias_done, conv_done, pv_part,
         o_evac, own_, set_up, aot_ready, aot_evac, res_ready, res_done, stored) = (
             sp.sem(n) for n in names)
        passed, q_cleared = sp.sem("passed"), sp.sem("q_cleared")
        N_WEIGHTS, N_HEAD = 8 + NR, 16 * (2 + NR)
        kv_in, kl_in = (kv_in0, kv_in1), (kl_in0, kl_in1)
        pt_in = [sp.sem(f"pt_in{m}") for m in range(NM // 2)]
        block = ctx.enter_context(nc.Block())

        def main_tile(par, qt):
            def operands(m, g):
                return [(qb[:, par, g, qt * P:(qt + 1) * P], kb[:, par, m * BANK:m * BANK + width[m]], slice(0, P))]
            return operands, lambda c: vb[:, par, c, :]

        def left_tile(lt):
            def operands(m, g):
                return [(ql[:, g, 4 * lt + i, :], kl[:, lt % 2, i, m * BANK:m * BANK + width[m]],
                         slice(32 * i, 32 * i + 32)) for i in range(4)]
            return operands, lambda c: vl[:, lt % 2, :, c, :]

        @block.sync
        def _(sync):
            sync.dma_start(nsq[:, 0:NMAIN], nsq_dram).then_inc(w_in, 16)
            for i in range(4):
                sync.dma_start(nsq[32 * i:32 * i + 32, NMAIN:NTILE],
                               nsql_dram.rearrange("t (l i) -> i t l", i=4)[i],
                               allow_slow_non_contiguous=True).then_inc(w_in, 16)
            sync.dma_start(svb[:, :], sv_dram.rearrange("n a -> a n").to_broadcast([P, C])).then_inc(w_in, 16)
            sync.wait_ge(q_cleared, 2)
            for g in range(NR):
                r = slice(32 * g, 32 * g + 32)
                sync.dma_start(ql[r, g], q_dram[:, :, QT1 * P:T].rearrange("h p t -> p h t")).then_inc(w_in, 16)
            sync.dma_start(wp[:, :, :], Wp.rearrange("(c p) n -> p c n", p=P)).then_inc(w_in, 16)
            sync.dma_start(bpb[:, :], bp.to_broadcast([P, D])).then_inc(w_in, 16)

            def head(h, par):
                sync.dma_start(kb[:, par, :], k_dram[h]).then_inc(kv_in[par], 16)
                for g in range(NR):
                    r = slice(32 * g, 32 * g + 32)
                    sync.dma_start(qb[r, par, g, :], q_dram[h]).then_inc(kv_in[par], 16)
                sync.dma_start(vb[:, par].rearrange("p c d -> p (c d)"),
                               v_dram[h].rearrange("p c d -> p (c d)")).then_inc(kv_in[par], 16)

            def left_keys(lt):
                sync.dma_start(kl[:, lt % 2], k_dram[4 * lt:4 * lt + 4].rearrange("h p n -> p h n")
                               ).then_inc(kl_in[lt % 2], 16)

            def left_values(lt):
                sync.dma_start(vl[:, lt % 2].rearrange("p h c d -> p h (c d)"),
                               v_dram[4 * lt:4 * lt + 4].rearrange("h p c d -> p h (c d)")).then_inc(kl_in[lt % 2], 16)

            def turns(tile):
                for m in range(0, NM, 2):
                    wait_apart(sync, conv_done, NPL + NM * tile + m + 2, passed)
                    wait_apart(sync, pv_part, NU * tile + 2 * m + 4, passed)
                    chunks = 2 * NR * BANK // P if m < NM - 2 else NR * (BANK // P + LCH)
                    sync.dma_start_transpose(
                        pt[:, m:m + 2].rearrange("p m c q -> p (m c) q")[:, 0:chunks],
                        pb[:, m // 2].rearrange("p m n -> p (m n)")[:, 0:chunks * P]).then_inc(pt_in[m // 2], 16)

            def pair(hp, last):
                for par in range(2):
                    for qt in range(QT1):
                        turns(hp * (2 * QT1) + par * QT1 + qt)
                        if qt == 0 and par == 0:
                            head(hp * 2 + 1, 1)
                        if qt == 0 and par == 1 and not last:
                            head(hp * 2 + 2, 0)

            sync.wait_ge(set_up, 1)
            head(0, 0)
            for lt in range(2):
                left_keys(lt)
                left_values(lt)
            with sync.Fori(0, H1 // 2 - 1) as hp:
                pair(hp, False)
            pair(H1 // 2 - 1, True)
            for lt in range(NLEFT):
                turns(NMAIN + lt)
                if lt + 2 < NLEFT:
                    left_keys(lt + 2)
                if 1 <= lt < NLEFT - 1:
                    left_values(lt + 1)
            full, rest = token_tiles(out)
            sync.wait_ge(res_done, NT)
            sync.dma_start(full, res[:, 0:NT - 1, :]).then_inc(stored, 16)
            sync.dma_start(rest, res[0:TR, NT - 1, :]).then_inc(stored, 16)
            sync.wait_ge(stored, 32)

        @block.gpsimd
        def _(pool):
            pool.memset(qb[:, :, :, :], 0.0).then_inc(q_cleared, 1)
            pool.memset(ql[:, :, :, :], 0.0).then_inc(q_cleared, 1)
            pool.memset(vb[:, 1], 0.0).then_inc(set_up, 1)
            for m in range(0, NM, 2):
                pool.memset(pt[:, m:m + 2], 0.0).then_inc(pt_in[m // 2], 16)
            pool.memset(pb[:, NM // 2 - 1, 1, :], 0.0).then_inc(pool_own, 1)
            pool.wait_ge(pool_own, 1)
            pool.nop().then_inc(conv_done, NPL)
            with pool.Fori(0, NTILE // 2) as i:
                for j in range(2):
                    tile = 2 * i + j
                    for m in range(NM):
                        wait_apart(pool, exp_done, 2 + NU * tile + 2 * m + 2, passed)
                        if m % 2 == 0:
                            wait_apart(pool, pt_in[m // 2], 16 * (tile + 1), passed)
                        to = pb[:, m // 2, m % 2, :]
                        if m < NM - 1:
                            pool.tensor_scalar(to, pi[:, m % NPL].rearrange("p g n -> p (g n)"), 1.0, 0.0,
                                               ALU.mult, ALU.add).then_inc(conv_done, 1)
                        else:
                            to = to[:, 0:NR * LCH * P].rearrange("p (g n) -> p g n", g=NR)
                            pool.tensor_scalar(to[:, :, 0:LW], pi[:, m % NPL, :, 0:LW], 1.0, 0.0,
                                               ALU.mult, ALU.add).then_inc(conv_done, 1)

        @block.scalar
        def _(act):
            act.nop().then_inc(exp_done, 2)
            act.wait_ge(sq_done, 1)
            UNROLL = 20
            with act.Fori(0, NTILE // UNROLL) as i:
                for j in range(UNROLL):
                    tile = UNROLL * i + j
                    act.wait_ge(bias_done, tile + 1)
                    act.wait_ge(o_evac, tile)
                    for n in range(NU):
                        m, g = n // 2, 2 * (n % 2)
                        w = width[m]
                        wait_apart(act, b_ready, NU * tile + n + 1, passed)
                        if n % 2 == 0:
                            wait_apart(act, conv_done, NM * tile + m + 1, passed)
                        act.activation(pi[:, m % NPL, g:g + 2, 0:w], psum[:, 3 + g:5 + g, 0:w], ACT.Exp,
                                       bias=nb[:, j % 2, 1:2], scale=sq[:, bass.ds(tile, 1)],
                                       accum_out=sums[:, j % 4, n:n + 1]).then_inc(exp_done, 1)

        @block.vector
        def _(dve):
            own = Chain(dve, own_)
            dve.nop().then_inc(o_evac, 3)
            dve.wait_ge(w_in, 16 * N_WEIGHTS)
            dve.tensor_scalar(sq[:, :], nsq[:, :], -1.0, None, ALU.mult).then_inc(sq_done, 1)

            def tile_col(tile):
                return slice(tile, tile + 1) if isinstance(tile, int) else bass.ds(tile, 1)

            def largest(tile, j, early=False):
                if not early:
                    dve.wait_ge(exp_done, NU * tile - 10)
                dve.wait_ge(a_done, NX * (tile + 1))
                dve.tensor_reduce(nb[:, j % 2, 0:1], mx[:, j % 2, :], AX.X, ALU.max).then_inc(max_found, 1)

            def bias(tile, j):
                dve.wait_ge(max_found, tile + 1)
                dve.tensor_scalar(nb[:, j % 2, 1:2], nb[:, j % 2, 0:1], nsq[:, tile_col(tile)], LN255,
                                  ALU.mult, ALU.add).then_inc(bias_done, 1)

            def sum_up(tile, slot):
                dve.wait_ge(exp_done, NU * tile + NU + 2)
                dve.tensor_reduce(osc[:, slot % 2, 0:1], sums[:, slot % 4, :], AX.X, ALU.add).then_inc(osc_done, 1)

            def invert(tile, slot):
                dve.wait_ge(osc_done, 2 * tile + 1)
                dve.reciprocal(osc[:, slot % 2, 1:2], osc[:, slot % 2, 0:1]).then_inc(osc_done, 1)

            def outputs(tile, slot, places):
                dve.wait_ge(pv_part, NU * (tile + 2))
                dve.wait_ge(osc_done, 2 * tile + 2)
                for rows, cols, dst, scales in places:
                    i = dve.scalar_tensor_tensor(out=dst, in0=psum[rows, OB, cols],
                                                 scalar=osc[rows, slot % 2, 1:2], in1=scales,
                                                 op0=ALU.mult, op1=ALU.mult)
                i.then_inc(o_evac, 1)

            def maximum(tile, j, ready=None, bias_of_last=True, steps=(3, 4, 7)):
                for k in range(NX):
                    dve.wait_ge(a_ready, NX * tile + k + 1)
                    dve.tensor_reduce(mx[:, j % 2, k:k + 1], psum[:, k % 3, 0:width[blocks[k][0]]], AX.X,
                                      ALU.max).then_inc(a_done, 1)
                    if bias_of_last and k == 0:
                        largest(tile - 1, j - 1, isinstance(tile, int) and tile <= 2)
                    if bias_of_last and k == 1:
                        bias(tile - 1, j - 1)
                    if ready is not None and k == steps[0]:
                        sum_up(*ready[0:2])
                    if ready is not None and k == steps[1]:
                        invert(*ready[0:2])
                    if ready is not None and k == steps[2]:
                        outputs(*ready)

            def head_places(h, qt):
                at = slice(h * HD1, (h + 1) * HD1) if isinstance(h, int) else bass.ds(h * HD1, HD1)
                return [(slice(0, P), slice(0, HD1), ao[:, qt, at], svb[:, at])]

            def left_places(lt):
                out_ = []
                for i in range(4):
                    at = slice((4 * lt + i) * HD1, (4 * lt + i + 1) * HD1)
                    rows = slice(32 * i, 32 * i + 32)
                    out_.append((rows, slice(HD1 * i, HD1 * (i + 1)), ao[0:TR, NT - 1, at], svb[rows, at]))
                return out_

            maximum(0, 0, bias_of_last=False)
            maximum(1, 1)
            maximum(2, 2)
            with dve.Fori(0, NMAIN // 12 - 1) as i:
                for j in range(12):
                    maximum(12 * i + j + 3, j + 3, (12 * i + j, j, head_places(2 * i + j // 6, j % 6)))
            for t in range(NMAIN - 12, NTILE):
                ready = (t, t, head_places(t // 6, t % 6) if t < NMAIN else left_places(t - NMAIN))
                if t + 3 < NTILE:
                    maximum(t + 3, t + 3, ready, steps=(3, 4, 7) if t + 3 <= NMAIN + 1 else (2, 3, 5))
                    continue
                if t + 3 == NTILE:
                    largest(t + 2, t + 2)
                    bias(t + 2, t + 2)
                sum_up(t, t)
                invert(t, t)
                outputs(*ready)
            for j in range(4):
                c, n0 = j // 2, 4 * (j % 2)
                w = min(4 * P, T - n0 * P)
                dve.wait_ge(aot_ready, j + 1)
                dve.tensor_copy(aoT[:, c, n0 * P:n0 * P + w], psum[:, j, 0:w]).then_inc(aot_evac, 1)
            for n in range(NT):
                rows = P if n < NT - 1 else TR
                dve.wait_ge(res_ready, n + 1)
                dve.tensor_tensor(res[0:rows, n, :], psum[0:rows, 4 + n % 3, 0:D], bpb[0:rows, :],
                                  ALU.add).then_inc(res_done, 1)

        @block.tensor
        def _(pe):
            def a_block(ops, k, tile, first=False):
                if not (first and k < 3):
                    pe.wait_ge(a_done, NX * tile + k - 2)
                for lhsT, rhs, rows in ops(*blocks[k]):
                    mm = pe.matmul(psum[rows, k % 3, 0:width[blocks[k][0]]], lhsT, rhs, start=True, stop=True)
                mm.then_inc(a_ready, 1)

            def b_unit(ops, n, tile):
                pe.wait_ge(exp_done, NU * tile + n + 1)
                m = n // 2
                for g in (2 * (n % 2), 2 * (n % 2) + 1):
                    for lhsT, rhs, rows in ops(m, g):
                        mm = pe.matmul(psum[rows, 3 + g, 0:width[m]], lhsT, rhs, start=True, stop=True)
                mm.then_inc(b_ready, 1)

            def pv_piece(values, cols, k, tile):
                m = k // 2
                if k == 0:
                    pe.wait_ge(o_evac, tile + 2)
                if k % 4 == 0:
                    pe.wait_ge(pt_in[m // 2], 16 * (tile + 1))
                n_ch = 4 if m < NM - 1 else LCH
                for g in (2 * (k % 2), 2 * (k % 2) + 1):
                    for j in range(n_ch):
                        c = 4 * m + j
                        rows = P if c < CH - 1 else CR
                        mm = pe.matmul(psum[:, OB, 0:cols], pt[0:rows, m, n_ch * g + j, :],
                                       values(g * CH + c)[0:rows], start=(k == 0 and g == 0 and j == 0),
                                       stop=(k == NU - 1 and g == NR - 1 and j == n_ch - 1))
                mm.then_inc(pv_part, 1)

            pieces = [[k for k in range(NU) if 2 + k * 10 // 12 == n] for n in range(NU)]

            def body(tile, cur, nxt, later, prev, prev_cols=HD1, done=AHEAD):
                a = [(nxt, k, tile + 1) for k in range(done, len(blocks))] if nxt is not None else []
                a += [(later, k, tile + 2) for k in range(AHEAD)] if later is not None else []
                for n in range(NU):
                    if cur is not None:
                        b_unit(cur[0], n, tile)
                    for ops, k, t in a[len(a) * n // NU:len(a) * (n + 1) // NU]:
                        a_block(ops[0], k, t)
                    for k in pieces[n]:
                        pv_piece(prev[1], prev_cols, k, tile)

            def pair(hp, last):
                for par in range(2):
                    for qt in range(QT1):
                        tile = hp * (2 * QT1) + par * QT1 + qt
                        prev = main_tile(par, qt - 1) if qt else main_tile(1 - par, QT1 - 1)
                        if qt == QT1 - 2:
                            if par == 0:
                                pe.wait_ge(kv_in[1], N_HEAD * (hp + 1))
                            elif not last:
                                pe.wait_ge(kv_in[0], N_HEAD * (hp + 2))
                            else:
                                pe.wait_ge(kl_in[0], 32)
                                pe.wait_ge(kl_in[1], 32)
                        ahead = []
                        for k in (qt + 1, qt + 2):
                            if k < QT1:
                                ahead.append(main_tile(par, k))
                            elif par == 1 and last:
                                ahead.append(left_tile(k - QT1))
                            else:
                                ahead.append(main_tile(1 - par, k - QT1))
                        body(tile, main_tile(par, qt), *ahead, prev)

            pe.wait_ge(w_in, 16 * N_WEIGHTS)
            pe.wait_ge(set_up, 1)
            pe.wait_ge(kv_in[0], N_HEAD)
            for k in range(len(blocks)):
                a_block(main_tile(0, 0)[0], k, 0, True)
            for k in range(AHEAD):
                a_block(main_tile(0, 1)[0], k, 1)
            with pe.Fori(0, H1 // 2 - 1) as hp:
                pair(hp, False)
            pair(H1 // 2 - 1, True)
            for lt in range(NLEFT):
                if 1 <= lt < NLEFT - 1:
                    pe.wait_ge(kl_in[(lt + 1) % 2], 48)
                if lt >= 3:
                    pe.wait_ge(kl_in[(lt - 1) % 2], 64)
                body(NMAIN + lt, left_tile(lt), left_tile(lt + 1) if lt + 1 < NLEFT else None, None,
                     left_tile(lt - 1) if lt else main_tile(1, QT1 - 1), 4 * HD1 if lt else HD1,
                     0 if lt else AHEAD)
            pe.wait_ge(kl_in[(NLEFT - 1) % 2], 64)
            body(NTILE, None, None, None, left_tile(NLEFT - 1), 4 * HD1)
            pe.wait_ge(o_evac, 3 + NTILE)
            for j in range(4):
                c, n0 = j // 2, 4 * (j % 2)
                for n in range(n0, min(n0 + 4, NT)):
                    rows = P if n < NT - 1 else TR
                    at = (n - n0) * P
                    mm = pe.transpose(psum[:, j, at:at + rows], ao[0:rows, n, c * P:(c + 1) * P], ident[0:rows, 0:rows])
                mm.then_inc(aot_ready, 1)
            pe.wait_ge(aot_evac, 4)
            for n in range(NT):
                rows = P if n < NT - 1 else TR
                if n >= 3:
                    pe.wait_ge(res_done, n - 2)
                for c in range(DC):
                    mm = pe.matmul(psum[0:rows, 4 + n % 3, 0:D], aoT[:, c, n * P:n * P + rows], wp[:, c, :],
                                   start=(c == 0), stop=(c == DC - 1))
                mm.then_inc(res_ready, 1)


def build_program(nc, a, out):
    def dram(name, shape, dt=F32):
        return nc.dram_tensor(name, shape, dt, kind="Internal").ap()

    xa, xb, xc = (dram(f"x_{n}", (T, D)) for n in "abc")
    add0, add1, add2, add3 = (dram(f"add_{n}", (T, D)) for n in range(4))
    q_dram = dram("q_int", (H1, 2 * HD1, T), F16)
    nsq_dram, nsql_dram = dram("q_scale", (P, NMAIN)), dram("q_scale_last", (TR, H1))
    k_dram = dram("k_split", (H1, P, RK), F16)
    v_dram = dram("v_int", (H1, P, NR * CH, HD1), BF16)
    sv_dram = dram("v_scale", (H1 * HD1, 1))
    with ExitStack() as ctx:
        sp = Space(nc, ctx, "all")
        ident, ones, xnT = sp.sb("ident", [P, P]), sp.sb("ones", [P, P]), sp.sb("xnT", [P, DC, T])
        identb = sp.sb("identb", [P, P], BF16)
        constants(nc, ident, identb, ones)
        layer_norm(nc, "ln0", ident, a["x"], None, None, None, xnT)
        attention0(nc, ident, xnT, a["ctxT"], a["mask"], a["Wq0"], a["bq0"], a["Wk0"], a["bk0"], a["Wv0"], a["bv0"],
                   a["Wo0"], a["qn_w"], a["kn_w"], add0.rearrange("(b s) d -> b s d", b=B))
        with nc.sbuf_tensor("all_xrow", [P, NT, D], F32) as xrow:
            layer_norm(nc, "ln1", ident, a["x"], add0, a["g_xattn"][0:1, 0:1], xa, xnT, xrow)
            moe0(nc, ident, ones, xnT, xrow, a["gateT0"], a["wi0"], a["wo0"], add1)
        layer_norm(nc, "ln2", ident, xa, add1, a["g_ffn"][0:1, 0:1], xb, xnT)
        kv1(nc, ident, identb, ones, a["ctxT"], a["Wkv1"], a["bkv1"], k_dram, v_dram, sv_dram)
        q1(nc, ident, xnT, a["Wq1"], a["bq1"], q_dram, nsq_dram, nsql_dram)
        attention1(nc, ident, q_dram, nsq_dram, nsql_dram, k_dram, v_dram, sv_dram, a["Wp1"], a["bp1"], add2)
        layer_norm(nc, "ln3", ident, xb, add2, a["g_xattn"][0:1, 1:2], xc, xnT)
        moe1(nc, ident, xnT, a["gateT1"], a["Wgu1"], a["Wd1"], add3)
        layer_norm(nc, "end", ident, xc, add3, a["g_ffn"][0:1, 1:2], out, None)


def lay_out(i):
    row = lambda v: v.reshape(1, -1)
    col = lambda v: v.reshape(-1, 1)
    gate = np.concatenate([i["L1_ffn_Wg"], i["L1_ffn_Wsg"].reshape(2, F1, D)])
    up = np.concatenate([i["L1_ffn_Wu"], i["L1_ffn_Wsu"].reshape(2, F1, D)])
    gate_up = np.stack([gate, up], 1).reshape(NX1, 2, F1, DC, P).transpose(0, 4, 3, 1, 2)
    down = np.concatenate([i["L1_ffn_Wd"], i["L1_ffn_Wsd"].reshape(D, 2, F1).transpose(1, 0, 2)])
    down = down.reshape(NX1, D, F1 // FC1, FC1).transpose(0, 3, 2, 1)
    return {
        "x": i["x"].reshape(T, D),
        "ctxT": i["ctx_2048"].reshape(B * SE, DC, P).transpose(1, 2, 0),
        "mask": i["mask_1xSxS2_ff0"].reshape(S, SE),
        "g_xattn": row(i["g_xattn"]), "g_ffn": row(i["g_ffn"]),
        "Wq0": i["L0_xattn_Wq"], "bq0": row(i["L0_xattn_bq"]), "Wk0": i["L0_xattn_Wk"], "bk0": row(i["L0_xattn_bk"]),
        "Wv0": i["L0_xattn_Wv"], "bv0": row(i["L0_xattn_bv"]), "Wo0": i["L0_xattn_Wo"],
        "qn_w": col(i["L0_xattn_qn_w"]), "kn_w": col(i["L0_xattn_kn_w"]),
        "gateT0": i["L0_ffn_gate_weight"].T, "wi0": i["L0_ffn_wi"], "wo0": i["L0_ffn_wo"],
        "Wq1": i["L1_xattn_Wq"], "bq1": row(i["L1_xattn_bq"]), "Wkv1": i["L1_xattn_Wkv"],
        "bkv1": row(i["L1_xattn_bkv"]), "Wp1": i["L1_xattn_Wp"], "bp1": row(i["L1_xattn_bp"]),
        "gateT1": i["L1_ffn_Wr"].T, "Wgu1": gate_up, "Wd1": down,
    }


def kernel(**inputs):
    import concourse.bacc as bacc
    from concourse.bass_utils import run_bass_kernel_spmd

    arrays = {n: np.ascontiguousarray(v) for n, v in lay_out({k: np.asarray(v) for k, v in inputs.items()}).items()}
    nc = bacc.Bacc("TRN2", target_bir_lowering=False, num_devices=1)
    args = {n: nc.dram_tensor(f"in_{n}", v.shape, mybir.dt.from_np(v.dtype), kind="ExternalInput").ap()
            for n, v in arrays.items()}
    out = nc.dram_tensor("out", (T, D), F32, kind="ExternalOutput").ap()
    build_program(nc, args, out)
    r = run_bass_kernel_spmd(nc, [{f"in_{n}": v for n, v in arrays.items()}], core_ids=[0])
    return r.results[0]["out"].reshape(B, S, D)
```
